# Optimizing a Trainium2 kernel written in Bass

```python
import numpy as np
import jax
import jax.numpy as jnp

def _softmax(x, axis=-1):
    return jax.nn.softmax(x, axis=axis)

def _gelu(x):
    return jax.nn.gelu(x, approximate=True)

def _silu(x):
    return jax.nn.silu(x)

def _sigmoid(x):
    return jax.nn.sigmoid(x)

def _layernorm(x, axis=-1, eps=1e-05):
    m = jnp.mean(x, axis=axis, keepdims=True)
    v = jnp.var(x, axis=axis, keepdims=True)
    return (x - m) / jnp.sqrt(v + eps)

def _scatter_add(tgt, idx, src, axis=0):
    return tgt.at[idx].add(src)

def _segment_sum(src, seg, n):
    return jax.ops.segment_sum(src, seg, n)
kernel_name = 'mk_gnn_preln_d4_gnn_r32_042dac'

def setup_inputs(seed: int=0):
    np.random.seed(seed)
    _w = jnp.asarray

    def _rec_inputs():
        import jax
        import jax.numpy as jnp
        _gk = jax.random.key(seed)
        x = -0.0003713 + 1 * jax.random.normal(jax.random.fold_in(_gk, 1), (3125, 128), jnp.float32)
        src = jax.random.randint(jax.random.fold_in(_gk, 2), (50000,), 0, 3125, jnp.int32)
        dst = jnp.minimum((3125 * jax.random.uniform(jax.random.fold_in(_gk, 3), (50000,)) ** 2.0).astype(jnp.int32), 99999)
        _o = jnp.argsort(dst, stable=True)
        src = src[_o]
        dst = dst[_o]
        return (x, src, dst)
    x, src, dst = _rec_inputs()

    def _L0_gnn_setup():
        import jax, jax.numpy as jnp
        import numpy as np
        N_NODES = 3125
        IN_DIM = 128
        EMB_DIM = 128
        HIDDEN = 4 * EMB_DIM
        LN_EPS = 1e-05
        key = jax.random.key(seed)
        ks = jax.random.split(key, 8)
        x = jax.random.normal(ks[0], (N_NODES, IN_DIM), dtype=jnp.float32)
        edge_index = jax.random.randint(ks[1], (2, 50000), 0, N_NODES, dtype=jnp.int64)
        eps = jnp.zeros((), dtype=jnp.float32)
        s1 = 1.0 / np.sqrt(IN_DIM)
        s2 = 1.0 / np.sqrt(HIDDEN)
        W1 = jax.random.uniform(ks[2], (IN_DIM, HIDDEN), jnp.float32, -s1, s1)
        b1 = jax.random.uniform(ks[3], (HIDDEN,), jnp.float32, -s1, s1)
        ln_g = jnp.ones((HIDDEN,), jnp.float32)
        ln_b = jnp.zeros((HIDDEN,), jnp.float32)
        W2 = jax.random.uniform(ks[4], (HIDDEN, EMB_DIM), jnp.float32, -s2, s2)
        b2 = jax.random.uniform(ks[5], (EMB_DIM,), jnp.float32, -s2, s2)
        return {'x': x, 'edge_index': edge_index, 'eps': eps, 'W1': W1, 'b1': b1, 'ln_g': ln_g, 'ln_b': ln_b, 'W2': W2, 'b2': b2}
    _L0_gnn_all = _L0_gnn_setup()
    _L0_gnn_in = {k: v for k, v in _L0_gnn_all.items() if k in ('eps', 'W1', 'b1', 'ln_g', 'ln_b', 'W2', 'b2')}
    del _L0_gnn_all

    def _L1_gnn_setup():
        import jax, jax.numpy as jnp
        import numpy as np
        N = 3125
        E = 50000
        IN = 128
        H = 128
        key = jax.random.key(seed)
        ks = jax.random.split(key, 9)
        x = jax.random.normal(ks[0], (N, IN), dtype=jnp.float32)
        edge_index = jax.random.randint(ks[1], (2, E), 0, N, dtype=jnp.int64)
        s_in = 1.0 / np.sqrt(IN)
        s_h = 1.0 / np.sqrt(H)
        W1 = jax.random.uniform(ks[2], (IN, H), jnp.float32, -s_in, s_in)
        b1 = jnp.zeros((H,), jnp.float32)
        W2 = jax.random.uniform(ks[3], (H, H), jnp.float32, -s_h, s_h)
        b2 = jnp.zeros((H,), jnp.float32)
        W3 = jax.random.uniform(ks[4], (H, H), jnp.float32, -s_h, s_h)
        b3 = jnp.zeros((H,), jnp.float32)
        return {'x': x, 'edge_index': edge_index, 'dropout': 0, 'W1': W1, 'b1': b1, 'W2': W2, 'b2': b2, 'W3': W3, 'b3': b3}
    _L1_gnn_all = _L1_gnn_setup()
    _L1_gnn_in = {k: v for k, v in _L1_gnn_all.items() if k in ('W1', 'b1', 'W2', 'b2', 'W3', 'b3')}
    del _L1_gnn_all

    def _L2_gnn_setup():
        import jax, jax.numpy as jnp
        import numpy as np
        N_NODES = 50000
        N_EDGES = 25000
        D_IN = 128
        H0 = 128
        H1 = 128
        D_OUT = 128
        NUM_HEADS = 1

        def _attention(x, row, col, n_nodes):
            scores = jnp.sum(x[row] * x[col], axis=-1)
            scores = jax.nn.leaky_relu(scores, negative_slope=0.2)
            w = jax.nn.softmax(scores, axis=0)
            msgs = w[:, None] * x[col]
            return jax.ops.segment_sum(msgs, row, num_segments=n_nodes)
        key = jax.random.key(seed)
        ks = jax.random.split(key, 5)
        x = jax.random.normal(ks[0], (N_NODES, D_IN), dtype=jnp.float32)
        edge_index = jax.random.randint(ks[1], (2, N_EDGES), 0, N_NODES, dtype=jnp.int32)
        W0 = jax.random.normal(ks[2], (NUM_HEADS, D_IN, H0), dtype=jnp.float32) * (2.0 / (D_IN + H0)) ** 0.5
        b0 = jnp.zeros((NUM_HEADS, H0), dtype=jnp.float32)
        W1 = jax.random.normal(ks[3], (NUM_HEADS, H0, H1), dtype=jnp.float32) * (2.0 / (H0 + H1)) ** 0.5
        b1 = jnp.zeros((NUM_HEADS, H1), dtype=jnp.float32)
        W2 = jax.random.normal(ks[4], (H1 * NUM_HEADS, D_OUT), dtype=jnp.float32) * (2.0 / (H1 + D_OUT)) ** 0.5
        b2 = jnp.zeros((D_OUT,), dtype=jnp.float32)
        return {'x': x, 'edge_index': edge_index, 'W0': W0, 'b0': b0, 'W1': W1, 'b1': b1, 'W2': W2, 'b2': b2}
    _L2_gnn_all = _L2_gnn_setup()
    _L2_gnn_in = {k: v for k, v in _L2_gnn_all.items() if k in ('W0', 'b0', 'W1', 'b1', 'W2', 'b2')}
    del _L2_gnn_all

    def _L3_gnn_setup():
        import jax, jax.numpy as jnp
        import numpy as np
        N_NODES = 50000
        N_EDGES = 25000
        IN_DIM = 128
        HIDDEN = 128

        def _gcn_conv(x, W, b, src, dst, norm, n):
            h = x @ W
            msg = h[src] * norm[:, None]
            out = jax.ops.segment_sum(msg, dst, num_segments=n)
            return out + b
        key = jax.random.key(seed)
        ks = jax.random.split(key, 6)
        x = jax.random.normal(ks[0], (N_NODES, IN_DIM), dtype=jnp.float32)
        edge_index = jax.random.randint(ks[1], (2, N_EDGES), 0, N_NODES, dtype=jnp.int32)
        W1 = jax.random.normal(ks[2], (IN_DIM, HIDDEN), dtype=jnp.float32) * 0.05
        b1 = jnp.zeros((HIDDEN,), dtype=jnp.float32)
        W2 = jax.random.normal(ks[3], (HIDDEN, HIDDEN), dtype=jnp.float32) * 0.05
        b2 = jnp.zeros((HIDDEN,), dtype=jnp.float32)
        return {'x': x, 'edge_index': edge_index, 'W1': W1, 'b1': b1, 'W2': W2, 'b2': b2}
    _L3_gnn_all = _L3_gnn_setup()
    _L3_gnn_in = {k: v for k, v in _L3_gnn_all.items() if k in ('W1', 'b1', 'W2', 'b2')}
    del _L3_gnn_all
    return {'x': x, 'src': src, 'dst': dst, 'L0_gnn_eps': _L0_gnn_in['eps'], 'L0_gnn_W1': _L0_gnn_in['W1'], 'L0_gnn_b1': _L0_gnn_in['b1'], 'L0_gnn_ln_g': _L0_gnn_in['ln_g'], 'L0_gnn_ln_b': _L0_gnn_in['ln_b'], 'L0_gnn_W2': _L0_gnn_in['W2'], 'L0_gnn_b2': _L0_gnn_in['b2'], 'L1_gnn_W1': _L1_gnn_in['W1'], 'L1_gnn_b1': _L1_gnn_in['b1'], 'L1_gnn_W2': _L1_gnn_in['W2'], 'L1_gnn_b2': _L1_gnn_in['b2'], 'L1_gnn_W3': _L1_gnn_in['W3'], 'L1_gnn_b3': _L1_gnn_in['b3'], 'L2_gnn_W0': _L2_gnn_in['W0'], 'L2_gnn_b0': _L2_gnn_in['b0'], 'L2_gnn_W1': _L2_gnn_in['W1'], 'L2_gnn_b1': _L2_gnn_in['b1'], 'L2_gnn_W2': _L2_gnn_in['W2'], 'L2_gnn_b2': _L2_gnn_in['b2'], 'L3_gnn_W1': _L3_gnn_in['W1'], 'L3_gnn_b1': _L3_gnn_in['b1'], 'L3_gnn_W2': _L3_gnn_in['W2'], 'L3_gnn_b2': _L3_gnn_in['b2']}

def reference(x, src, dst, L0_gnn_eps, L0_gnn_W1, L0_gnn_b1, L0_gnn_ln_g, L0_gnn_ln_b, L0_gnn_W2, L0_gnn_b2, L1_gnn_W1, L1_gnn_b1, L1_gnn_W2, L1_gnn_b2, L1_gnn_W3, L1_gnn_b3, L2_gnn_W0, L2_gnn_b0, L2_gnn_W1, L2_gnn_b1, L2_gnn_W2, L2_gnn_b2, L3_gnn_W1, L3_gnn_b1, L3_gnn_W2, L3_gnn_b2):
    import jax
    import jax.numpy as jnp

    def _L0_gnn_ref(x, edge_index, eps, W1, b1, ln_g, ln_b, W2, b2):
        import jax, jax.numpy as jnp
        import numpy as np
        N_NODES = 3125
        IN_DIM = 128
        EMB_DIM = 128
        HIDDEN = 4 * EMB_DIM
        LN_EPS = 1e-05
        src, dst = (edge_index[0], edge_index[1])
        agg = jax.ops.segment_sum(x[src], dst, num_segments=N_NODES)
        h = (1.0 + eps) * x + agg
        h = h @ W1 + b1
        mu = jnp.mean(h, axis=-1, keepdims=True)
        var = jnp.var(h, axis=-1, keepdims=True)
        h = (h - mu) * jax.lax.rsqrt(var + LN_EPS) * ln_g + ln_b
        h = jax.nn.gelu(h, approximate=False)
        return h @ W2 + b2

    def _L1_gnn_ref(x, edge_index, dropout, W1, b1, W2, b2, W3, b3):
        import jax, jax.numpy as jnp
        import numpy as np
        N = 3125
        E = 50000
        IN = 128
        H = 128
        n = x.shape[0]
        loops = jnp.arange(n, dtype=edge_index.dtype)
        src = jnp.concatenate([edge_index[0], loops])
        dst = jnp.concatenate([edge_index[1], loops])
        deg = jax.ops.segment_sum(jnp.ones(src.shape[0], x.dtype), dst, num_segments=n)
        dinv = jax.lax.rsqrt(jnp.maximum(deg, 1.0))
        norm = dinv[src] * dinv[dst]

        def gcn(h, W, b):
            h = h @ W
            msg = h[src] * norm[:, None]
            agg = jax.ops.segment_sum(msg, dst, num_segments=n)
            return agg + b
        h = jax.nn.relu(gcn(x, W1, b1))
        h = jax.nn.relu(gcn(h, W2, b2))
        return gcn(h, W3, b3)

    def _L2_gnn_ref(x, edge_index, W0, b0, W1, b1, W2, b2):
        import jax, jax.numpy as jnp
        import numpy as np
        N_NODES = 50000
        N_EDGES = 25000
        D_IN = 128
        H0 = 128
        H1 = 128
        D_OUT = 128
        NUM_HEADS = 1

        def _attention(x, row, col, n_nodes):
            scores = jnp.sum(x[row] * x[col], axis=-1)
            scores = jax.nn.leaky_relu(scores, negative_slope=0.2)
            w = jax.nn.softmax(scores, axis=0)
            msgs = w[:, None] * x[col]
            return jax.ops.segment_sum(msgs, row, num_segments=n_nodes)
        row, col = (edge_index[0], edge_index[1])
        n = x.shape[0]
        heads = []
        for i in range(NUM_HEADS):
            h = jax.nn.relu(x @ W0[i] + b0[i])
            heads.append(_attention(h, row, col, n))
        x = jnp.concatenate(heads, axis=-1)
        heads = []
        for i in range(NUM_HEADS):
            h = jax.nn.relu(x @ W1[i] + b1[i])
            heads.append(_attention(h, row, col, n))
        x = jnp.concatenate(heads, axis=-1)
        return x @ W2 + b2

    def _L3_gnn_ref(x, edge_index, W1, b1, W2, b2):
        import jax, jax.numpy as jnp
        import numpy as np
        N_NODES = 50000
        N_EDGES = 25000
        IN_DIM = 128
        HIDDEN = 128

        def _gcn_conv(x, W, b, src, dst, norm, n):
            h = x @ W
            msg = h[src] * norm[:, None]
            out = jax.ops.segment_sum(msg, dst, num_segments=n)
            return out + b
        n = x.shape[0]
        loops = jnp.arange(n, dtype=edge_index.dtype)
        src = jnp.concatenate([edge_index[0], loops])
        dst = jnp.concatenate([edge_index[1], loops])
        deg = jax.ops.segment_sum(jnp.ones(src.shape, dtype=x.dtype), dst, num_segments=n)
        dinv = jax.lax.rsqrt(deg)
        norm = dinv[src] * dinv[dst]
        h = jax.nn.relu(_gcn_conv(x, W1, b1, src, dst, norm, n))
        return _gcn_conv(h, W2, b2, src, dst, norm, n)
    edge_index = jnp.stack([src, dst])
    h = jnp.maximum(_layernorm(x, axis=-1), 0.0)
    x = x + _L0_gnn_ref(h, edge_index, L0_gnn_eps, L0_gnn_W1, L0_gnn_b1, L0_gnn_ln_g, L0_gnn_ln_b, L0_gnn_W2, L0_gnn_b2)
    h = jnp.maximum(_layernorm(x, axis=-1), 0.0)
    x = x + _L1_gnn_ref(h, edge_index, 0, L1_gnn_W1, L1_gnn_b1, L1_gnn_W2, L1_gnn_b2, L1_gnn_W3, L1_gnn_b3)
    h = jnp.maximum(_layernorm(x, axis=-1), 0.0)
    x = x + _L2_gnn_ref(h, edge_index, L2_gnn_W0, L2_gnn_b0, L2_gnn_W1, L2_gnn_b1, L2_gnn_W2, L2_gnn_b2)
    h = jnp.maximum(_layernorm(x, axis=-1), 0.0)
    x = x + _L3_gnn_ref(h, edge_index, L3_gnn_W1, L3_gnn_b1, L3_gnn_W2, L3_gnn_b2)
    return x

_drawn_inputs = setup_inputs


def setup_inputs(seed=0):
    import zlib

    import numpy as np

    out = dict(_drawn_inputs(seed))
    spreads = {'L0_gnn_ln_g': (1.0, 0.2),
     'L0_gnn_ln_b': (0.0, 0.281),
     'L1_gnn_b1': (0.0, 0.564),
     'L1_gnn_b2': (0.0, 0.314),
     'L1_gnn_b3': (0.0, 0.1),
     'L2_gnn_b0': (0.0, 0.8),
     'L2_gnn_b1': (0.0, 2.0),
     'L2_gnn_b2': (0.0, 0.339),
     'L3_gnn_b1': (0.0, 0.745),
     'L3_gnn_b2': (0.0, 0.328)}
    factors = {'L0_gnn_b1': 8.0,
     'L2_gnn_W0': 8.0,
     'L2_gnn_W1': 8.0,
     'L2_gnn_W2': 8.0,
     'L1_gnn_W1': 2.803,
     'L3_gnn_W1': 2.686}
    for name, (base, spread) in spreads.items():
        noise = np.random.default_rng([zlib.crc32(name.encode()), seed]).standard_normal(out[name].shape)
        drawn = base * np.exp(spread * noise) if base else spread * noise
        out[name] = jnp.asarray(drawn.astype(out[name].dtype))
    for name, factor in factors.items():
        out[name] = (out[name] * factor).astype(out[name].dtype)
    return out
```

```python
from contextlib import ExitStack

import concourse.bass as bass
from concourse import mybir

F32 = mybir.dt.float32
BF16 = mybir.dt.bfloat16
FP16 = mybir.dt.float16
I32 = mybir.dt.int32
ALU = mybir.AluOpType
ACT = mybir.ActivationFunctionType
AX = mybir.AxisListType
ds = bass.ds

P = 128
D = 128
N = 3125
TILES = -(-N // P)
NPAD = TILES * P
LAST = N - (TILES - 1) * P
HID = 4 * D
LN_EPS = 1e-5

E_EDGES = 50000
EC = 125
CHUNKS = E_EDGES // EC
GROUPS = 4
GC = CHUNKS // GROUPS
WIN = 20
KEYS = TILES * WIN
ROUNDS = -(-N // WIN)
FAR = 10000.0
TURN = 16

AHEAD = 3

BLOCKS = 5
BT = TILES // BLOCKS
BW = BT * P
HALF = BW // 2
PIECES = -(-TILES // 4)
STAGES = 5

SLICES = 10
SW = NPAD // SLICES
LEAD = 6
SBANKS = 5

PARTS = 3


def gnn_kernel(nc, t):
    with ExitStack() as ctx:
        build(nc, t, ctx)


def build(nc, t, ctx):
    def sem(name):
        return ctx.enter_context(nc.semaphore(name))

    A = ctx.enter_context(nc.sbuf_tensor("adjacency", [P, TILES, NPAD], FP16))
    ARENA = (212800 - TILES * NPAD * 2) // 4
    arena = ctx.enter_context(nc.sbuf_tensor("arena", [P, ARENA], F32))
    at = [0]

    def take(cols, dt=F32, start=None):
        a = at[0] if start is None else start
        width = cols if dt in (F32, I32) else -(-cols // 2)
        at[0] = a + width
        assert at[0] <= ARENA, (at[0], ARENA)
        v = arena[:, a:a + width]
        return v if dt == F32 else v.bitcast(dt)

    ident = take(P)
    ident16 = take(P, FP16)
    identb = take(P, BF16)
    ones = take(P)
    one_eps = take(2)[:, 0:1]
    dinv = take(TILES + 1)[:, 0:TILES]
    deg_parts = take(TILES * PIECES + 1)[:, 0:TILES * PIECES].rearrange("p (t k) -> p t k", t=TILES)
    half_neg = take(8)
    hstat = take(6)
    scrap = take(2)
    peak = take(2)[:, 0:1]
    top = take(2)[0:1, 0:1]
    neg_top = take(SLICES)
    least = take(2)[:, 0:1]
    wts = take(SLICES)
    sums = take(SLICES)
    total = take(2)
    scale8 = take(SLICES)
    bcol = take(2)
    hmv = take(4).rearrange("p (b s) -> p b s", b=2)
    hrstd = take(2)
    stats = take(TILES * 6 + 2)[:, 0:TILES * 6].rearrange("p (t s) -> p t s", t=TILES)
    mean_var = take(TILES * 2)[:, :].rearrange("p (t s) -> p t s", t=TILES)
    rstd = take(TILES + 1)[:, 0:TILES]
    shift = take(TILES + 1)[:, 0:TILES]
    gamma = take(4)
    beta = take(4)
    wmat = take(3 * D).rearrange("p (l f) -> p l f", l=3)
    brow = take(3 * D).rearrange("p (l f) -> p l f", l=3)
    BUILD_AT = at[0]
    aggT = take(BW)
    work = take(2 * BW).rearrange("p (b n) -> p b n", b=2)
    rest = take(2 * BW).rearrange("p (b n) -> p b n", b=2)
    PARTS_AT = at[0]
    parts = take(PARTS * TILES * D, BF16).rearrange("p (k t f) -> p k t f", k=PARTS, t=TILES)
    OVER = at[0]
    G = take(TILES * D).rearrange("p (t f) -> p t f", t=TILES)
    at[0] = OVER
    w1 = take(HID)
    w2 = take(HID).rearrange("p (k f) -> p k f", k=4)
    b1row = take(HID)
    gel = take(HID).rearrange("p (k f) -> p k f", k=4)
    stage = take(STAGES * 512, FP16).rearrange("p (b n) -> p b n", b=STAGES)
    hT = work[:, 0, :]
    xnew = work[:, 1, :].rearrange("p (t f) -> p t f", t=BT)
    hid = rest.rearrange("p b n -> p (b n)")[:, 0:2 * HID].rearrange("p (b n) -> p b n", b=2)

    A32 = A[:, :, :].rearrange("p t n -> p (t n)").bitcast(F32)
    cut = [0]

    def carve(cols):
        cut[0] += cols
        return A32[:, cut[0] - cols:cut[0]]

    Z = [carve(TILES * SW).rearrange("p (t n) -> p t n", t=TILES)]
    Ab = [carve(TILES * SW // 2).bitcast(FP16).rearrange("p (t n) -> p t n", t=TILES)]
    mask = carve(SBANKS * SW).bitcast(FP16).rearrange("p (b n) -> p b n", b=2 * SBANKS)
    EARLY = cut[0] * 2 // NPAD
    Z.append(carve(TILES * SW).rearrange("p (t n) -> p t n", t=TILES))
    Ab.append(carve(TILES * SW // 2).bitcast(FP16).rearrange("p (t n) -> p t n", t=TILES))
    XT = carve(NPAD)
    rowmax = carve(TILES + 1)[:, 0:TILES]
    rowsum = carve(2 * TILES).rearrange("p (c t) -> p c t", c=2)
    GONE = -(-cut[0] * 2 // NPAD)
    HT = arena[:, BUILD_AT:BUILD_AT + NPAD]
    H = parts.rearrange("p k t f -> p (k t f)").bitcast(F32)[:, 0:NPAD].rearrange("p (t f) -> p t f", t=TILES)

    psum = ctx.enter_context(nc.psum_tensor("psum", [P, 8, 512], F32))
    pflat = psum[:, :, :].rearrange("p b n -> p (b n)")

    Ad = nc.dram_tensor("adjacency_by_dst", (TILES, P, NPAD), FP16, kind="Internal").ap()
    At = nc.dram_tensor("adjacency_by_src", (P, TILES * NPAD), FP16, kind="Internal").ap()
    x3 = nc.dram_tensor("x_after_l2", (NPAD, D), F32, kind="Internal").ap()
    x3v = x3.rearrange("(t p) f -> p t f", p=P)
    x1 = nc.dram_tensor("x_after_l0", (NPAD, D), F32, kind="Internal").ap()
    x1v = x1.rearrange("(t p) f -> p t f", p=P)
    xin_v = t["x"][0:(TILES - 1) * P, :].rearrange("(t p) f -> p t f", p=P)
    Aflat = A[:, :, :].rearrange("p t n -> p (t n)")

    at[0] = BUILD_AT
    edges_i = take(2 * GROUPS * EC, I32)[0:GC].rearrange("p (w g j) -> p w g j", w=2, g=GROUPS)
    rel = take(GROUPS * EC)[0:GC].rearrange("p (g j) -> p g j", g=GROUPS)
    shi = take(GROUPS * EC)[0:GC].rearrange("p (g j) -> p g j", g=GROUPS)
    slo = take(GROUPS * EC)[0:GC].rearrange("p (g j) -> p g j", g=GROUPS)
    tmp_i = take(GROUPS * EC, I32)[0:GC].rearrange("p (g j) -> p g j", g=GROUPS)
    key = take(GROUPS * EC)[0:GC].rearrange("p (g j) -> p g j", g=GROUPS)
    tmp_f = take(GROUPS * EC)[0:GC].rearrange("p (g j) -> p g j", g=GROUPS)
    base = take(GROUPS)[0:GC]
    keyT = take(CHUNKS + AHEAD + 1)[0:EC]
    nsloT = take(CHUNKS)[0:EC]
    base_f = take(CHUNKS)[0:1]
    base_i = take(CHUNKS, I32)[0:1]
    iota_i = take(KEYS, I32)
    iota16 = take(KEYS, FP16)
    hot_key = take(4 * KEYS, FP16)[0:EC].rearrange("p (b n) -> p b n", b=4)
    hot_slo = take(TURN * P, FP16)[0:EC].rearrange("p (b n) -> p b n", b=TURN)

    dist = take(TURN * P, FP16)[0:EC].rearrange("p (b n) -> p b n", b=TURN)
    one = ones[:, 0:1]

    s_dist = sem("distances_ready")
    s_edges = sem("edges_loaded")
    s_ones = sem("ones_made")
    s_iota = sem("iota_made")
    s_iota16 = sem("iota16_made")
    s_ident = sem("ident_made")
    s_zero = sem("a_zeroed")
    s_prep = sem("dve_prep")
    s_keyT = sem("keys_transposed")
    s_keysb = sem("keys_in_sbuf")
    s_hk = sem("hot_key_ready")
    s_hs = sem("hot_slo_ready")
    s_out = sem("chunk_product_ready")
    s_acc = sem("chunk_added")
    s_base = sem("bases_in_sbuf")

    BUILT = TURN + CHUNKS

    s_x = sem("x_loaded")
    s_w = sem("layer_weights_loaded")
    s_eps = sem("eps_loaded")
    s_misc = sem("small_constants_ready")
    s_bn = sem("tile_stats_ready")
    s_mv = sem("mean_var_ready")
    s_ve = sem("variance_plus_eps_ready")
    s_rs = sem("rstd_ready")
    s_sh = sem("shift_ready")
    s_h = sem("h_block_ready")
    s_hi = sem("hi_part_ready")
    s_r1 = sem("rest_ready")
    s_mid = sem("mid_part_ready")
    s_parts = sem("block_parts_ready")
    s_agg = sem("agg_block_ready")
    s_aggT = sem("agg_half_in_sbuf")
    s_hTp = sem("h_transposed")
    s_hT = sem("scaled_h_in_sbuf")
    s_y = sem("weight_product_ready")
    s_u = sem("scaled_product_ready")
    s_ub = sem("biased_product_ready")
    s_g = sem("block_output_ready")
    s_hp = sem("hidden_product_ready")
    s_hb = sem("hidden_biased")
    s_hbn = sem("hidden_stats_ready")
    s_hmv = sem("hidden_mean_var_ready")
    s_hve = sem("hidden_variance_plus_eps_ready")
    s_hrs = sem("hidden_rstd_ready")
    s_hn = sem("hidden_normalised")
    s_hnT = sem("hidden_transposed")
    s_gel = sem("gelu_ready")
    s_o = sem("mlp_product_ready")
    s_xb = sem("x_block_loaded")
    s_xbb = sem("x_block_biased")
    s_xn = sem("x_tile_updated")
    s_x1 = sem("x1_block_stored")
    s_tp = sem("adjacency_piece_transposed")
    s_ts = sem("adjacency_piece_staged")
    s_td = [sem(f"adjacency_stage{b}_stored") for b in range(STAGES)]
    s_dg = sem("degree_steps")
    s_dinv = sem("dinv_ready")
    s_self = sem("self_loops_added")
    s_at = sem("adjacency_saved")
    s_fin = sem("output_stored")
    s_gx = sem("x_reloaded")

    s_xT = sem("x_transposed")
    s_xTs = sem("xT_in_sbuf")
    s_hl = sem("attention_h_product")
    s_hls = sem("attention_hT_ready")
    s_ht = sem("attention_h_transposed")
    s_hts = sem("attention_h_ready")
    s_ad = [sem(f"adjacency_slice_group{g}_loaded") for g in range(BLOCKS)]
    s_mask = sem("mask_ready")
    s_s = sem("scores_ready")
    s_z = sem("masked_scores_ready")
    s_rm = sem("row_peak_ready")
    s_rmT = sem("row_peak_transposed")
    s_top = sem("slice_top_ready")
    s_tb = sem("slice_top_broadcast")
    s_nt = sem("slice_neg_top_ready")
    s_e = sem("exp_ready")
    s_sum = sem("slice_row_sums_ready")
    s_p = sem("edge_weights_ready")
    s_pv = sem("weighted_sum_step")
    s_ot = sem("slice_sum_in_sbuf")
    s_fs = sem("softmax_total_steps")
    s_wt = sem("slice_weights_ready")
    s_ls = sem("slice_sums_ready")
    s_sc = sem("slices_scaled")
    s_x3p = sem("attention_output_product")
    s_x3 = sem("x3_ready")
    s_x3d = sem("x3_saved")
    s_back = [sem(f"adjacency_{w}_reloaded") for w in ("first_tiles", "next_tiles", "last_tiles")]

    def dst_view(a):
        return a.rearrange("o (g c j) -> c (o g) j", g=GROUPS, c=GC)

    block = ctx.enter_context(nc.Block())



    def blk(c):
        return ds(c * BT, BT)

    PN = BT * PIECES

    def piece(n):
        q, k = divmod(n, PIECES)
        return q, 4 * k, min(4, TILES - 4 * k)

    @block.sync
    def _(sp):
        sp.dma_start(edges_i[:, 0], dst_view(t["dst"])).then_inc(s_edges, 16)
        sp.dma_start(edges_i[:, 1], dst_view(t["src"])).then_inc(s_edges, 16)
        sp.dma_start(one_eps, t["L0_gnn_eps"].partition_broadcast(P).rearrange("p a b -> p (a b)")).then_inc(s_eps, 16)
        sp.wait_ge(s_acc, BUILT)
        sp.wait_ge(s_misc, 2)
        for c in range(BLOCKS):
            e = min((c + 1) * BT, TILES - 1)
            sp.dma_start(G[:, c * BT:e, :], xin_v[:, c * BT:e, :]).then_inc(s_x, 16)
        sp.dma_start(G[0:LAST, TILES - 1, :], t["x"][(TILES - 1) * P:N, :]).then_inc(s_x, 16)
        sp.wait_ge(s_h, BLOCKS)
        sp.dma_start(w1, t["L0_gnn_W1"]).then_inc(s_w, 16)
        sp.dma_start(w2, t["L0_gnn_W2"].rearrange("(k p) f -> p k f", p=P)).then_inc(s_w, 16)
        sp.dma_start(b1row, t["L0_gnn_b1"].partition_broadcast(P).rearrange("p a b -> p (a b)")).then_inc(s_w, 16)
        sp.dma_start(gamma, t["L0_gnn_ln_g"].rearrange("o (k p) -> p (o k)", p=P),
                     allow_slow_non_contiguous=True).then_inc(s_w, 16)
        sp.dma_start(beta, t["L0_gnn_ln_b"].rearrange("o (k p) -> p (o k)", p=P),
                     allow_slow_non_contiguous=True).then_inc(s_w, 16)
        sp.dma_start(brow[:, 0, :], t["L0_gnn_b2"].partition_broadcast(P).rearrange("p a b -> p (a b)")).then_inc(s_w, 16)
        sp.wait_ge(s_parts, BLOCKS)

        def l0_block(c, last):
            sp.wait_ge(s_x1, 16 * c + 16)
            if last:
                sp.dma_start(xnew[:, 0:BT - 1, :], xin_v[:, (BLOCKS - 1) * BT:, :]).then_inc(s_xb, 16)
                sp.dma_start(xnew[0:LAST, BT - 1, :], t["x"][(TILES - 1) * P:N, :]).then_inc(s_xb, 16)
            else:
                sp.dma_start(xnew[:, :, :], xin_v[:, blk(c), :]).then_inc(s_xb, 32)
            for n in range(PN):
                q, st, k = piece(n)
                sp.wait_ge(s_ts, c * PN + n + 1 + 2)
                sp.dma_start(Ad[ds(c * BT + q, 1), :, st * P:(st + k) * P].rearrange("o p n -> (o p) n"),
                             stage[:, n % STAGES, 0:k * P]).then_inc(s_td[n % STAGES], 16)
            sp.wait_ge(s_xn, (c + 1) * BT)
            sp.dma_start(x1v[:, blk(c), :], xnew[:, :, :]).then_inc(s_x1, 16)

        with sp.Fori(0, BLOCKS - 1) as c:
            l0_block(c, False)
        l0_block(BLOCKS - 1, True)
        sp.wait_ge(s_x1, 16 * BLOCKS + 16)
        sp.wait_ge(s_o, TILES)
        for b in range(STAGES):
            sp.wait_ge(s_td[b], 16 + 16 * BLOCKS * PN // STAGES)
        for c in range(BLOCKS):
            sp.dma_start(G[:, blk(c), :], x1v[:, blk(c), :]).then_inc(s_gx, 16)
        for l in range(3):
            sp.dma_start(wmat[:, l, :], t[f"L1_gnn_W{l + 1}"]).then_inc(s_w, 16)
            sp.dma_start(brow[:, l, :], t[f"L1_gnn_b{l + 1}"].partition_broadcast(P).rearrange("p a b -> p (a b)"))\
                .then_inc(s_w, 16)
        sp.wait_ge(s_self, 2)
        sp.dma_start(At, Aflat).then_inc(s_at, 16)
        sp.wait_ge(s_parts, 4 * BLOCKS)
        for c in range(BLOCKS):
            sp.dma_start(G[:, blk(c), :], x1v[:, blk(c), :]).then_inc(s_gx, 16)
        sp.wait_ge(s_g, 3 * BLOCKS + 1)
        for l, n in enumerate(("L2_gnn_W0", "L2_gnn_W1", "L2_gnn_W2")):
            sp.dma_start(wmat[:, l, :], t[n]).then_inc(s_w, 16)
        for l in range(2):
            sp.dma_start(bcol[:, l:l + 1], t[f"L2_gnn_b{l}"].rearrange("o p -> p o"),
                         allow_slow_non_contiguous=True).then_inc(s_w, 16)
        sp.dma_start(brow[:, 0, :], t["L2_gnn_b2"].partition_broadcast(P).rearrange("p a b -> p (a b)"))\
            .then_inc(s_w, 16)
        sp.wait_ge(s_at, 16)
        for l in range(2):
            def load(c, b):
                k = SLICES * l + c
                for g in range(BLOCKS):
                    sp.wait_ge(s_p, TILES * k + BT * (g + 1))
                    sp.wait_ge(s_ad[g], 16 * (k + 1))
                    sp.dma_start(Ab[b][:, g * BT:(g + 1) * BT, :],
                                 Ad[g * BT:(g + 1) * BT, :, ds(c * SW, SW)].rearrange("t p n -> p t n"))\
                        .then_inc(s_ad[g], 16)

            with sp.Fori(0, SLICES // 2) as i:
                c = i * 2
                load(c, 0)
                load(c + 1, 1)
        At_v = At.rearrange("p (t n) -> p t n", n=NPAD)
        sp.wait_ge(s_pv, TILES * (2 * SLICES + 1))
        sp.wait_ge(s_z, TILES * 2 * SLICES + SBANKS)
        sp.dma_start(A[:, 0:EARLY, :], At_v[:, 0:EARLY, :]).then_inc(s_back[0], 16)
        sp.wait_ge(s_x3, BLOCKS)
        for c in range(BLOCKS):
            sp.dma_start(x3v[:, blk(c), :], G[:, blk(c), :]).then_inc(s_x3d, 16)
        for l in range(2):
            sp.dma_start(wmat[:, l, :], t[f"L3_gnn_W{l + 1}"]).then_inc(s_w, 16)
            sp.dma_start(brow[:, l, :], t[f"L3_gnn_b{l + 1}"].partition_broadcast(P).rearrange("p a b -> p (a b)"))\
                .then_inc(s_w, 16)
        for e, (lo, hi) in enumerate(((EARLY, (EARLY + GONE) // 2), ((EARLY + GONE) // 2, GONE))):
            sp.dma_start(A[:, lo:hi, :], At_v[:, lo:hi, :]).then_inc(s_back[1 + e], 16)
        sp.wait_ge(s_parts, 6 * BLOCKS)
        sp.wait_ge(s_x3d, 16 * BLOCKS)
        for c in range(BLOCKS):
            sp.dma_start(G[:, blk(c), :], x3v[:, blk(c), :]).then_inc(s_gx, 16)
        out_v = t["out"][0:(TILES - 1) * P, :].rearrange("(t p) f -> p t f", p=P)
        for c in range(BLOCKS):
            e = min((c + 1) * BT, TILES - 1)
            sp.wait_ge(s_g, 4 * BLOCKS + c + 2)
            sp.dma_start(out_v[:, c * BT:e, :], G[:, c * BT:e, :]).then_inc(s_fin, 16)
        sp.dma_start(t["out"][(TILES - 1) * P:N, :], G[0:LAST, TILES - 1, :]).then_inc(s_fin, 16)
        sp.wait_ge(s_fin, 16 * (BLOCKS + 1))

    @block.gpsimd
    def _(pool):
        pool.iota(iota_i, [[1, KEYS]], base=0, channel_multiplier=0).then_inc(s_iota, 1)
        pool.memset(ident, 0.0).then_inc(s_ident, 1)
        pool.wait_ge(s_ident, 1)
        pool.affine_select(out=ident, in_=ident, compare_op=ALU.not_equal, fill=1.0, base=0,
                           pattern=[[-1, P]], channel_multiplier=1).then_inc(s_ident, 1)
        pool.memset(half_neg, -0.5).then_inc(s_ident, 1)
        pool.memset(A[:, TILES // 2:, :], 0.0).then_inc(s_zero, 1)
        pool.wait_ge(s_ident, 2)
        pool.tensor_copy(ident16, ident).then_inc(s_ident, 1)
        pool.tensor_copy(identb, ident).then_inc(s_ident, 1)
        pool.wait_ge(s_eps, 16)
        pool.tensor_scalar(one_eps, one_eps, 1.0, None, ALU.add).then_inc(s_misc, 1)
        pool.wait_ge(s_acc, BUILT)
        pool.memset(G[:, TILES - 1, :], 0.0).then_inc(s_misc, 1)
        pool.wait_ge(s_ident, 5)

        def power(out, n):
            pool.tensor_tensor(out, out, half_neg[:, 0:n], ALU.pow)

        def norm_power(p):
            for c in range(BLOCKS):
                pool.wait_ge(s_ve, BLOCKS * p + c + 1)
                r = rstd[:, blk(c)]
                pool.tensor_tensor(r, r, half_neg[:, 0:BT], ALU.pow).then_inc(s_rs, 1)

        norm_power(0)
        with pool.Fori(0, TILES) as g:
            pool.wait_ge(s_hve, g + 1)
            r = hrstd[:, ds(g % 2, 1)]
            pool.tensor_tensor(r, r, half_neg[:, 0:1], ALU.pow).then_inc(s_hrs, 1)
        pool.wait_ge(s_dg, 2)
        pool.tensor_tensor(dinv, dinv, half_neg[:, 0:1].broadcast_to([P, TILES]), ALU.pow).then_inc(s_dinv, 1)
        norm_power(1)
        norm_power(2)
        norm_power(3)

    @block.scalar
    def _(act):
        act.preload_act_table(ACT.Square)
        act.wait_ge(s_iota16, 1)
        act.wait_ge(s_ones, 1)
        act.wait_ge(s_keysb, 3)
        with act.Fori(0, CHUNKS // TURN) as i:
            for h in range(TURN // 4):
                act.wait_ge(s_out, i * TURN + 4 * h + 4)
                if h:
                    act.wait_ge(s_hs, i * (TURN // 4) + h)
                for k in range(4 * h, 4 * h + 4):
                    act.activation(dist[:, k, :], iota16[0:EC, 0:P], ACT.Square,
                                   bias=nsloT[:, ds(i * TURN + k, 1)]).then_inc(s_dist, 1)
                act.wait_ge(s_dist, i * TURN + 4 * h + 4)
                act.activation(hot_slo[:, 4 * h:4 * h + 4, :], dist[:, 4 * h:4 * h + 4, :], ACT.Relu,
                               bias=one[0:EC, :], scale=-1.0).then_inc(s_hs, 1)

        def flat(v):
            return v.rearrange("p t f -> p (t f)")

        def split(p, nb, normal):
            for c in range(BLOCKS + 1):
                n = BLOCKS * p + c
                if c < BLOCKS:
                    if normal:
                        act.wait_ge(s_sh, BLOCKS * nb + c + 1)
                        if c >= 2:
                            act.wait_ge(s_r1, n - 1)
                            act.wait_ge(s_hi, n - 1)
                        for q in range(BT):
                            tt = c * BT + q
                            last = act.activation(work[:, c % 2, q * D:(q + 1) * D], G[:, tt, :], ACT.Relu,
                                                  bias=shift[:, tt:tt + 1], scale=rstd[:, tt:tt + 1])
                        last.then_inc(s_h, 1)
                        act.wait_ge(s_h, BLOCKS * nb + c + 1)
                        src = work[:, c % 2, :]
                    else:
                        act.wait_ge(s_g, BLOCKS * (p - 2) + c + 1 + 1)
                        src = flat(G[:, blk(c), :])
                    act.activation(flat(parts[:, 0, blk(c), :]), src, ACT.Copy).then_inc(s_hi, 1)
                if c:
                    act.wait_ge(s_r1, n)
                    act.activation(flat(parts[:, 1, blk(c - 1), :]), rest[:, (c - 1) % 2, :], ACT.Copy).then_inc(s_mid, 1)

        act.wait_ge(s_acc, BUILT)
        split(0, 0, True)
        act.wait_ge(s_w, 16 * 6)
        act.wait_ge(s_misc, 1)
        with act.Fori(0, BLOCKS) as c:
            for n in range(PN):
                q, st, k = piece(n)
                act.wait_ge(s_tp, c * PN + n + 1)
                act.wait_ge(s_td[n % STAGES], 16 * (c * (PN // STAGES) + n // STAGES) + 16)
                act.activation(stage[:, n % STAGES, 0:k * P], psum[:, 2 + n % 2, 0:k * P], ACT.Copy,
                               accum_out=deg_parts[:, ds(c * BT + q, 1), st // 4:st // 4 + 1]
                               .rearrange("p a b -> p (a b)")).then_inc(s_ts, 1)
            act.wait_ge(s_hTp, c + 1)
            act.wait_ge(s_aggT, 2 * c + 1)
            act.activation(hT, pflat[:, 4 * 512:4 * 512 + BW], ACT.Copy, scale=one_eps).then_inc(s_hT, 1)
            for q in range(BT):
                act.wait_ge(s_hnT, c * BT + q + 1)
                act.wait_ge(s_o, c * BT + q + 1)
                for k in range(4):
                    last = act.activation(gel[:, k, :], psum[:, 6, k * P:(k + 1) * P], ACT.Gelu,
                                          bias=beta[:, k:k + 1], scale=gamma[:, k:k + 1])
                last.then_inc(s_gel, 1)

        def gcn(p):
            with act.Fori(0, BLOCKS) as c:
                act.wait_ge(s_agg, BLOCKS * p + c + 1)
                act.wait_ge(s_y, BLOCKS * (p - 1) + c + 1)
                act.activation(aggT[:, 0:HALF], psum[:, 0, 0:HALF], ACT.Copy).then_inc(s_aggT, 1)

        for l in range(3):
            act.wait_ge(s_agg, BLOCKS * (l + 1))
            split(l + 1, 1, l == 0)
            gcn(l + 1)

        def normed(nb, done):
            for c in range(BLOCKS):
                act.wait_ge(s_sh, BLOCKS * nb + c + 1)
                if c >= 2:
                    act.wait_ge(done, c - 1)
                for q in range(BT):
                    tt = c * BT + q
                    last = act.activation(work[:, c % 2, q * D:(q + 1) * D], G[:, tt, :], ACT.Relu,
                                          bias=shift[:, tt:tt + 1], scale=rstd[:, tt:tt + 1])
                last.then_inc(s_h, 1)
                if c:
                    xt(c - 1)
            xt(BLOCKS - 1)

        def xt(c):
            act.wait_ge(s_xT, c + 1)
            act.activation(XT[:, c * BW:(c + 1) * BW], pflat[:, (4 + 2 * (c % 2)) * 512:(4 + 2 * (c % 2)) * 512 + BW],
                           ACT.Copy).then_inc(s_xTs, 1)

        act.wait_ge(s_at, 16)
        act.wait_ge(s_agg, 4 * BLOCKS)
        act.wait_ge(s_w, 16 * 18)
        normed(2, s_xT)
        for l in range(2):
            for c in range(SLICES):
                k = SLICES * l + c
                act.wait_ge(s_hl, k + 1)
                act.activation(HT[:, c * SW:(c + 1) * SW], psum[:, c % 2, 0:SW], ACT.Relu,
                               bias=bcol[:, l:l + 1]).then_inc(s_hls, 1)

            def exps(c, b):
                k = SLICES * l + c
                act.wait_ge(s_nt, k + 1)
                for j in range(TILES):
                    act.activation(Z[b][:, j, :], Z[b][:, j, :], ACT.Exp, bias=neg_top[:, ds(c, 1)]).then_inc(s_e, 1)
                act.wait_ge(s_pv, TILES * (k + 3))
                act.activation(XT[:, ds(c * SW, SW)], psum[:, 5 + b, 0:SW], ACT.Copy).then_inc(s_ot, 2)

            with act.Fori(0, SLICES // 2) as i:
                c = i * 2
                exps(c, 0)
                exps(c + 1, 1)
            act.wait_ge(s_fs, 3 * l + 1)
            act.activation(wts, neg_top, ACT.Exp, bias=least, scale=-1.0).then_inc(s_wt, 1)
        act.wait_ge(s_x3, BLOCKS)
        for p in (4, 5):
            act.wait_ge(s_agg, BLOCKS * p)
            split(p, 3, p == 4)
            gcn(p)

    @block.tensor
    def _(pe):
        pe.wait_ge(s_ident, 5)
        pe.wait_ge(s_prep, 10)
        for g in range(GROUPS):
            pe.transpose(psum[0:EC, 0, g * GC:(g + 1) * GC], key[:, g, :], ident[0:GC, 0:GC])
            pe.transpose(psum[0:EC, 1, g * GC:(g + 1) * GC], slo[:, g, :], ident[0:GC, 0:GC])
            last = pe.transpose(psum[0:1, 2, g * GC:(g + 1) * GC], base[:, g:g + 1], ident[0:GC, 0:GC])
        last.then_inc(s_keyT, 1)
        pe.sem_inc(s_out, TURN)
        with pe.Fori(0, CHUNKS // TURN) as i:
            for k in range(TURN):
                if k % 4 == 0:
                    pe.wait_ge(s_hs, i * (TURN // 4) + k // 4 + 1)
                pe.wait_ge(s_hk, i * TURN + k + 1)
                pe.wait_ge(s_acc, i * TURN + TURN + k - 3)
                pe.matmul(psum[:, 4 + k % 4, 0:KEYS], hot_slo[:, k, :], hot_key[:, k % 4, :],
                          start=True, stop=True).then_inc(s_out, 1)

        def aggregate(p, c, after=None):
            pe.wait_ge(s_aggT, (BLOCKS * p + c) * 2 + 1)
            for tt in range(TILES):
                if tt % BT == 0:
                    pe.wait_ge(s_parts, BLOCKS * p + tt // BT + 1)
                for k in range(PARTS):
                    for h in range(2):
                        last = pe.matmul(psum[:, h, 0:HALF], parts[:, k, tt, :],
                                         A[:, tt, ds(c * BW + h * HALF, HALF)],
                                         start=(tt == 0 and k == 0), stop=(tt == TILES - 1 and k == PARTS - 1))
                if tt == TILES - 1:
                    last.then_inc(s_agg, 1)
                if after:
                    after(tt)

        pe.wait_ge(s_acc, BUILT)
        with pe.Fori(0, BLOCKS) as c:
            def transposed(tt):
                for n in range(PN * tt // TILES, PN * (tt + 1) // TILES):
                    q, st, k = piece(n)
                    pe.wait_ge(s_ts, c * PN + n + (2 if n == 0 else 1))
                    for j in range(k):
                        last = pe.matmul(psum[:, 2 + n % 2, j * P:(j + 1) * P],
                                         A[:, st + j, ds((c * BT + q) * P, P)], ident16, start=True, stop=True)
                    last.then_inc(s_tp, 1)

            aggregate(0, c, transposed)
            pe.wait_ge(s_hb, c * BT)
            for q in range(BT):
                for k in range(PARTS):
                    last = pe.matmul(pflat[:, 4 * 512 + q * P:4 * 512 + (q + 1) * P],
                                     parts[:, k, ds(c * BT + q, 1), :].rearrange("p a f -> p (a f)"), identb,
                                     start=(k == 0), stop=(k == PARTS - 1))
            last.then_inc(s_hTp, 1)
            pe.wait_ge(s_aggT, 2 * c + 3)
            pe.wait_ge(s_w, 16 * 6)
            for q in range(BT + 2):
                g = c * BT + q
                if q < BT:
                    if q >= 2:
                        pe.wait_ge(s_hb, g - 1)
                    pe.matmul(psum[:, 4 + q % 2, :], aggT[:, q * P:(q + 1) * P], w1, start=True, stop=True)\
                        .then_inc(s_hp, 1)
                if 1 <= q <= BT:
                    pe.wait_ge(s_hn, g)
                    pe.wait_ge(s_gel, g)
                    for k in range(4):
                        last = pe.transpose(psum[:, 6, k * P:(k + 1) * P], hid[:, (q - 1) % 2, k * P:(k + 1) * P],
                                            ident)
                    last.then_inc(s_hnT, 1)
                if q >= 2:
                    pe.wait_ge(s_gel, g)
                    pe.wait_ge(s_xn, g - 2)
                    for k in range(4):
                        last = pe.matmul(psum[:, 7, 0:D], gel[:, k, :], w2[:, k, :], start=(k == 0), stop=(k == 3))
                    last.then_inc(s_o, 1)

        def gcn(p, l):
            with pe.Fori(0, BLOCKS) as c:
                aggregate(p, c)
                pe.wait_ge(s_aggT, (BLOCKS * p + c) * 2 + 3)
                pe.wait_ge(s_u, BLOCKS * (p - 1) + c + 1)
                for q in range(BT):
                    last = pe.matmul(pflat[:, 4 * 512 + q * P:4 * 512 + (q + 1) * P], aggT[:, q * P:(q + 1) * P],
                                     wmat[:, l, :], start=True, stop=True)
                last.then_inc(s_y, 1)

        pe.wait_ge(s_w, 16 * 12)
        pe.wait_ge(s_self, 2)
        for l in range(3):
            gcn(l + 1, l)

        pe.wait_ge(s_w, 16 * 18)
        pe.wait_ge(s_u, 3 * BLOCKS + 1)
        for c in range(BLOCKS):
            pe.wait_ge(s_h, 2 * BLOCKS + c + 1)
            if c >= 2:
                pe.wait_ge(s_xTs, c - 1)
            b = (4 + 2 * (c % 2)) * 512
            for q in range(BT):
                last = pe.transpose(pflat[:, b + q * P:b + (q + 1) * P], work[:, c % 2, q * D:(q + 1) * D], ident)
            last.then_inc(s_xT, 1)
        for l in range(2):
            if l:
                pe.wait_ge(s_sc, SLICES)
            else:
                pe.wait_ge(s_xTs, BLOCKS)
            for c in range(SLICES):
                k = SLICES * l + c
                if c >= 2:
                    pe.wait_ge(s_hls, k - 1)
                pe.matmul(psum[:, c % 2, 0:SW], wmat[:, l, :], XT[:, c * SW:(c + 1) * SW], start=True, stop=True)\
                    .then_inc(s_hl, 1)
            pe.wait_ge(s_hls, SLICES * (l + 1))
            for n in range(PIECES):
                m = PIECES * l + n
                if n >= 2:
                    pe.wait_ge(s_hts, m - 1)
                for tt in range(4 * n, min(4 * n + 4, TILES)):
                    last = pe.transpose(psum[:, 2 + n % 2, (tt - 4 * n) * P:(tt - 4 * n + 1) * P],
                                        HT[:, tt * P:(tt + 1) * P], ident)
                last.then_inc(s_ht, 1)
            pe.wait_ge(s_hts, PIECES * (l + 1))

            def scores(c, j):
                m = TILES * (SLICES * l + c) + j
                pe.wait_ge(s_z, m + 1)
                pe.matmul(psum[:, j % SBANKS, 0:SW], HT[:, j * P:(j + 1) * P], HT[:, ds(c * SW, SW)],
                          start=True, stop=True).then_inc(s_s, 1)

            def weighted(c, b, j):
                k = SLICES * l + c
                if j == 0:
                    pe.wait_ge(s_ot, k + 1)
                pe.wait_ge(s_p, TILES * (k + 2) + j + 1)
                pe.matmul(psum[:, 5 + b, 0:SW], H[:, j, :], Z[b][:, j, :], start=(j == 0), stop=(j == TILES - 1))\
                    .then_inc(s_pv, 1)

            def turn_peak(c):
                pe.wait_ge(s_rm, SLICES * l + c + 1)
                pe.transpose(psum[0:1, 7, 0:P], peak, ident).then_inc(s_rmT, 1)

            def spread_top(c):
                pe.wait_ge(s_top, SLICES * l + c + 1)
                pe.matmul(psum[:, 7, 256:257], ones[0:1, :], top, start=True, stop=True).then_inc(s_tb, 1)

            def step(c, b):
                for j in range(LEAD):
                    scores(c + 1, j)
                    if j == 1:
                        turn_peak(c)
                    if j == 3:
                        spread_top(c)
                for j in range(TILES):
                    weighted(c, b, j)
                    if j + LEAD < TILES:
                        scores(c + 1, j + LEAD)

            for j in range(TILES):
                scores(0, j)
            with pe.Fori(0, (SLICES - 2) // 2) as i:
                c = i * 2
                step(c, 0)
                step(c + 1, 1)
            step(SLICES - 2, 0)
            turn_peak(SLICES - 1)
            spread_top(SLICES - 1)
            for j in range(TILES):
                weighted(SLICES - 1, 1, j)
            pe.wait_ge(s_sum, SLICES * (l + 1))
            pe.matmul(psum[:, 7, 0:SLICES], ones, sums, start=True, stop=True).then_inc(s_ls, 1)
        pe.wait_ge(s_sc, 2 * SLICES)
        for c in range(BLOCKS):
            if c >= 2:
                pe.wait_ge(s_x3, c - 1)
            b = (0 + 2 * (c % 2)) * 512
            for q in range(BT):
                tt = c * BT + q
                last = pe.matmul(pflat[:, b + q * P:b + (q + 1) * P], XT[:, tt * P:(tt + 1) * P], wmat[:, 2, :],
                                 start=True, stop=True)
            last.then_inc(s_x3p, 1)
        pe.wait_ge(s_w, 16 * 22)
        pe.wait_ge(s_x3, BLOCKS)
        for r in s_back:
            pe.wait_ge(r, 16)
        for l in range(2):
            gcn(l + 4, l)

    @block.vector
    def _(dve):
        prep = [0]

        def link(ins):
            prep[0] += 1
            ins.then_inc(s_prep, 1)
            dve.wait_ge(s_prep, prep[0])

        for s, v in ((s_aggT, 1), (s_ts, 2), (s_x1, 16), (s_o, 1), (s_y, 1), (s_u, 1), (s_g, 1), (s_gel, 1), (s_ot, 2), (s_p, 2 * TILES), (s_z, SBANKS), (s_pv, 2 * TILES)):
            if v:
                dve.sem_inc(s, v)
        for b in range(STAGES):
            dve.sem_inc(s_td[b], 16)
        for g in range(BLOCKS):
            dve.sem_inc(s_ad[g], 16)
        dve.memset(ones, 1.0).then_inc(s_ones, 1)
        dve.wait_ge(s_iota, 1)
        dve.tensor_copy(iota16, iota_i).then_inc(s_iota16, 1)
        dve.wait_ge(s_edges, 32)
        link(dve.tensor_copy(rel, edges_i[:, 0]))
        link(dve.tensor_reduce(base, rel, AX.X, ALU.min))
        link(dve.tensor_tensor(rel, rel, base.unsqueeze(2).broadcast_to([GC, GROUPS, EC]), ALU.subtract))
        link(dve.tensor_scalar(tmp_i, edges_i[:, 1], 7, None, ALU.arith_shift_right))
        link(dve.tensor_copy(shi, tmp_i))
        link(dve.tensor_scalar(edges_i[:, 0], edges_i[:, 1], 127, None, ALU.bitwise_and))
        link(dve.tensor_copy(slo, edges_i[:, 0]))
        link(dve.scalar_tensor_tensor(out=key, in0=shi, scalar=float(WIN), in1=rel, op0=ALU.mult, op1=ALU.add))
        link(dve.tensor_scalar(tmp_f, rel, float(WIN), FAR, ALU.is_ge, ALU.mult))
        link(dve.tensor_tensor(key, key, tmp_f, ALU.add))
        dve.memset(A[:, 0:TILES // 2, :], 0.0).then_inc(s_zero, 1)
        dve.wait_ge(s_keyT, 1)
        dve.memset(keyT[:, CHUNKS:], -1.0).then_inc(s_keysb, 1)
        dve.tensor_copy(keyT[:, 0:CHUNKS], psum[0:EC, 0, 0:CHUNKS]).then_inc(s_keysb, 1)
        dve.tensor_scalar(nsloT, psum[0:EC, 1, 0:CHUNKS], -1.0, None, ALU.mult).then_inc(s_keysb, 1)
        dve.tensor_copy(base_i, psum[0:1, 2, 0:CHUNKS]).then_inc(s_base, 1)
        dve.wait_ge(s_keysb, 3)
        dve.wait_ge(s_base, 1)
        dve.wait_ge(s_zero, 2)
        dve.sem_inc(s_acc, TURN)

        def hot(i, k):
            dve.wait_ge(s_out, i * TURN + TURN + k - 3)
            dve.tensor_scalar(hot_key[:, k % 4, :], iota16[0:EC, :], keyT[:, ds(i * TURN + k, 1)], None,
                              ALU.is_equal).then_inc(s_hk, 1)

        for k in range(AHEAD):
            hot(0, k)
        with dve.Fori(0, CHUNKS // TURN) as i:
            _, lows = nc.values_load_multi_w_load_instructions(
                base_i[:, ds(i * TURN, TURN)], engines=[mybir.EngineType.DVE], min_val=0, max_val=N - 1,
                skip_runtime_bounds_check_because="a destination is a node: 0 to N - 1")

            def add(k, lo):
                dve.wait_ge(s_out, i * TURN + TURN + k + 1)
                dve.wait_ge(s_acc, i * TURN + TURN + k)
                win = A[:, :, ds(lo, WIN)]
                dve.tensor_tensor(win, win, psum[:, 4 + k % 4, 0:KEYS].rearrange("p (t w) -> p t w", w=WIN),
                                  ALU.add).then_inc(s_acc, 1)

            for k in range(TURN):
                hot(i, k + AHEAD)
                add(k, lows[k])
        dve.wait_ge(s_acc, BUILT)

        def flat(v):
            return v.rearrange("p t f -> p (t f)")

        def norm_block(nb, c, degree):
            n = BLOCKS * nb + c + 1
            for tt in range(c * BT, (c + 1) * BT):
                last = dve.bn_stats(stats[:, tt, :], G[:, tt, :])
            last.then_inc(s_bn, 1)
            dve.wait_ge(s_bn, n)
            for tt in range(c * BT, (c + 1) * BT):
                last = dve.bn_aggr(mean_var[:, tt, :], stats[:, tt, :])
            last.then_inc(s_mv, 1)
            dve.wait_ge(s_mv, n)
            dve.tensor_scalar(rstd[:, blk(c)], mean_var[:, blk(c), 1], LN_EPS, None, ALU.add)\
                .then_inc(s_ve, 1)
            dve.wait_ge(s_rs, n)
            if degree:
                link(dve.tensor_tensor(rstd[:, blk(c)], rstd[:, blk(c)], dinv[:, blk(c)], ALU.mult))
            dve.scalar_tensor_tensor(out=shift[:, blk(c)], in0=mean_var[:, blk(c), 0], scalar=-1.0,
                                     in1=rstd[:, blk(c)], op0=ALU.mult, op1=ALU.mult).then_inc(s_sh, 1)

        def norm_stats(nb, degree):
            for c in range(BLOCKS):
                norm_block(nb, c, degree)

        def split(p, nb, normal, degree):
            for c in range(BLOCKS + 2):
                if c < BLOCKS and normal:
                    norm_block(nb, c, degree)
                if 1 <= c <= BLOCKS:
                    n = BLOCKS * p + c
                    dve.wait_ge(s_hi, n)
                    if c >= 3:
                        dve.wait_ge(s_mid, n - 2)
                        dve.wait_ge(s_parts, n - 2)
                    if not normal:
                        dve.wait_ge(s_g, BLOCKS * (p - 2) + c + 1)
                    src = work[:, (c - 1) % 2, :] if normal else flat(G[:, blk(c - 1), :])
                    dve.tensor_tensor(rest[:, (c - 1) % 2, :], src, flat(parts[:, 0, blk(c - 1), :]),
                                      ALU.subtract).then_inc(s_r1, 1)
                if c >= 2:
                    n = BLOCKS * p + c - 1
                    dve.wait_ge(s_mid, n)
                    dve.wait_ge(s_r1, n)
                    dve.tensor_tensor(flat(parts[:, 2, blk(c - 2), :]), rest[:, c % 2, :],
                                      flat(parts[:, 1, blk(c - 2), :]), ALU.subtract).then_inc(s_parts, 1)

        dve.wait_ge(s_x, 16 * (BLOCKS + 1))
        split(0, 0, True, False)
        dve.wait_ge(s_w, 16 * 6)
        with dve.Fori(0, BLOCKS) as c:
            dve.wait_ge(s_agg, c + 1)
            dve.wait_ge(s_hT, c + 1)
            for h in range(2):
                dve.tensor_tensor(aggT[:, h * HALF:(h + 1) * HALF], psum[:, h, 0:HALF],
                                  hT[:, h * HALF:(h + 1) * HALF], ALU.add).then_inc(s_aggT, 1)
            dve.wait_ge(s_xb, 32 * (c + 1))
            dve.tensor_tensor(xnew, xnew, brow[:, 0, :].unsqueeze(1).broadcast_to([P, BT, D]), ALU.add)\
                .then_inc(s_xbb, 1)
            for q in range(BT + 2):
                g = c * BT + q
                b = q % 2
                if q < BT:
                    if q >= 2:
                        dve.wait_ge(s_hnT, g - 1)
                    dve.wait_ge(s_hp, g + 1)
                    dve.tensor_tensor(hid[:, b, :], psum[:, 4 + b, :], b1row, ALU.add).then_inc(s_hb, 1)
                    dve.wait_ge(s_hb, g + 1)
                    dve.bn_stats(hstat, hid[:, b, :]).then_inc(s_hbn, 1)
                if 1 <= q <= BT:
                    dve.wait_ge(s_hrs, g)
                if q < BT:
                    dve.wait_ge(s_hbn, g + 1)
                if 1 <= q <= BT:
                    dve.tensor_scalar(hid[:, 1 - b, :], hid[:, 1 - b, :], hmv[:, 1 - b, 0:1],
                                      hrstd[:, ds((g - 1) % 2, 1)], ALU.subtract, ALU.mult).then_inc(s_hn, 1)
                elif q == 0:
                    dve.memset(scrap, 0.0)
                if q < BT:
                    dve.bn_aggr(hmv[:, b, :], hstat).then_inc(s_hmv, 1)
                    dve.wait_ge(s_hmv, g + 1)
                    dve.tensor_scalar(hrstd[:, ds(g % 2, 1)], hmv[:, b, 1:2], LN_EPS, None, ALU.add).then_inc(s_hve, 1)
                if q >= 2:
                    dve.wait_ge(s_o, g)
                    if q == 2:
                        dve.wait_ge(s_xbb, c + 1)
                    dve.tensor_tensor(xnew[:, q - 2, :], xnew[:, q - 2, :], psum[:, 7, 0:D], ALU.add)\
                        .then_inc(s_xn, 1)

        dve.wait_ge(s_ts, BLOCKS * PN + 2)
        dve.tensor_reduce(dinv, deg_parts, AX.X, ALU.add).then_inc(s_dg, 1)
        dve.wait_ge(s_dg, 1)
        dve.tensor_scalar(dinv, dinv, 1.0, 1.0, ALU.add, ALU.max).then_inc(s_dg, 1)
        dve.wait_ge(s_agg, BLOCKS)
        dve.wait_ge(s_tp, BLOCKS * PN)
        W = NPAD + P
        dve_diag = Aflat[:, 0:(TILES - 1) * W].rearrange("p (t w) -> p t w", w=W)[:, :, 0:P]
        dve.tensor_tensor(dve_diag, dve_diag, ident16.unsqueeze(1).broadcast_to([P, TILES - 1, P]), ALU.add)\
            .then_inc(s_self, 1)
        lastd = A[:, TILES - 1, (TILES - 1) * P:]
        dve.tensor_tensor(lastd, lastd, ident16, ALU.add).then_inc(s_self, 1)

        def gcn(p, l, final):
            with dve.Fori(0, BLOCKS) as c:
                n = BLOCKS * (p - 1) + c + 1
                dve.wait_ge(s_agg, BLOCKS * p + c + 1)
                dve.wait_ge(s_y, n)
                dve.tensor_copy(aggT[:, HALF:BW], psum[:, 1, 0:HALF]).then_inc(s_aggT, 1)
                dve.wait_ge(s_y, n + 1)
                u = work[:, 0, :].rearrange("p (t f) -> p t f", t=BT)
                v = work[:, 1, :].rearrange("p (t f) -> p t f", t=BT)
                y = pflat[:, 4 * 512:4 * 512 + BW].rearrange("p (t f) -> p t f", t=BT)
                d = dinv[:, blk(c)].unsqueeze(2).broadcast_to([P, BT, D])
                dve.tensor_tensor(u, y, d, ALU.mult).then_inc(s_u, 1)
                dve.wait_ge(s_u, n + 1)
                dve.tensor_tensor(v, u, brow[:, l, :].unsqueeze(1).broadcast_to([P, BT, D]), ALU.add)\
                    .then_inc(s_ub, 1)
                dve.wait_ge(s_ub, n)
                if final:
                    dve.tensor_tensor(G[:, blk(c), :], G[:, blk(c), :], v, ALU.add).then_inc(s_g, 1)
                else:
                    dve.scalar_tensor_tensor(out=G[:, blk(c), :], in0=v, scalar=0.0, in1=d, op0=ALU.max,
                                             op1=ALU.mult).then_inc(s_g, 1)

        dve.wait_ge(s_gx, 16 * BLOCKS)
        dve.wait_ge(s_dinv, 1)
        dve.wait_ge(s_w, 16 * 12)
        for l in range(3):
            split(l + 1, 1, l == 0, True)
            if l == 2:
                dve.wait_ge(s_gx, 32 * BLOCKS)
            gcn(l + 1, l, l == 2)

        dve.wait_ge(s_g, 3 * BLOCKS + 1)
        norm_stats(2, False)
        dve.wait_ge(s_w, 16 * 18)
        dve.wait_ge(s_h, 3 * BLOCKS)
        dve.wait_ge(s_agg, 4 * BLOCKS)
        for c in range(BLOCKS):
            dve.tensor_tensor(G[:, blk(c), :], G[:, blk(c), :],
                              brow[:, 0, :].unsqueeze(1).broadcast_to([P, BT, D]), ALU.add).then_inc(s_xbb, 1)
        for l in range(2):
            for n in range(PIECES):
                dve.wait_ge(s_ht, PIECES * l + n + 1)
                w = min(4, TILES - 4 * n)
                dve.tensor_copy(flat(H[:, 4 * n:4 * n + w, :]), psum[:, 2 + n % 2, 0:w * P]).then_inc(s_hts, 1)

            def edges(c, b, j):
                k = SLICES * l + c
                dve.wait_ge(s_ad[j // BT], 16 * (k + 2))
                h = j // SBANKS % 2
                dve.tensor_scalar(mask[:, SBANKS * h:SBANKS * (h + 1), :], Ab[b][:, j:j + SBANKS, :], 1.0, None,
                                  ALU.min).then_inc(s_mask, 1)

            def masked_waits(c, j):
                m = TILES * (SLICES * l + c) + j
                dve.wait_ge(s_s, m + 1)
                dve.wait_ge(s_pv, m + 1)
                if j % SBANKS == 0:
                    dve.wait_ge(s_mask, BLOCKS * (SLICES * l + c) + j // SBANKS + 1)

            def masked(b, j):
                dve.tensor_tensor_reduce(Z[b][:, j, :], mask[:, j % (2 * SBANKS), :], psum[:, j % SBANKS, 0:SW], 1.0,
                                         0.0, ALU.mult, ALU.max, rowmax[:, j:j + 1]).then_inc(s_z, 1)

            def weights(c, b, j):
                k = SLICES * l + c
                dve.wait_ge(s_e, TILES * k + j + 1)
                dve.tensor_tensor_reduce(Z[b][:, j, :], Z[b][:, j, :], Ab[b][:, j, :], 1.0, 0.0,
                                         ALU.mult, ALU.add, rowsum[:, b, j:j + 1]).then_inc(s_p, 1)

            def slice_sum(c, b):
                dve.wait_ge(s_p, TILES * (SLICES * l + c + 3))
                dve.tensor_reduce(sums[:, ds(c, 1)], rowsum[:, b, :], AX.X, ALU.add).then_inc(s_sum, 1)

            def slice_peak(c):
                dve.wait_ge(s_z, TILES * (SLICES * l + c + 1) + SBANKS)
                dve.tensor_reduce(peak, rowmax, AX.X, ALU.max).then_inc(s_rm, 1)

            def slice_top(c):
                dve.wait_ge(s_rmT, SLICES * l + c + 1)
                dve.tensor_reduce(top, psum[0:1, 7, 0:P], AX.X, ALU.max).then_inc(s_top, 1)

            def slice_neg(c):
                dve.wait_ge(s_tb, SLICES * l + c + 1)
                dve.tensor_scalar(neg_top[:, ds(c, 1)], psum[:, 7, 256:257], -1.0, None, ALU.mult).then_inc(s_nt, 1)

            def step(c, b):
                slice_peak(c)
                edges(c + 1, 1 - b, 0)
                masked_waits(c + 1, 0)
                slice_top(c)
                masked(1 - b, 0)
                masked_waits(c + 1, 1)
                slice_neg(c)
                masked(1 - b, 1)
                for j in range(TILES):
                    n = j + 2
                    if n < TILES:
                        if n % SBANKS == 0:
                            edges(c + 1, 1 - b, n)
                        masked_waits(c + 1, n)
                    weights(c, b, j)
                    if n < TILES:
                        masked(1 - b, n)
                slice_sum(c, b)

            for j in range(TILES):
                if j % SBANKS == 0:
                    edges(0, 0, j)
                masked_waits(0, j)
                masked(0, j)
            with dve.Fori(0, (SLICES - 2) // 2) as i:
                c = i * 2
                step(c, 0)
                step(c + 1, 1)
            step(SLICES - 2, 0)
            slice_peak(SLICES - 1)
            slice_top(SLICES - 1)
            slice_neg(SLICES - 1)
            for j in range(TILES):
                weights(SLICES - 1, 1, j)
            slice_sum(SLICES - 1, 1)
            dve.wait_ge(s_nt, SLICES * (l + 1))
            dve.tensor_reduce(least, neg_top, AX.X, ALU.min).then_inc(s_fs, 1)
            dve.wait_ge(s_ls, l + 1)
            dve.wait_ge(s_wt, l + 1)
            dve.tensor_tensor_reduce(scale8, wts, psum[:, 7, 0:SLICES], 1.0, 0.0, ALU.mult, ALU.add,
                                     total[:, 0:1]).then_inc(s_fs, 1)
            dve.wait_ge(s_fs, 3 * l + 2)
            dve.reciprocal(total[:, 1:2], total[:, 0:1]).then_inc(s_fs, 1)
            dve.wait_ge(s_fs, 3 * l + 3)
            link(dve.tensor_scalar(scale8, wts, total[:, 1:2], None, ALU.mult))
            dve.wait_ge(s_ot, SLICES * (l + 1) + 2)
            for c in range(SLICES):
                v = XT[:, c * SW:(c + 1) * SW]
                dve.tensor_scalar(v, v, scale8[:, c:c + 1], None, ALU.mult).then_inc(s_sc, 1)
        dve.wait_ge(s_xbb, 2 * BLOCKS)
        for c in range(BLOCKS):
            dve.wait_ge(s_x3p, c + 1)
            b = (0 + 2 * (c % 2)) * 512
            g = flat(G[:, blk(c), :])
            dve.tensor_tensor(g, g, pflat[:, b:b + BW], ALU.add).then_inc(s_x3, 1)

        dve.wait_ge(s_x3, BLOCKS)
        dve.wait_ge(s_w, 16 * 22)
        for l in range(2):
            split(l + 4, 3, l == 0, True)
            dve.wait_ge(s_x3d, 16 * BLOCKS)
            if l:
                dve.wait_ge(s_gx, 48 * BLOCKS)
            gcn(l + 4, l, l == 1)


_INS = ["x", "src", "dst", "L0_gnn_eps", "L0_gnn_W1", "L0_gnn_b1", "L0_gnn_ln_g", "L0_gnn_ln_b", "L0_gnn_W2",
        "L0_gnn_b2", "L1_gnn_W1", "L1_gnn_b1", "L1_gnn_W2", "L1_gnn_b2", "L1_gnn_W3", "L1_gnn_b3",
        "L2_gnn_W0", "L2_gnn_b0", "L2_gnn_W1", "L2_gnn_b1", "L2_gnn_W2", "L2_gnn_b2",
        "L3_gnn_W1", "L3_gnn_b1", "L3_gnn_W2", "L3_gnn_b2"]


def kernel(**inputs):
    import numpy as _np
    import concourse.bacc as _bacc
    from concourse import mybir as _mybir
    from concourse.bass_utils import run_bass_kernel_spmd as _run

    nc = _bacc.Bacc("TRN2", target_bir_lowering=False, num_devices=1)
    arrays, t = {}, {}
    for name in _INS:
        a = _np.ascontiguousarray(inputs[name])
        if a.ndim < 2:
            a = a.reshape(1, -1)
        if a.ndim == 3:
            a = a.reshape(a.shape[1:])
        arrays["in_" + name] = a
        t[name] = nc.dram_tensor("in_" + name, a.shape, _mybir.dt.from_np(a.dtype), kind="ExternalInput").ap()
    t["out"] = nc.dram_tensor("out", (N, D), F32, kind="ExternalOutput").ap()
    gnn_kernel(nc, t)
    r = _run(nc, [arrays], core_ids=[0])
    return r.results[0]["out"]
```

```python
from contextlib import ExitStack

import concourse.bass as bass
from concourse import mybir

F32 = mybir.dt.float32
FP16 = mybir.dt.float16
I32 = mybir.dt.int32
ALU = mybir.AluOpType
ACT = mybir.ActivationFunctionType
AX = mybir.AxisListType
ds = bass.ds

P = 128
D = 128
N = 3125
TILES = -(-N // P)
NPAD = TILES * P
LAST = N - (TILES - 1) * P
HID = 4 * D
LN_EPS = 1e-5

E_EDGES = 50000
EC = 125
CHUNKS = E_EDGES // EC
GROUPS = 4
GC = CHUNKS // GROUPS
WIN = 20
KEYS = TILES * WIN
ROUNDS = -(-N // WIN)
FAR = 10000.0
TURN = 16
BANKS = 8
HT_AT = TILES - 4
HOTS = 8
PREP_TILES = 3
DVE_ZEROS = 2
ACT_ZEROS = 11

PREPARED = 14
WIDE_STEPS = 4
AHEAD = 6

BLOCKS = 5
BT = TILES // BLOCKS
BW = BT * P
HALF = BW // 2
PIECES = -(-TILES // 4)
STAGES = 5

SLICES = 10
SW = NPAD // SLICES
LEAD = 6
SBANKS = 5

PARTS = 2
LN_SCALE = 4096.0
LOW_SCALE = 2048.0
TOP_POWER = 14
LEAST_TOP = 2.0 ** -60
EXPONENT = 0x7F800000
SCALE_STEPS = 5
ENDS = 3
Y_AT = 6


def gnn_kernel(nc, t):
    with ExitStack() as ctx:
        build(nc, t, ctx)


def build(nc, t, ctx):
    def sem(name):
        return ctx.enter_context(nc.semaphore(name))

    A = ctx.enter_context(nc.sbuf_tensor("adjacency", [P, TILES, NPAD], FP16))
    ARENA = (212800 - TILES * NPAD * 2) // 4
    arena = ctx.enter_context(nc.sbuf_tensor("arena", [P, ARENA], F32))
    at = [0]

    def take(cols, dt=F32, start=None):
        a = at[0] if start is None else start
        width = cols if dt in (F32, I32) else -(-cols // 2)
        at[0] = a + width
        assert at[0] <= ARENA, (at[0], ARENA)
        v = arena[:, a:a + width]
        return v if dt == F32 else v.bitcast(dt)

    ident = take(P)
    ident16 = take(P, FP16)
    ones = take(P)
    one_eps = take(2)[:, 0:1]
    dinv = take(TILES + 1)[:, 0:TILES]
    deg_parts = take(TILES * PIECES + 1)[:, 0:TILES * PIECES].rearrange("p (t k) -> p t k", t=TILES)
    half_neg = take(8)
    hstat = take(6)
    scrap = take(2)
    zero = take(2)[:, 0:1]
    scales = take(2)
    top_bits = take(2)[0:1, :]
    block_top = take(BLOCKS + 1)[:, 0:BLOCKS]
    dinv_out = take(TILES + 1)[:, 0:TILES]
    wide = take(2, I32)[0:1, 0:1]
    peak = take(2)[:, 0:1]
    top = take(2)[0:1, 0:1]
    neg_top = take(SLICES)
    least = take(2)[:, 0:1]
    wts = take(SLICES)
    sums = take(SLICES)
    total = take(2)
    scale8 = take(SLICES)
    bcol = take(2)
    hmv = take(4).rearrange("p (b s) -> p b s", b=2)
    hrstd = take(2)
    stats = take(TILES * 6 + 2)[:, 0:TILES * 6].rearrange("p (t s) -> p t s", t=TILES)
    mean_var = take(TILES * 2)[:, :].rearrange("p (t s) -> p t s", t=TILES)
    rstd = take(TILES + 1)[:, 0:TILES]
    shift = take(TILES + 1)[:, 0:TILES]
    gamma = take(4)
    beta = take(4)
    wmat = take(3 * D).rearrange("p (l f) -> p l f", l=3)
    brow = take(3 * D).rearrange("p (l f) -> p l f", l=3)
    BUILD_AT = at[0]
    aggT = take(BW)
    work = take(2 * BW).rearrange("p (b n) -> p b n", b=2)
    rest = take(2 * BW).rearrange("p (b n) -> p b n", b=2)
    PARTS_AT = at[0]
    parts = take(PARTS * TILES * D, FP16).rearrange("p (k t f) -> p k t f", k=PARTS, t=TILES)
    OVER = at[0]
    G = take(TILES * D).rearrange("p (t f) -> p t f", t=TILES)
    at[0] = OVER
    w1 = take(HID)
    w2 = take(HID).rearrange("p (k f) -> p k f", k=4)
    b1row = take(HID)
    gel = take(HID).rearrange("p (k f) -> p k f", k=4)
    stage = take(STAGES * 512, FP16).rearrange("p (b n) -> p b n", b=STAGES)
    AFTER_G = max(at[0], OVER + TILES * D)
    hT = work[:, 0, :]
    xnew = work[:, 1, :].rearrange("p (t f) -> p t f", t=BT)
    hid = rest.rearrange("p b n -> p (b n)")[:, 0:2 * HID].rearrange("p (b n) -> p b n", b=2)

    A32 = A[:, :, :].rearrange("p t n -> p (t n)").bitcast(F32)
    cut = [0]

    def carve(cols):
        cut[0] += cols
        return A32[:, cut[0] - cols:cut[0]]

    Z = [carve(TILES * SW).rearrange("p (t n) -> p t n", t=TILES)]
    Ab = [carve(TILES * SW // 2).bitcast(FP16).rearrange("p (t n) -> p t n", t=TILES)]
    mask = carve(SBANKS * SW).bitcast(FP16).rearrange("p (b n) -> p b n", b=2 * SBANKS)
    EARLY = cut[0] * 2 // NPAD
    Z.append(carve(TILES * SW).rearrange("p (t n) -> p t n", t=TILES))
    Ab.append(carve(TILES * SW // 2).bitcast(FP16).rearrange("p (t n) -> p t n", t=TILES))
    XT = carve(NPAD)
    rowmax = carve(TILES + 1)[:, 0:TILES]
    rowsum = carve(2 * TILES).rearrange("p (c t) -> p c t", c=2)
    GONE = -(-cut[0] * 2 // NPAD)
    HT = arena[:, BUILD_AT:BUILD_AT + NPAD]
    H = parts.rearrange("p k t f -> p (k t f)").bitcast(F32)[:, 0:NPAD].rearrange("p (t f) -> p t f", t=TILES)

    psum = ctx.enter_context(nc.psum_tensor("psum", [P, 8, 512], F32))
    pflat = psum[:, :, :].rearrange("p b n -> p (b n)")

    Ad = nc.dram_tensor("adjacency_by_dst", (TILES, P, NPAD), FP16, kind="Internal").ap()
    At = nc.dram_tensor("adjacency_by_src", (P, TILES * NPAD), FP16, kind="Internal").ap()
    x3 = nc.dram_tensor("x_after_l2", (NPAD, D), F32, kind="Internal").ap()
    x3v = x3.rearrange("(t p) f -> p t f", p=P)
    x1 = nc.dram_tensor("x_after_l0", (NPAD, D), F32, kind="Internal").ap()
    x1v = x1.rearrange("(t p) f -> p t f", p=P)
    xin_v = t["x"][0:(TILES - 1) * P, :].rearrange("(t p) f -> p t f", p=P)
    Aflat = A[:, :, :].rearrange("p t n -> p (t n)")

    at[0] = BUILD_AT
    keyT = take(CHUNKS + AHEAD + 1)[0:EC]
    sloT = take(CHUNKS + AHEAD + 1)[0:EC]
    dstT = take(CHUNKS)[0:EC]
    shiT = take(CHUNKS)[0:EC]
    base_i = take(CHUNKS, I32)[0:1]
    widest = take(2)[0:1, 0:1]
    iota16 = take(KEYS, FP16)
    hot_key = take(HOTS * KEYS, FP16)[0:EC].rearrange("p (b n) -> p b n", b=HOTS)
    counts = take(BANKS * KEYS, FP16).rearrange("p (b n) -> p b n", b=BANKS)
    iota_i = counts[:, 0:2, :].rearrange("p b n -> p (b n)").bitcast(I32)
    assert at[0] <= OVER
    at[0] = AFTER_G
    out_of = take(2 * CHUNKS)[0:EC].rearrange("p (s k) -> p s k", s=2)
    hot_slo = take(HOTS * P, FP16)[0:EC].rearrange("p (b n) -> p b n", b=HOTS)

    prep_at = [(TILES - PREP_TILES) * NPAD // 2]

    def edge_array(cols=GROUPS * EC, dt=F32):
        v = A32[0:GC, prep_at[0]:prep_at[0] + cols]
        prep_at[0] += cols
        assert prep_at[0] <= TILES * NPAD // 2
        if cols == GROUPS * EC:
            v = v.rearrange("p (g j) -> p g j", g=GROUPS)
        return v if dt == F32 else v.bitcast(dt)

    dst_i, src_i, part_i = edge_array(dt=I32), edge_array(dt=I32), edge_array(dt=I32)
    dst_f, rel, shi, slo = edge_array(), edge_array(), edge_array(), edge_array()
    key, beyond = edge_array(), edge_array()
    base, base_ii = edge_array(GROUPS), edge_array(GROUPS, I32)
    span = edge_array(2)[:, 0:1]

    s_edges = sem("edges_loaded")
    s_ones = sem("ones_made")
    s_iota = sem("iota_made")
    s_iota16 = sem("iota16_made")
    s_ident = sem("ident_made")
    s_zero = sem("a_zeroed")
    s_prep = sem("dve_prep")
    s_keyT = sem("keys_transposed")
    s_keysb = sem("keys_in_sbuf")
    s_hk = sem("hot_pair_ready")
    s_out = sem("chunk_product_ready")
    s_cnt = sem("chunk_pair_counts_ready")
    s_wkey = sem("wide_round_key_steps")
    s_whot = sem("wide_hots_ready")
    s_wout = sem("wide_products_ready")
    s_wadd = sem("wide_window_ready")
    s_acc = sem("chunk_added")
    s_base = sem("bases_in_sbuf")

    BUILT = TURN + CHUNKS + 1

    s_x = sem("x_loaded")
    s_w = sem("layer_weights_loaded")
    s_eps = sem("eps_loaded")
    s_misc = sem("small_constants_ready")
    s_bn = sem("tile_stats_ready")
    s_mv = sem("mean_var_ready")
    s_ve = sem("variance_plus_eps_ready")
    s_rs = sem("rstd_ready")
    s_sh = sem("shift_ready")
    s_h = sem("h_block_ready")
    s_hi = sem("hi_part_ready")
    s_r1 = sem("rest_ready")
    s_scale = sem("pass_scale_ready")
    s_st = sem("pass_scale_steps")
    s_low = sem("low_half_scaled")
    s_bt = sem("block_top_ready")
    s_sp = sem("pass_scale_products")
    s_parts = sem("block_parts_ready")
    s_agg = sem("agg_block_ready")
    s_aggT = sem("agg_half_in_sbuf")
    s_hTp = sem("h_transposed")
    s_hT = sem("scaled_h_in_sbuf")
    s_y = sem("weight_product_ready")
    s_u = sem("scaled_product_ready")
    s_ub = sem("biased_product_ready")
    s_g = sem("block_output_ready")
    s_hp = sem("hidden_product_ready")
    s_hb = sem("hidden_biased")
    s_hbn = sem("hidden_stats_ready")
    s_hmv = sem("hidden_mean_var_ready")
    s_hve = sem("hidden_variance_plus_eps_ready")
    s_hrs = sem("hidden_rstd_ready")
    s_hn = sem("hidden_normalised")
    s_hnT = sem("hidden_transposed")
    s_gel = sem("gelu_ready")
    s_o = sem("mlp_product_ready")
    s_xb = sem("x_block_loaded")
    s_xbb = sem("x_block_biased")
    s_xn = sem("x_tile_updated")
    s_x1 = sem("x1_block_stored")
    s_tp = sem("adjacency_piece_transposed")
    s_ts = sem("adjacency_piece_staged")
    s_td = [sem(f"adjacency_stage{b}_stored") for b in range(STAGES)]
    s_dg = sem("degree_steps")
    s_dinv = sem("dinv_ready")
    s_self = sem("self_loops_added")
    s_at = sem("adjacency_saved")
    s_fin = sem("output_stored")
    s_gx = sem("x_reloaded")

    s_xT = sem("x_transposed")
    s_xTs = sem("xT_in_sbuf")
    s_hl = sem("attention_h_product")
    s_hls = sem("attention_hT_ready")
    s_ht = sem("attention_h_transposed")
    s_hts = sem("attention_h_ready")
    s_ad = [sem(f"adjacency_slice_group{g}_loaded") for g in range(BLOCKS)]
    s_mask = sem("mask_ready")
    s_s = sem("scores_ready")
    s_z = sem("masked_scores_ready")
    s_rm = sem("row_peak_ready")
    s_rmT = sem("row_peak_transposed")
    s_top = sem("slice_top_ready")
    s_tb = sem("slice_top_broadcast")
    s_nt = sem("slice_neg_top_ready")
    s_e = sem("exp_ready")
    s_sum = sem("slice_row_sums_ready")
    s_p = sem("edge_weights_ready")
    s_pv = sem("weighted_sum_step")
    s_ot = sem("slice_sum_in_sbuf")
    s_fs = sem("softmax_total_steps")
    s_wt = sem("slice_weights_ready")
    s_ls = sem("slice_sums_ready")
    s_sc = sem("slices_scaled")
    s_x3p = sem("attention_output_product")
    s_x3 = sem("x3_ready")
    s_x3d = sem("x3_saved")
    s_back = [sem(f"adjacency_{w}_reloaded") for w in ("first_tiles", "next_tiles", "last_tiles")]

    def dst_view(a):
        return a.rearrange("o (g c j) -> c (o g) j", g=GROUPS, c=GC)

    block = ctx.enter_context(nc.Block())



    def blk(c):
        return ds(c * BT, BT)

    PN = BT * PIECES

    def piece(n):
        q, k = divmod(n, PIECES)
        return q, 4 * k, min(4, TILES - 4 * k)

    def pieces_at(tt):
        steps = TILES - ENDS
        return range(PN * min(tt, steps) // steps, PN * min(tt + 1, steps) // steps)

    def mlp_at(tt):
        q, r = divmod(tt, 3)
        step, q = (("hidden", q), ("output", q - 2), ("transpose", q - 1))[r]
        return (step if 0 <= q < BT else None), q

    @block.sync
    def _(sp):
        sp.dma_start(dst_i, dst_view(t["dst"])).then_inc(s_edges, 16)
        sp.dma_start(src_i, dst_view(t["src"])).then_inc(s_edges, 16)
        for c in range(BLOCKS):
            e = min((c + 1) * BT, TILES - 1)
            sp.dma_start(G[:, c * BT:e, :], xin_v[:, c * BT:e, :]).then_inc(s_x, 16)
        sp.wait_ge(s_misc, 1)
        sp.dma_start(G[0:LAST, TILES - 1, :], t["x"][(TILES - 1) * P:N, :]).then_inc(s_x, 16)
        sp.dma_start(one_eps, t["L0_gnn_eps"].partition_broadcast(P).rearrange("p a b -> p (a b)")).then_inc(s_eps, 16)
        sp.wait_ge(s_r1, BLOCKS)
        sp.dma_start(w1, t["L0_gnn_W1"]).then_inc(s_w, 16)
        sp.dma_start(w2, t["L0_gnn_W2"].rearrange("(k p) f -> p k f", p=P)).then_inc(s_w, 16)
        sp.dma_start(b1row, t["L0_gnn_b1"].partition_broadcast(P).rearrange("p a b -> p (a b)")).then_inc(s_w, 16)
        sp.dma_start(gamma, t["L0_gnn_ln_g"].rearrange("o (k p) -> p (o k)", p=P),
                     allow_slow_non_contiguous=True).then_inc(s_w, 16)
        sp.dma_start(beta, t["L0_gnn_ln_b"].rearrange("o (k p) -> p (o k)", p=P),
                     allow_slow_non_contiguous=True).then_inc(s_w, 16)
        sp.dma_start(brow[:, 0, :], t["L0_gnn_b2"].partition_broadcast(P).rearrange("p a b -> p (a b)")).then_inc(s_w, 16)
        sp.wait_ge(s_parts, BLOCKS)

        def pieces_out(c):
            for n in range(PN):
                q, st, k = piece(n)
                sp.wait_ge(s_ts, c * PN + n + 1 + 2)
                sp.dma_start(Ad[ds(c * BT + q, 1), :, st * P:(st + k) * P].rearrange("o p n -> (o p) n"),
                             stage[:, n % STAGES, 0:k * P]).then_inc(s_td[n % STAGES], 16)

        def x1_out(m):
            sp.wait_ge(s_xn, (m + 1) * BT + 1)
            sp.dma_start(x1v[:, blk(m), :], xnew[:, :, :]).then_inc(s_x1, 16)

        pieces_out(0)
        with sp.Fori(1, BLOCKS) as c:
            sp.wait_ge(s_x1, 16 * c)
            sp.dma_start(xnew[:, :, :], xin_v[:, ds((c - 1) * BT, BT), :]).then_inc(s_xb, 32)
            pieces_out(c)
            x1_out(c - 1)
        sp.wait_ge(s_x1, 16 * BLOCKS)
        sp.dma_start(xnew[:, 0:BT - 1, :], xin_v[:, (BLOCKS - 1) * BT:, :]).then_inc(s_xb, 16)
        sp.dma_start(xnew[0:LAST, BT - 1, :], t["x"][(TILES - 1) * P:N, :]).then_inc(s_xb, 16)
        x1_out(BLOCKS - 1)
        sp.wait_ge(s_x1, 16 * BLOCKS + 16)
        sp.wait_ge(s_o, TILES)
        for b in range(STAGES):
            sp.wait_ge(s_td[b], 16 + 16 * BLOCKS * PN // STAGES)
        for c in range(BLOCKS):
            sp.dma_start(G[:, blk(c), :], x1v[:, blk(c), :]).then_inc(s_gx, 16)
        for l in range(3):
            sp.dma_start(wmat[:, l, :], t[f"L1_gnn_W{l + 1}"]).then_inc(s_w, 16)
            sp.dma_start(brow[:, l, :], t[f"L1_gnn_b{l + 1}"].partition_broadcast(P).rearrange("p a b -> p (a b)"))\
                .then_inc(s_w, 16)
        sp.wait_ge(s_self, 2)
        sp.dma_start(At, Aflat).then_inc(s_at, 16)
        sp.wait_ge(s_parts, 4 * BLOCKS)
        for c in range(BLOCKS):
            sp.dma_start(G[:, blk(c), :], x1v[:, blk(c), :]).then_inc(s_gx, 16)
        sp.wait_ge(s_g, 3 * BLOCKS + 1)
        for l, n in enumerate(("L2_gnn_W0", "L2_gnn_W1", "L2_gnn_W2")):
            sp.dma_start(wmat[:, l, :], t[n]).then_inc(s_w, 16)
        for l in range(2):
            sp.dma_start(bcol[:, l:l + 1], t[f"L2_gnn_b{l}"].rearrange("o p -> p o"),
                         allow_slow_non_contiguous=True).then_inc(s_w, 16)
        sp.dma_start(brow[:, 0, :], t["L2_gnn_b2"].partition_broadcast(P).rearrange("p a b -> p (a b)"))\
            .then_inc(s_w, 16)
        sp.wait_ge(s_at, 16)
        for l in range(2):
            def load(c, b):
                k = SLICES * l + c
                for g in range(BLOCKS):
                    sp.wait_ge(s_p, TILES * k + BT * (g + 1))
                    sp.wait_ge(s_ad[g], 16 * (k + 1))
                    sp.dma_start(Ab[b][:, g * BT:(g + 1) * BT, :],
                                 Ad[g * BT:(g + 1) * BT, :, ds(c * SW, SW)].rearrange("t p n -> p t n"))\
                        .then_inc(s_ad[g], 16)

            with sp.Fori(0, SLICES // 2) as i:
                c = i * 2
                load(c, 0)
                load(c + 1, 1)
        At_v = At.rearrange("p (t n) -> p t n", n=NPAD)
        sp.wait_ge(s_pv, TILES * (2 * SLICES + 1))
        sp.wait_ge(s_z, TILES * 2 * SLICES + SBANKS)
        sp.dma_start(A[:, 0:EARLY, :], At_v[:, 0:EARLY, :]).then_inc(s_back[0], 16)
        sp.wait_ge(s_x3, BLOCKS)
        for c in range(BLOCKS):
            sp.dma_start(x3v[:, blk(c), :], G[:, blk(c), :]).then_inc(s_x3d, 16)
        for l in range(2):
            sp.dma_start(wmat[:, l, :], t[f"L3_gnn_W{l + 1}"]).then_inc(s_w, 16)
            sp.dma_start(brow[:, l, :], t[f"L3_gnn_b{l + 1}"].partition_broadcast(P).rearrange("p a b -> p (a b)"))\
                .then_inc(s_w, 16)
        for e, (lo, hi) in enumerate(((EARLY, (EARLY + GONE) // 2), ((EARLY + GONE) // 2, GONE))):
            sp.dma_start(A[:, lo:hi, :], At_v[:, lo:hi, :]).then_inc(s_back[1 + e], 16)
        sp.wait_ge(s_parts, 6 * BLOCKS)
        sp.wait_ge(s_x3d, 16 * BLOCKS)
        for c in range(BLOCKS):
            sp.dma_start(G[:, blk(c), :], x3v[:, blk(c), :]).then_inc(s_gx, 16)
        out_v = t["out"][0:(TILES - 1) * P, :].rearrange("(t p) f -> p t f", p=P)
        for c in range(BLOCKS):
            e = min((c + 1) * BT, TILES - 1)
            sp.wait_ge(s_g, 4 * BLOCKS + c + 2)
            sp.dma_start(out_v[:, c * BT:e, :], G[:, c * BT:e, :]).then_inc(s_fin, 16)
        sp.dma_start(t["out"][(TILES - 1) * P:N, :], G[0:LAST, TILES - 1, :]).then_inc(s_fin, 16)
        sp.wait_ge(s_fin, 16 * (BLOCKS + 1))

    def zeros_of(lo, hi):
        return A32[:, lo * NPAD // 2:hi * NPAD // 2]

    @block.gpsimd
    def _(pool):
        pool.memset(G[:, TILES - 1, :], 0.0).then_inc(s_misc, 1)
        pool.iota(iota_i, [[1, KEYS]], base=0, channel_multiplier=0).then_inc(s_iota, 1)
        pool.memset(ident, 0.0).then_inc(s_ident, 1)
        pool.wait_ge(s_ident, 1)
        pool.affine_select(out=ident, in_=ident, compare_op=ALU.not_equal, fill=1.0, base=0,
                           pattern=[[-1, P]], channel_multiplier=1).then_inc(s_ident, 1)
        pool.memset(half_neg, -0.5).then_inc(s_ident, 1)
        pool.wait_ge(s_ident, 2)
        pool.tensor_copy(ident16, ident).then_inc(s_ident, 1)
        pool.sem_inc(s_ident, 1)
        pool.memset(zeros_of(DVE_ZEROS + ACT_ZEROS, TILES - PREP_TILES), 0.0).then_inc(s_zero, 1)
        pool.wait_ge(s_ident, 5)
        pool.wait_ge(s_eps, 16)
        pool.tensor_scalar(one_eps, one_eps, 1.0, 1.0 / LN_SCALE, ALU.add, ALU.mult).then_inc(s_misc, 1)

        def power(out, n):
            pool.tensor_tensor(out, out, half_neg[:, 0:n], ALU.pow)

        def norm_power(p):
            for c in range(BLOCKS):
                pool.wait_ge(s_ve, BLOCKS * p + c + 1)
                r = rstd[:, blk(c)]
                pool.tensor_tensor(r, r, half_neg[:, 0:BT], ALU.pow).then_inc(s_rs, 1)

        pool.wait_ge(s_ve, BLOCKS)
        pool.tensor_tensor(rstd, rstd, half_neg[:, 0:1].broadcast_to([P, TILES]), ALU.pow).then_inc(s_rs, BLOCKS)
        with pool.Fori(0, TILES) as g:
            pool.wait_ge(s_hve, g + 1)
            r = hrstd[:, ds(g % 2, 1)]
            pool.tensor_tensor(r, r, half_neg[:, 0:1], ALU.pow).then_inc(s_hrs, 1)
        pool.wait_ge(s_dg, 2)
        pool.tensor_tensor(dinv, dinv, half_neg[:, 0:1].broadcast_to([P, TILES]), ALU.pow).then_inc(s_dinv, 1)
        norm_power(1)
        norm_power(2)
        norm_power(3)

    @block.scalar
    def _(act):
        act.preload_act_table(ACT.Copy)
        act.wait_ge(s_ones, 2)
        for tt in range(DVE_ZEROS, DVE_ZEROS + ACT_ZEROS):
            last = act.activation(zeros_of(tt, tt + 1), zero.broadcast_to([P, NPAD // 2]), ACT.Copy)
        act.wait_ge(s_keyT, 1)
        for tt in range(TILES - PREP_TILES, TILES):
            last = act.activation(zeros_of(tt, tt + 1), zero.broadcast_to([P, NPAD // 2]), ACT.Copy)
        last.then_inc(s_zero, 1)
        act.wait_ge(s_sh, BLOCKS)
        for c in range(BLOCKS):
            for tt in range(c * BT, (c + 1) * BT):
                last = act.activation(G[:, tt, :], G[:, tt, :], ACT.Relu,
                                      bias=shift[:, tt:tt + 1], scale=rstd[:, tt:tt + 1])
            last.then_inc(s_h, 1)
        with act.Fori(0, CHUNKS // TURN) as i:
            for k in range(0, TURN, 2):
                b = k % BANKS
                act.wait_ge(s_out, i * TURN + TURN + k + 2)
                act.wait_ge(s_acc, i * TURN + TURN + k + 2 - BANKS)
                act.activation(counts[:, b:b + 2, :], psum[:, b:b + 2, 0:KEYS], ACT.Copy).then_inc(s_cnt, 1)

        def flat(v):
            return v.rearrange("p t f -> p (t f)")

        def split(p, nb, normal):
            for c in range(BLOCKS + 1):
                n = BLOCKS * p + c
                if c < BLOCKS:
                    if normal:
                        act.wait_ge(s_sh, BLOCKS * nb + c + 1)
                        if c >= 2:
                            act.wait_ge(s_r1, n - 1)
                            act.wait_ge(s_hi, n - 1)
                        for q in range(BT):
                            tt = c * BT + q
                            last = act.activation(work[:, c % 2, q * D:(q + 1) * D], G[:, tt, :], ACT.Relu,
                                                  bias=shift[:, tt:tt + 1], scale=rstd[:, tt:tt + 1])
                        last.then_inc(s_h, 1)
                        act.wait_ge(s_h, BLOCKS * nb + c + 1)
                        src = work[:, c % 2, :]
                    else:
                        if p:
                            act.wait_ge(s_g, BLOCKS * (p - 2) + c + 1 + 1)
                        src = flat(G[:, blk(c), :])
                    if c == 0 and p:
                        act.wait_ge(s_scale, p)
                    act.activation(flat(parts[:, 0, blk(c), :]), src, ACT.Copy,
                                   scale=scales[:, 0:1] if p else LN_SCALE).then_inc(s_hi, 1)
                if c:
                    act.wait_ge(s_r1, n)
                    act.activation(flat(parts[:, 1, blk(c - 1), :]), rest[:, (c - 1) % 2, :], ACT.Copy,
                                   scale=LOW_SCALE if p else 1.0).then_inc(s_parts, 1)

        act.wait_ge(s_acc, BUILT)
        act.wait_ge(s_h, BLOCKS)
        split(0, 0, False)
        act.wait_ge(s_w, 16 * 6)
        act.wait_ge(s_misc, 2)

        def gelu(m, q):
            act.wait_ge(s_hnT, m * BT + q + 1)
            act.wait_ge(s_o, m * BT + q + 1)
            for k in range(4):
                last = act.activation(gel[:, k, :], psum[:, 6, k * P:(k + 1) * P], ACT.Gelu,
                                      bias=beta[:, k:k + 1], scale=gamma[:, k:k + 1])
            last.then_inc(s_gel, 1)

        def l0_step(c, m):
            for tt in range(TILES):
                for n in pieces_at(tt):
                    q, st, k = piece(n)
                    act.wait_ge(s_tp, c * PN + n + 1)
                    act.wait_ge(s_td[n % STAGES], 16 * (c * (PN // STAGES) + n // STAGES) + 16)
                    act.activation(stage[:, n % STAGES, 0:k * P], psum[:, 2 + n % 2, 0:k * P], ACT.Copy,
                                   accum_out=deg_parts[:, ds(c * BT + q, 1), st // 4:st // 4 + 1]
                                   .rearrange("p a b -> p (a b)")).then_inc(s_ts, 1)
                step, q = mlp_at(tt)
                if m is not None and step == "transpose":
                    gelu(m, q)
                if tt == HT_AT:
                    act.wait_ge(s_hTp, c + 1)
                    act.wait_ge(s_aggT, 2 * c + 2)
                    act.activation(hT, pflat[:, 4 * 512:4 * 512 + BW], ACT.Copy, scale=one_eps).then_inc(s_hT, 1)

        l0_step(0, None)
        with act.Fori(1, BLOCKS) as c:
            l0_step(c, c - 1)
        for q in range(BT):
            gelu(BLOCKS - 1, q)

        for l in range(3):
            act.wait_ge(s_agg, 2 * BLOCKS * (l + 1))
            split(l + 1, 1, l == 0)

        def normed(nb, done):
            for c in range(BLOCKS):
                act.wait_ge(s_sh, BLOCKS * nb + c + 1)
                if c >= 2:
                    act.wait_ge(done, c - 1)
                for q in range(BT):
                    tt = c * BT + q
                    last = act.activation(work[:, c % 2, q * D:(q + 1) * D], G[:, tt, :], ACT.Relu,
                                          bias=shift[:, tt:tt + 1], scale=rstd[:, tt:tt + 1])
                last.then_inc(s_h, 1)
                if c:
                    xt(c - 1)
            xt(BLOCKS - 1)

        def xt(c):
            act.wait_ge(s_xT, c + 1)
            act.activation(XT[:, c * BW:(c + 1) * BW], pflat[:, (4 + 2 * (c % 2)) * 512:(4 + 2 * (c % 2)) * 512 + BW],
                           ACT.Copy).then_inc(s_xTs, 1)

        act.wait_ge(s_at, 16)
        act.wait_ge(s_agg, 2 * 4 * BLOCKS)
        act.wait_ge(s_w, 16 * 18)
        normed(2, s_xT)
        for l in range(2):
            for c in range(SLICES):
                k = SLICES * l + c
                act.wait_ge(s_hl, k + 1)
                act.activation(HT[:, c * SW:(c + 1) * SW], psum[:, c % 2, 0:SW], ACT.Relu,
                               bias=bcol[:, l:l + 1]).then_inc(s_hls, 1)

            def exps(c, b):
                k = SLICES * l + c
                act.wait_ge(s_nt, k + 1)
                for j in range(TILES):
                    act.activation(Z[b][:, j, :], Z[b][:, j, :], ACT.Exp, bias=neg_top[:, ds(c, 1)]).then_inc(s_e, 1)
                act.wait_ge(s_pv, TILES * (k + 3))
                act.activation(XT[:, ds(c * SW, SW)], psum[:, 5 + b, 0:SW], ACT.Copy).then_inc(s_ot, 2)

            with act.Fori(0, SLICES // 2) as i:
                c = i * 2
                exps(c, 0)
                exps(c + 1, 1)
            act.wait_ge(s_fs, 3 * l + 1)
            act.activation(wts, neg_top, ACT.Exp, bias=least, scale=-1.0).then_inc(s_wt, 1)
        act.wait_ge(s_x3, BLOCKS)
        for p in (4, 5):
            act.wait_ge(s_agg, 2 * BLOCKS * p)
            split(p, 3, p == 4)

    @block.tensor
    def _(pe):
        pe.wait_ge(s_ident, 5)
        pe.wait_ge(s_prep, PREPARED)
        for g in range(GROUPS):
            for b, v in enumerate((key, slo, dst_f, shi)):
                pe.transpose(psum[0:EC, b, g * GC:(g + 1) * GC], v[:, g, :], ident[0:GC, 0:GC])
            pe.transpose(psum[0:1, 4, g * GC:(g + 1) * GC], base[:, g:g + 1], ident[0:GC, 0:GC])
        pe.transpose(psum[0:1, 4, CHUNKS:CHUNKS + GC], span, ident[0:GC, 0:GC]).then_inc(s_keyT, 1)
        pe.wait_ge(s_keysb, 7)
        pe.sem_inc(s_out, TURN)
        with pe.Fori(0, CHUNKS // TURN) as i:
            for k in range(TURN):
                pe.wait_ge(s_hk, i * TURN + k + 1)
                if k % 2 == 0:
                    pe.wait_ge(s_cnt, i * (TURN // 2) + k // 2 + 1)
                pe.matmul(psum[:, k % BANKS, 0:KEYS], hot_slo[:, k % HOTS, :], hot_key[:, k % HOTS, :],
                          start=True, stop=True).then_inc(s_out, 1)
        pe.wait_ge(s_keysb, 7)
        _, flags = nc.values_load_multi_w_load_instructions(
            wide, engines=[mybir.EngineType.PE], min_val=0, max_val=1,
            skip_runtime_bounds_check_because="a comparison's result")
        with pe.If(flags[0]):
            with pe.Fori(0, ROUNDS) as r:
                def wide_products(n, first=False, last=False):
                    pe.wait_ge(s_whot, r * (CHUNKS // HOTS) + n + 1)
                    for k in range(HOTS):
                        done = pe.matmul(psum[:, 0, 0:KEYS], hot_slo[:, k, :], hot_key[:, k, :],
                                         start=(first and k == 0), stop=(last and k == HOTS - 1))
                    done.then_inc(s_wout, 1)

                pe.wait_ge(s_wadd, r + 1)
                wide_products(0, first=True)
                with pe.Fori(1, CHUNKS // HOTS - 1) as n:
                    wide_products(n)
                wide_products(CHUNKS // HOTS - 1, last=True)

        def aggregate(p, c, after=None):
            n = BLOCKS * p + c
            first, last_steps = range(ENDS), range(TILES - ENDS, TILES)
            for group in (first, *([tt] for tt in range(ENDS, TILES - ENDS)), last_steps):
                for tt in group:
                    if tt % BT == 0:
                        pe.wait_ge(s_parts, BLOCKS * p + tt // BT + 1)
                for h in range(2):
                    if group is first:
                        pe.wait_ge(s_aggT, 2 * n + 1 + h)
                    for tt in group:
                        for k in range(PARTS):
                            bank = h if p == 0 else 2 * k + h
                            start = tt == 0 and (k == 0 or p > 0)
                            stop = tt == TILES - 1 and (k == PARTS - 1 or p > 0)
                            last = pe.matmul(psum[:, bank, 0:HALF], parts[:, k, tt, :],
                                             A[:, tt, ds(c * BW + h * HALF, HALF)], start=start, stop=stop)
                    if group is last_steps:
                        last.then_inc(s_agg, 1)
                if after:
                    for tt in group:
                        after(tt)

        def mlp(m, step, q):
            g = m * BT + q
            if step == "hidden":
                pe.wait_ge(s_aggT, 2 * m + 4)
                if q >= 2:
                    pe.wait_ge(s_hb, g - 1)
                else:
                    pe.wait_ge(s_hT, m + 1)
                pe.matmul(psum[:, 4 + q % 2, :], aggT[:, q * P:(q + 1) * P], w1, start=True, stop=True)\
                    .then_inc(s_hp, 1)
            if step == "transpose":
                pe.wait_ge(s_hn, g + 1)
                pe.wait_ge(s_gel, g + 1)
                for k in range(4):
                    last = pe.transpose(psum[:, 6, k * P:(k + 1) * P], hid[:, q % 2, k * P:(k + 1) * P], ident)
                last.then_inc(s_hnT, 1)
            if step == "output":
                pe.wait_ge(s_gel, g + 2)
                pe.wait_ge(s_xn, g + 1)
                for k in range(4):
                    last = pe.matmul(psum[:, 7, 0:D], gel[:, k, :], w2[:, k, :], start=(k == 0), stop=(k == 3))
                last.then_inc(s_o, 1)

        def l0_step(c, m):
            def between(tt):
                for n in pieces_at(tt):
                    q, st, k = piece(n)
                    pe.wait_ge(s_ts, c * PN + n + (2 if n == 0 else 1))
                    for j in range(k):
                        last = pe.matmul(psum[:, 2 + n % 2, j * P:(j + 1) * P],
                                         A[:, st + j, ds((c * BT + q) * P, P)], ident16, start=True, stop=True)
                    last.then_inc(s_tp, 1)
                if m is not None:
                    mlp(m, *mlp_at(tt))
                if tt == HT_AT:
                    if m is not None:
                        pe.wait_ge(s_hb, (m + 1) * BT)
                    for q in range(BT):
                        for k in range(PARTS):
                            last = pe.matmul(pflat[:, 4 * 512 + q * P:4 * 512 + (q + 1) * P],
                                             parts[:, k, ds(c * BT + q, 1), :].rearrange("p a f -> p (a f)"), ident16,
                                             start=(k == 0), stop=(k == PARTS - 1))
                    last.then_inc(s_hTp, 1)

            aggregate(0, c, between)

        l0_step(0, None)
        pe.wait_ge(s_w, 16 * 6)
        with pe.Fori(1, BLOCKS) as c:
            l0_step(c, c - 1)
        for tt in range(TILES):
            mlp(BLOCKS - 1, *mlp_at(tt))

        passes = [0]

        def gcn(p, l, scaled):
            def weigh(c):
                pe.wait_ge(s_aggT, (BLOCKS * p + c) * 2 + 4)
                pe.wait_ge(s_u, BLOCKS * (p - 1) + c + 1)
                for q in range(BT):
                    last = pe.matmul(pflat[:, 4 * 512 + q * P:4 * 512 + (q + 1) * P], aggT[:, q * P:(q + 1) * P],
                                     wmat[:, l, :], start=True, stop=True)
                last.then_inc(s_y, 1)

            aggregate(p, 0)
            with pe.Fori(1, BLOCKS) as c:
                aggregate(p, c, lambda tt: weigh(c - 1) if tt == Y_AT else None)
            weigh(BLOCKS - 1)
            if l < scaled:
                m = passes[0]
                passes[0] += 1
                pe.wait_ge(s_st, SCALE_STEPS * m + 1)
                pe.transpose(psum[0:1, 7, 0:P], peak, ident).then_inc(s_sp, 1)
                pe.wait_ge(s_st, SCALE_STEPS * m + SCALE_STEPS)
                pe.matmul(psum[:, 7, 256:258], ones[0:1, :], top_bits, start=True, stop=True).then_inc(s_sp, 1)

        pe.wait_ge(s_w, 16 * 12)
        pe.wait_ge(s_self, 2)
        for l in range(3):
            gcn(l + 1, l, 2)

        pe.wait_ge(s_w, 16 * 18)
        pe.wait_ge(s_u, 3 * BLOCKS + 1)
        for c in range(BLOCKS):
            pe.wait_ge(s_h, 2 * BLOCKS + c + 1)
            if c >= 2:
                pe.wait_ge(s_xTs, c - 1)
            b = (4 + 2 * (c % 2)) * 512
            for q in range(BT):
                last = pe.transpose(pflat[:, b + q * P:b + (q + 1) * P], work[:, c % 2, q * D:(q + 1) * D], ident)
            last.then_inc(s_xT, 1)
        for l in range(2):
            if l:
                pe.wait_ge(s_sc, SLICES)
            else:
                pe.wait_ge(s_xTs, BLOCKS)
            for c in range(SLICES):
                k = SLICES * l + c
                if c >= 2:
                    pe.wait_ge(s_hls, k - 1)
                pe.matmul(psum[:, c % 2, 0:SW], wmat[:, l, :], XT[:, c * SW:(c + 1) * SW], start=True, stop=True)\
                    .then_inc(s_hl, 1)
            pe.wait_ge(s_hls, SLICES * (l + 1))
            for n in range(PIECES):
                m = PIECES * l + n
                if n >= 2:
                    pe.wait_ge(s_hts, m - 1)
                for tt in range(4 * n, min(4 * n + 4, TILES)):
                    last = pe.transpose(psum[:, 2 + n % 2, (tt - 4 * n) * P:(tt - 4 * n + 1) * P],
                                        HT[:, tt * P:(tt + 1) * P], ident)
                last.then_inc(s_ht, 1)
            pe.wait_ge(s_hts, PIECES * (l + 1))

            def scores(c, j):
                m = TILES * (SLICES * l + c) + j
                pe.wait_ge(s_z, m + 1)
                pe.matmul(psum[:, j % SBANKS, 0:SW], HT[:, j * P:(j + 1) * P], HT[:, ds(c * SW, SW)],
                          start=True, stop=True).then_inc(s_s, 1)

            def weighted(c, b, j):
                k = SLICES * l + c
                if j == 0:
                    pe.wait_ge(s_ot, k + 1)
                pe.wait_ge(s_p, TILES * (k + 2) + j + 1)
                pe.matmul(psum[:, 5 + b, 0:SW], H[:, j, :], Z[b][:, j, :], start=(j == 0), stop=(j == TILES - 1))\
                    .then_inc(s_pv, 1)

            def turn_peak(c):
                pe.wait_ge(s_rm, SLICES * l + c + 1)
                pe.transpose(psum[0:1, 7, 0:P], peak, ident).then_inc(s_rmT, 1)

            def spread_top(c):
                pe.wait_ge(s_top, SLICES * l + c + 1)
                pe.matmul(psum[:, 7, 256:257], ones[0:1, :], top, start=True, stop=True).then_inc(s_tb, 1)

            def step(c, b):
                for j in range(LEAD):
                    scores(c + 1, j)
                    if j == 1:
                        turn_peak(c)
                    if j == 3:
                        spread_top(c)
                for j in range(TILES):
                    weighted(c, b, j)
                    if j + LEAD < TILES:
                        scores(c + 1, j + LEAD)

            for j in range(TILES):
                scores(0, j)
            with pe.Fori(0, (SLICES - 2) // 2) as i:
                c = i * 2
                step(c, 0)
                step(c + 1, 1)
            step(SLICES - 2, 0)
            turn_peak(SLICES - 1)
            spread_top(SLICES - 1)
            for j in range(TILES):
                weighted(SLICES - 1, 1, j)
            pe.wait_ge(s_sum, SLICES * (l + 1))
            pe.matmul(psum[:, 7, 0:SLICES], ones, sums, start=True, stop=True).then_inc(s_ls, 1)
        pe.wait_ge(s_sc, 2 * SLICES)
        for c in range(BLOCKS):
            if c >= 2:
                pe.wait_ge(s_x3, c - 1)
            b = (0 + 2 * (c % 2)) * 512
            for q in range(BT):
                tt = c * BT + q
                last = pe.matmul(pflat[:, b + q * P:b + (q + 1) * P], XT[:, tt * P:(tt + 1) * P], wmat[:, 2, :],
                                 start=True, stop=True)
            last.then_inc(s_x3p, 1)
        pe.wait_ge(s_w, 16 * 22)
        pe.wait_ge(s_x3, BLOCKS)
        for r in s_back:
            pe.wait_ge(r, 16)
        for l in range(2):
            gcn(l + 4, l, 1)

    @block.vector
    def _(dve):
        prep = [0]

        def link(ins):
            prep[0] += 1
            ins.then_inc(s_prep, 1)
            dve.wait_ge(s_prep, prep[0])

        def flat(v):
            return v.rearrange("p t f -> p (t f)")

        def norm_block(nb, c, degree):
            n = BLOCKS * nb + c + 1
            for tt in range(c * BT, (c + 1) * BT):
                last = dve.bn_stats(stats[:, tt, :], G[:, tt, :])
            last.then_inc(s_bn, 1)
            dve.wait_ge(s_bn, n)
            for tt in range(c * BT, (c + 1) * BT):
                last = dve.bn_aggr(mean_var[:, tt, :], stats[:, tt, :])
            last.then_inc(s_mv, 1)
            dve.wait_ge(s_mv, n)
            dve.tensor_scalar(rstd[:, blk(c)], mean_var[:, blk(c), 1], LN_EPS, None, ALU.add)\
                .then_inc(s_ve, 1)
            dve.wait_ge(s_rs, n)
            if degree:
                link(dve.tensor_tensor(rstd[:, blk(c)], rstd[:, blk(c)], dinv[:, blk(c)], ALU.mult))
            dve.scalar_tensor_tensor(out=shift[:, blk(c)], in0=mean_var[:, blk(c), 0], scalar=-1.0,
                                     in1=rstd[:, blk(c)], op0=ALU.mult, op1=ALU.mult).then_inc(s_sh, 1)

        def norm_stats(nb, degree):
            for c in range(BLOCKS):
                norm_block(nb, c, degree)

        for s, v in ((s_aggT, 2), (s_ts, 2), (s_x1, 16), (s_o, 1), (s_y, 1), (s_u, 1), (s_g, 1), (s_gel, 1),
                     (s_ot, 2), (s_p, 2 * TILES), (s_z, SBANKS), (s_pv, 2 * TILES), (s_cnt, BANKS // 2),
                     (s_wadd, 1), (s_wout, 1), (s_xn, 1)):
            dve.sem_inc(s, v)
        for b in range(STAGES):
            dve.sem_inc(s_td[b], 16)
        for g in range(BLOCKS):
            dve.sem_inc(s_ad[g], 16)
        dve.memset(ones, 1.0).then_inc(s_ones, 1)
        dve.memset(zero, 0.0).then_inc(s_ones, 1)
        dve.memset(zeros_of(0, DVE_ZEROS), 0.0).then_inc(s_zero, 1)
        dve.wait_ge(s_edges, 32)
        link(dve.tensor_copy(dst_f, dst_i))
        link(dve.tensor_reduce(base, dst_f, AX.X, ALU.min))
        link(dve.tensor_copy(base_ii, base))
        link(dve.tensor_scalar(base_ii, base_ii, 0xFFFE, None, ALU.bitwise_and))
        link(dve.tensor_copy(base, base_ii))
        link(dve.tensor_tensor(rel, dst_f, base.unsqueeze(2).broadcast_to([GC, GROUPS, EC]), ALU.subtract))
        link(dve.tensor_reduce(span, rel, AX.XY, ALU.max))
        link(dve.tensor_scalar(part_i, src_i, 7, None, ALU.arith_shift_right))
        link(dve.tensor_copy(shi, part_i))
        link(dve.tensor_scalar(dst_i, src_i, P - 1, None, ALU.bitwise_and))
        link(dve.tensor_copy(slo, dst_i))
        link(dve.scalar_tensor_tensor(out=key, in0=shi, scalar=float(WIN), in1=rel, op0=ALU.mult, op1=ALU.add))
        link(dve.tensor_scalar(beyond, rel, float(WIN), FAR, ALU.is_ge, ALU.mult))
        link(dve.tensor_tensor(key, key, beyond, ALU.add))
        assert prep[0] == PREPARED
        dve.wait_ge(s_iota, 1)
        dve.tensor_copy(iota16, iota_i).then_inc(s_iota16, 1)
        dve.memset(keyT[:, CHUNKS:], -1.0).then_inc(s_keysb, 1)
        dve.memset(sloT[:, CHUNKS:], -1.0).then_inc(s_keysb, 1)
        for c in range(BLOCKS):
            dve.wait_ge(s_x, 16 * (BLOCKS + 1))
            for tt in range(c * BT, (c + 1) * BT):
                last = dve.bn_stats(stats[:, tt, :], G[:, tt, :])
            last.then_inc(s_bn, 1)
        dve.wait_ge(s_bn, BLOCKS)
        for tt in range(TILES):
            last = dve.bn_aggr(mean_var[:, tt, :], stats[:, tt, :])
        last.then_inc(s_mv, BLOCKS)
        dve.wait_ge(s_mv, BLOCKS)
        dve.tensor_scalar(rstd, mean_var[:, :, 1], LN_EPS, None, ALU.add).then_inc(s_ve, BLOCKS)
        dve.wait_ge(s_keyT, 1)
        dve.tensor_copy(keyT[:, 0:CHUNKS], psum[0:EC, 0, 0:CHUNKS]).then_inc(s_keysb, 1)
        dve.tensor_copy(sloT[:, 0:CHUNKS], psum[0:EC, 1, 0:CHUNKS]).then_inc(s_keysb, 1)
        dve.tensor_copy(dstT, psum[0:EC, 2, 0:CHUNKS]).then_inc(s_keysb, 1)
        dve.tensor_scalar(shiT, psum[0:EC, 3, 0:CHUNKS], float(WIN), None, ALU.mult).then_inc(s_keysb, 1)
        link(dve.tensor_reduce(widest, psum[0:1, 4, CHUNKS:CHUNKS + GC], AX.X, ALU.max))
        dve.tensor_copy(base_i, psum[0:1, 4, 0:CHUNKS]).then_inc(s_base, 1)
        dve.tensor_scalar(wide, widest, float(WIN), None, ALU.is_ge).then_inc(s_keysb, 1)
        dve.wait_ge(s_rs, BLOCKS)
        dve.scalar_tensor_tensor(out=shift, in0=mean_var[:, :, 0], scalar=-1.0, in1=rstd, op0=ALU.mult,
                                 op1=ALU.mult).then_inc(s_sh, BLOCKS)
        dve.wait_ge(s_keysb, 7)
        dve.wait_ge(s_base, 1)
        dve.wait_ge(s_iota16, 1)
        dve.wait_ge(s_zero, 3)
        dve.sem_inc(s_acc, TURN)

        def hots(b, chunk):
            dve.tensor_scalar(hot_key[:, b, :], iota16[0:EC, :], keyT[:, ds(chunk, 1)], None, ALU.is_equal)
            return dve.tensor_scalar(hot_slo[:, b, :], iota16[0:EC, 0:P], sloT[:, ds(chunk, 1)], None, ALU.is_equal)

        def hot(i, k):
            dve.wait_ge(s_out, i * TURN + TURN + k + 1 - HOTS)
            hots(k % HOTS, i * TURN + k).then_inc(s_hk, 1)

        for k in range(AHEAD):
            hot(0, k)
        with dve.Fori(0, CHUNKS // TURN) as i:
            _, lows = nc.values_load_multi_w_load_instructions(
                base_i[:, ds(i * TURN, TURN)], engines=[mybir.EngineType.DVE], min_val=0, max_val=N - 1,
                skip_runtime_bounds_check_because="a destination is a node: 0 to N - 1")

            def add(k, lo):
                dve.wait_ge(s_cnt, i * (TURN // 2) + k // 2 + 1 + BANKS // 2)
                dve.wait_ge(s_acc, i * TURN + TURN + k)
                win = A[:, :, ds(lo, WIN)]
                dve.tensor_tensor(win, win, counts[:, k % BANKS, :].rearrange("p (t w) -> p t w", w=WIN),
                                  ALU.add).then_inc(s_acc, 1)

            for k in range(TURN):
                hot(i, k + AHEAD)
                add(k, lows[k])
        dve.wait_ge(s_acc, BUILT - 1)
        dve.wait_ge(s_hk, CHUNKS + AHEAD)
        _, flags = nc.values_load_multi_w_load_instructions(
            wide, engines=[mybir.EngineType.DVE], min_val=0, max_val=1,
            skip_runtime_bounds_check_because="a comparison's result")
        with dve.If(flags[0]):
            with dve.Fori(0, ROUNDS) as r:
                wide_steps = [0]

                def wide_link(ins):
                    wide_steps[0] += 1
                    ins.then_inc(s_wkey, 1)
                    dve.wait_ge(s_wkey, r * WIDE_STEPS + wide_steps[0])

                dve.tensor_scalar(out_of[:, 0, :], dstT, float(WIN), FAR, ALU.is_ge, ALU.mult)
                dve.tensor_scalar(out_of[:, 1, :], dstT, 0.0, FAR, ALU.is_lt, ALU.mult)
                wide_link(dve.tensor_tensor(keyT[:, 0:CHUNKS], shiT, dstT, ALU.add))
                wide_link(dve.tensor_tensor(keyT[:, 0:CHUNKS], keyT[:, 0:CHUNKS], out_of[:, 0, :], ALU.add))
                dve.tensor_tensor(keyT[:, 0:CHUNKS], keyT[:, 0:CHUNKS], out_of[:, 1, :], ALU.add).then_inc(s_wkey, 1)
                dve.tensor_scalar(dstT, dstT, float(WIN), None, ALU.subtract).then_inc(s_wkey, 1)
                with dve.Fori(0, CHUNKS // HOTS) as n:
                    dve.wait_ge(s_wkey, r * WIDE_STEPS + WIDE_STEPS)
                    dve.wait_ge(s_wout, r * (CHUNKS // HOTS) + n + 1)
                    for k in range(HOTS):
                        last = hots(k, n * HOTS + k)
                    last.then_inc(s_whot, 1)
                dve.wait_ge(s_wout, r * (CHUNKS // HOTS) + CHUNKS // HOTS + 1)
                dve.tensor_copy(A[:, :, ds(r * WIN, WIN)], psum[:, 0, 0:KEYS].rearrange("p (t w) -> p t w", w=WIN))\
                    .then_inc(s_wadd, 1)
            dve.wait_ge(s_wadd, ROUNDS + 1)
        dve.sem_inc(s_acc, 1)

        def split(p, nb, normal, degree):
            for c in range(BLOCKS + 1):
                if c < BLOCKS and normal:
                    norm_block(nb, c, degree)
                if c:
                    n = BLOCKS * p + c
                    dve.wait_ge(s_hi, n)
                    if c >= 3:
                        dve.wait_ge(s_parts, n - 2)
                    if p and not normal:
                        dve.wait_ge(s_g, BLOCKS * (p - 2) + c + 1)
                    src = work[:, (c - 1) % 2, :] if normal else flat(G[:, blk(c - 1), :])
                    dve.scalar_tensor_tensor(out=rest[:, (c - 1) % 2, :], in0=src,
                                             scalar=scales[:, 0:1] if p else LN_SCALE,
                                             in1=flat(parts[:, 0, blk(c - 1), :]),
                                             op0=ALU.mult, op1=ALU.subtract).then_inc(s_r1, 1)

        split(0, 0, False, False)
        dve.wait_ge(s_w, 16 * 6)

        def aggregated(c):
            dve.wait_ge(s_hT, c + 1)
            for h in range(2):
                dve.wait_ge(s_agg, 2 * c + 1 + h)
                dve.scalar_tensor_tensor(out=aggT[:, h * HALF:(h + 1) * HALF], in0=psum[:, h, 0:HALF],
                                         scalar=1.0 / LN_SCALE, in1=hT[:, h * HALF:(h + 1) * HALF],
                                         op0=ALU.mult, op1=ALU.add).then_inc(s_aggT, 1)

        def mlp(m):
            for q in range(BT + 2):
                g = m * BT + q
                b = q % 2
                if q < BT:
                    if q >= 2:
                        dve.wait_ge(s_hnT, g - 1)
                    dve.wait_ge(s_hp, g + 1)
                    dve.tensor_tensor(hid[:, b, :], psum[:, 4 + b, :], b1row, ALU.add).then_inc(s_hb, 1)
                    dve.wait_ge(s_hb, g + 1)
                    dve.bn_stats(hstat, hid[:, b, :]).then_inc(s_hbn, 1)
                if 1 <= q <= BT:
                    dve.wait_ge(s_hrs, g)
                if q < BT:
                    dve.wait_ge(s_hbn, g + 1)
                if 1 <= q <= BT:
                    dve.tensor_scalar(hid[:, 1 - b, :], hid[:, 1 - b, :], hmv[:, 1 - b, 0:1],
                                      hrstd[:, ds((g - 1) % 2, 1)], ALU.subtract, ALU.mult).then_inc(s_hn, 1)
                elif q == 0:
                    dve.memset(scrap, 0.0)
                if q < BT:
                    dve.bn_aggr(hmv[:, b, :], hstat).then_inc(s_hmv, 1)
                    dve.wait_ge(s_hmv, g + 1)
                    dve.tensor_scalar(hrstd[:, ds(g % 2, 1)], hmv[:, b, 1:2], LN_EPS, None, ALU.add).then_inc(s_hve, 1)
                if q == 1:
                    dve.wait_ge(s_xb, 32 * (m + 1))
                    dve.tensor_tensor(xnew, xnew, brow[:, 0, :].unsqueeze(1).broadcast_to([P, BT, D]), ALU.add)\
                        .then_inc(s_xbb, 1)
                if q >= 2:
                    dve.wait_ge(s_o, g)
                    if q == 2:
                        dve.wait_ge(s_xbb, m + 1)
                    dve.tensor_tensor(xnew[:, q - 2, :], xnew[:, q - 2, :], psum[:, 7, 0:D], ALU.add)\
                        .then_inc(s_xn, 1)

        aggregated(0)
        with dve.Fori(1, BLOCKS) as c:
            mlp(c - 1)
            aggregated(c)
        mlp(BLOCKS - 1)

        dve.wait_ge(s_ts, BLOCKS * PN + 2)
        dve.tensor_reduce(dinv, deg_parts, AX.X, ALU.add).then_inc(s_dg, 1)
        dve.wait_ge(s_dg, 1)
        dve.tensor_scalar(dinv, dinv, 1.0, 1.0, ALU.add, ALU.max).then_inc(s_dg, 1)
        dve.wait_ge(s_agg, 2 * BLOCKS)
        dve.wait_ge(s_tp, BLOCKS * PN)
        W = NPAD + P
        dve_diag = Aflat[:, 0:(TILES - 1) * W].rearrange("p (t w) -> p t w", w=W)[:, :, 0:P]
        dve.tensor_tensor(dve_diag, dve_diag, ident16.unsqueeze(1).broadcast_to([P, TILES - 1, P]), ALU.add)\
            .then_inc(s_self, 1)
        lastd = A[:, TILES - 1, (TILES - 1) * P:]
        dve.tensor_tensor(lastd, lastd, ident16, ALU.add).then_inc(s_self, 1)

        passes = [0]
        low = rest[:, 0, :].rearrange("p (h n) -> p h n", h=2)

        def static_scale():
            dve.memset(scales[:, 0:1], LN_SCALE).then_inc(s_scale, 1)
            link(dve.tensor_scalar(dinv_out, dinv, 1.0 / LN_SCALE, None, ALU.mult))

        def gcn(p, l, final):
            with dve.Fori(0, BLOCKS) as c:
                n = BLOCKS * (p - 1) + c + 1
                dve.wait_ge(s_y, n)
                for h in range(2):
                    dve.wait_ge(s_agg, 2 * (BLOCKS * p + c) + 1 + h)
                    dve.tensor_scalar(low[:, h, :], psum[:, 2 + h, 0:HALF], 1.0 / LOW_SCALE, None, ALU.mult)\
                        .then_inc(s_low, 1)
                    dve.wait_ge(s_low, 2 * n + h - 1)
                    dve.tensor_tensor(aggT[:, h * HALF:(h + 1) * HALF], low[:, h, :], psum[:, h, 0:HALF],
                                      ALU.add).then_inc(s_aggT, 1)
                dve.wait_ge(s_y, n + 1)
                u = work[:, 0, :].rearrange("p (t f) -> p t f", t=BT)
                v = work[:, 1, :].rearrange("p (t f) -> p t f", t=BT)
                y = pflat[:, 4 * 512:4 * 512 + BW].rearrange("p (t f) -> p t f", t=BT)
                d = dinv[:, blk(c)].unsqueeze(2).broadcast_to([P, BT, D])
                dve.tensor_tensor(u, y, dinv_out[:, blk(c)].unsqueeze(2).broadcast_to([P, BT, D]), ALU.mult)\
                    .then_inc(s_u, 1)
                dve.wait_ge(s_u, n + 1)
                dve.tensor_tensor(v, u, brow[:, l, :].unsqueeze(1).broadcast_to([P, BT, D]), ALU.add)\
                    .then_inc(s_ub, 1)
                dve.wait_ge(s_ub, n)
                if final:
                    dve.tensor_tensor(G[:, blk(c), :], G[:, blk(c), :], v, ALU.add).then_inc(s_g, 1)
                else:
                    dve.scalar_tensor_tensor(out=G[:, blk(c), :], in0=v, scalar=0.0, in1=d, op0=ALU.max,
                                             op1=ALU.mult).then_inc(s_g, 1)
                    dve.wait_ge(s_g, n + 1)
                    dve.tensor_reduce(block_top[:, ds(c, 1)], G[:, blk(c), :], AX.XY, ALU.max).then_inc(s_bt, 1)
            if final:
                return
            m = passes[0]
            passes[0] += 1
            steps = [SCALE_STEPS * m]

            def scale_step(ins):
                steps[0] += 1
                ins.then_inc(s_st, 1)
                return steps[0]

            dve.wait_ge(s_bt, BLOCKS * (m + 1))
            scale_step(dve.tensor_reduce(peak, block_top, AX.X, ALU.max))
            dve.wait_ge(s_sp, 2 * m + 1)
            dve.wait_ge(s_st, scale_step(dve.tensor_reduce(top_bits[:, 0:1], psum[0:1, 7, 0:P], AX.X, ALU.max)))
            dve.wait_ge(s_st, scale_step(dve.tensor_scalar(top_bits[:, 0:1], top_bits[:, 0:1], LEAST_TOP, None,
                                                           ALU.max)))
            bits = top_bits.bitcast(I32)
            dve.wait_ge(s_st, scale_step(dve.tensor_scalar(bits[:, 1:2], bits[:, 0:1], EXPONENT, None,
                                                           ALU.bitwise_and)))
            scale_step(dve.tensor_scalar(bits[:, 0:1], bits[:, 1:2], -1.0, float((127 + 127 + TOP_POWER) << 23),
                                         ALU.mult, ALU.add))
            dve.wait_ge(s_sp, 2 * m + 2)
            dve.tensor_copy(scales[:, 0:1], psum[:, 7, 256:257]).then_inc(s_scale, 1)
            link(dve.tensor_scalar(scales[:, 1:2], psum[:, 7, 257:258], 2.0 ** -TOP_POWER, None, ALU.mult))
            link(dve.tensor_scalar(dinv_out, dinv, scales[:, 1:2], None, ALU.mult))

        dve.wait_ge(s_gx, 16 * BLOCKS)
        dve.wait_ge(s_dinv, 1)
        dve.wait_ge(s_w, 16 * 12)
        static_scale()
        for l in range(3):
            split(l + 1, 1, l == 0, True)
            if l == 2:
                dve.wait_ge(s_gx, 32 * BLOCKS)
            gcn(l + 1, l, l == 2)

        dve.wait_ge(s_g, 3 * BLOCKS + 1)
        norm_stats(2, False)
        dve.wait_ge(s_w, 16 * 18)
        dve.wait_ge(s_h, 3 * BLOCKS)
        dve.wait_ge(s_agg, 2 * 4 * BLOCKS)
        for c in range(BLOCKS):
            dve.tensor_tensor(G[:, blk(c), :], G[:, blk(c), :],
                              brow[:, 0, :].unsqueeze(1).broadcast_to([P, BT, D]), ALU.add).then_inc(s_xbb, 1)
        for l in range(2):
            for n in range(PIECES):
                dve.wait_ge(s_ht, PIECES * l + n + 1)
                w = min(4, TILES - 4 * n)
                dve.tensor_copy(flat(H[:, 4 * n:4 * n + w, :]), psum[:, 2 + n % 2, 0:w * P]).then_inc(s_hts, 1)

            def edges(c, b, j):
                k = SLICES * l + c
                dve.wait_ge(s_ad[j // BT], 16 * (k + 2))
                h = j // SBANKS % 2
                dve.tensor_scalar(mask[:, SBANKS * h:SBANKS * (h + 1), :], Ab[b][:, j:j + SBANKS, :], 1.0, None,
                                  ALU.min).then_inc(s_mask, 1)

            def masked_waits(c, j):
                m = TILES * (SLICES * l + c) + j
                dve.wait_ge(s_s, m + 1)
                dve.wait_ge(s_pv, m + 1)
                if j % SBANKS == 0:
                    dve.wait_ge(s_mask, BLOCKS * (SLICES * l + c) + j // SBANKS + 1)

            def masked(b, j):
                dve.tensor_tensor_reduce(Z[b][:, j, :], mask[:, j % (2 * SBANKS), :], psum[:, j % SBANKS, 0:SW], 1.0,
                                         0.0, ALU.mult, ALU.max, rowmax[:, j:j + 1]).then_inc(s_z, 1)

            def weights(c, b, j):
                k = SLICES * l + c
                dve.wait_ge(s_e, TILES * k + j + 1)
                dve.tensor_tensor_reduce(Z[b][:, j, :], Z[b][:, j, :], Ab[b][:, j, :], 1.0, 0.0,
                                         ALU.mult, ALU.add, rowsum[:, b, j:j + 1]).then_inc(s_p, 1)

            def slice_sum(c, b):
                dve.wait_ge(s_p, TILES * (SLICES * l + c + 3))
                dve.tensor_reduce(sums[:, ds(c, 1)], rowsum[:, b, :], AX.X, ALU.add).then_inc(s_sum, 1)

            def slice_peak(c):
                dve.wait_ge(s_z, TILES * (SLICES * l + c + 1) + SBANKS)
                dve.tensor_reduce(peak, rowmax, AX.X, ALU.max).then_inc(s_rm, 1)

            def slice_top(c):
                dve.wait_ge(s_rmT, SLICES * l + c + 1)
                dve.tensor_reduce(top, psum[0:1, 7, 0:P], AX.X, ALU.max).then_inc(s_top, 1)

            def slice_neg(c):
                dve.wait_ge(s_tb, SLICES * l + c + 1)
                dve.tensor_scalar(neg_top[:, ds(c, 1)], psum[:, 7, 256:257], -1.0, None, ALU.mult).then_inc(s_nt, 1)

            def step(c, b):
                slice_peak(c)
                edges(c + 1, 1 - b, 0)
                masked_waits(c + 1, 0)
                slice_top(c)
                masked(1 - b, 0)
                masked_waits(c + 1, 1)
                slice_neg(c)
                masked(1 - b, 1)
                for j in range(TILES):
                    n = j + 2
                    if n < TILES:
                        if n % SBANKS == 0:
                            edges(c + 1, 1 - b, n)
                        masked_waits(c + 1, n)
                    weights(c, b, j)
                    if n < TILES:
                        masked(1 - b, n)
                slice_sum(c, b)

            for j in range(TILES):
                if j % SBANKS == 0:
                    edges(0, 0, j)
                masked_waits(0, j)
                masked(0, j)
            with dve.Fori(0, (SLICES - 2) // 2) as i:
                c = i * 2
                step(c, 0)
                step(c + 1, 1)
            step(SLICES - 2, 0)
            slice_peak(SLICES - 1)
            slice_top(SLICES - 1)
            slice_neg(SLICES - 1)
            for j in range(TILES):
                weights(SLICES - 1, 1, j)
            slice_sum(SLICES - 1, 1)
            dve.wait_ge(s_nt, SLICES * (l + 1))
            dve.tensor_reduce(least, neg_top, AX.X, ALU.min).then_inc(s_fs, 1)
            dve.wait_ge(s_ls, l + 1)
            dve.wait_ge(s_wt, l + 1)
            dve.tensor_tensor_reduce(scale8, wts, psum[:, 7, 0:SLICES], 1.0, 0.0, ALU.mult, ALU.add,
                                     total[:, 0:1]).then_inc(s_fs, 1)
            dve.wait_ge(s_fs, 3 * l + 2)
            dve.reciprocal(total[:, 1:2], total[:, 0:1]).then_inc(s_fs, 1)
            dve.wait_ge(s_fs, 3 * l + 3)
            link(dve.tensor_scalar(scale8, wts, total[:, 1:2], None, ALU.mult))
            dve.wait_ge(s_ot, SLICES * (l + 1) + 2)
            for c in range(SLICES):
                v = XT[:, c * SW:(c + 1) * SW]
                dve.tensor_scalar(v, v, scale8[:, c:c + 1], None, ALU.mult).then_inc(s_sc, 1)
        dve.wait_ge(s_xbb, 2 * BLOCKS)
        for c in range(BLOCKS):
            dve.wait_ge(s_x3p, c + 1)
            b = (0 + 2 * (c % 2)) * 512
            g = flat(G[:, blk(c), :])
            dve.tensor_tensor(g, g, pflat[:, b:b + BW], ALU.add).then_inc(s_x3, 1)

        dve.wait_ge(s_x3, BLOCKS)
        dve.wait_ge(s_w, 16 * 22)
        static_scale()
        for l in range(2):
            split(l + 4, 3, l == 0, True)
            dve.wait_ge(s_x3d, 16 * BLOCKS)
            if l:
                dve.wait_ge(s_gx, 48 * BLOCKS)
            gcn(l + 4, l, l == 1)


_INS = ["x", "src", "dst", "L0_gnn_eps", "L0_gnn_W1", "L0_gnn_b1", "L0_gnn_ln_g", "L0_gnn_ln_b", "L0_gnn_W2",
        "L0_gnn_b2", "L1_gnn_W1", "L1_gnn_b1", "L1_gnn_W2", "L1_gnn_b2", "L1_gnn_W3", "L1_gnn_b3",
        "L2_gnn_W0", "L2_gnn_b0", "L2_gnn_W1", "L2_gnn_b1", "L2_gnn_W2", "L2_gnn_b2",
        "L3_gnn_W1", "L3_gnn_b1", "L3_gnn_W2", "L3_gnn_b2"]


def kernel(**inputs):
    import numpy as _np
    import concourse.bacc as _bacc
    from concourse import mybir as _mybir
    from concourse.bass_utils import run_bass_kernel_spmd as _run

    nc = _bacc.Bacc("TRN2", target_bir_lowering=False, num_devices=1)
    arrays, t = {}, {}
    for name in _INS:
        a = _np.ascontiguousarray(inputs[name])
        if a.ndim < 2:
            a = a.reshape(1, -1)
        if a.ndim == 3:
            a = a.reshape(a.shape[1:])
        arrays["in_" + name] = a
        t[name] = nc.dram_tensor("in_" + name, a.shape, _mybir.dt.from_np(a.dtype), kind="ExternalInput").ap()
    t["out"] = nc.dram_tensor("out", (N, D), F32, kind="ExternalOutput").ap()
    gnn_kernel(nc, t)
    r = _run(nc, [arrays], core_ids=[0])
    return r.results[0]["out"]
```

```python
from contextlib import ExitStack

import concourse.bass as bass
from concourse import mybir

F32 = mybir.dt.float32
FP16 = mybir.dt.float16
I32 = mybir.dt.int32
ALU = mybir.AluOpType
ACT = mybir.ActivationFunctionType
AX = mybir.AxisListType
ds = bass.ds

P = 128
D = 128
N = 3125
TILES = -(-N // P)
NPAD = TILES * P
LAST = N - (TILES - 1) * P
HID = 4 * D
LN_EPS = 1e-5

E_EDGES = 50000
EC = 125
CHUNKS = E_EDGES // EC
GROUPS = 4
GC = CHUNKS // GROUPS
WIN = 20
KEYS = TILES * WIN
ROUNDS = -(-N // WIN)
FAR = 10000.0
TURN = 40
LOADED = 20
BANKS = 8
HT_AT = TILES - 5
GROUP = 4
HOTS = 8
PREP_TILES = 3
DVE_ZEROS = 2
ACT_ZEROS = 11

PREPARED = 14
WIDE_STEPS = 4
AHEAD = 4

BLOCKS = 5
BT = TILES // BLOCKS
BW = BT * P
HALF = BW // 2
PIECES = -(-TILES // 4)
STAGES = 5

SLICES = 8
SW = NPAD // SLICES
TURN_EVERY = 3
LEAD = 7
SBANKS = 5

PARTS = 2
LN_SCALE = 4096.0
LOW_SCALE = 2048.0
TOP_POWER = 14
LEAST_TOP = 2.0 ** -60
EXPONENT = 0x7F800000
SCALE_STEPS = 5
ENDS = 4
Y_AT = 6


def gnn_kernel(nc, t):
    with ExitStack() as ctx:
        build(nc, t, ctx)


def build(nc, t, ctx):
    def sem(name):
        return ctx.enter_context(nc.semaphore(name))

    A = ctx.enter_context(nc.sbuf_tensor("adjacency", [P, TILES, NPAD], FP16))
    ARENA = (212800 - TILES * NPAD * 2) // 4
    arena = ctx.enter_context(nc.sbuf_tensor("arena", [P, ARENA], F32))
    at = [0]

    def take(cols, dt=F32, start=None):
        a = at[0] if start is None else start
        width = cols if dt in (F32, I32) else -(-cols // 2)
        at[0] = a + width
        assert at[0] <= ARENA, (at[0], ARENA)
        v = arena[:, a:a + width]
        return v if dt == F32 else v.bitcast(dt)

    ident = take(P)
    ident16 = take(P, FP16)
    ones = take(P)
    one_eps = take(2)[:, 0:1]
    dinv = take(TILES + 1)[:, 0:TILES]
    deg_parts = take(TILES * PIECES + 1)[:, 0:TILES * PIECES].rearrange("p (t k) -> p t k", t=TILES)
    half_neg = take(8)
    hstat = take(6)
    scrap = take(2)
    zero = take(2)[:, 0:1]
    scales = take(2)
    top_bits = take(2)[0:1, :]
    block_top = take(BLOCKS + 1)[:, 0:BLOCKS]
    dinv_out = take(TILES + 1)[:, 0:TILES]
    wide = take(2, I32)[0:1, 0:1]
    peak = take(2)[:, 0:1]
    top = take(2)[0:1, 0:1]
    neg_top = take(SLICES)
    least = take(2)[:, 0:1]
    wts = take(SLICES)
    sums = take(SLICES)
    total = take(2)
    scale8 = take(SLICES)
    bcol = take(2)
    hmv = take(4).rearrange("p (b s) -> p b s", b=2)
    hrstd = take(2)
    mean_var = take(TILES * 2)[:, :].rearrange("p (t s) -> p t s", t=TILES)
    rstd = take(TILES + 1)[:, 0:TILES]
    shift = take(TILES + 1)[:, 0:TILES]
    block_stats = take(BT * 6).rearrange("p (t s) -> p t s", t=BT)
    block_mv = take(BT * 2).rearrange("p (t s) -> p t s", t=BT)
    gamma = take(4)
    beta = take(4)
    brow = take(3 * D).rearrange("p (l f) -> p l f", l=3)
    wmat = take(3 * D).rearrange("p (l f) -> p l f", l=3)
    b1row = arena[:, at[0] - 5 * D:at[0] - 5 * D + HID]
    BUILD_AT = at[0]
    aggT = take(BW)
    work = take(2 * BW).rearrange("p (b n) -> p b n", b=2)
    rest = take(2 * BW).rearrange("p (b n) -> p b n", b=2)
    PARTS_AT = at[0]
    parts = take(PARTS * TILES * D, FP16).rearrange("p (k t f) -> p k t f", k=PARTS, t=TILES)
    OVER = at[0]
    w1 = take(HID)
    w2 = take(HID).rearrange("p (k f) -> p k f", k=4)
    gel = take(HID).rearrange("p (k f) -> p k f", k=4)
    G = take(TILES * D).rearrange("p (t f) -> p t f", t=TILES)
    AFTER_G = at[0]
    at[0] -= BW
    STAGE_W = 512
    stage = [take(STAGE_W, FP16) for _ in range(STAGES - 1)]
    stage.append(arena[:, PARTS_AT - STAGE_W // 2:PARTS_AT].bitcast(FP16))
    assert 2 * HID + STAGE_W // 2 <= 2 * BW
    hT = work[:, 0, :]
    xnew = work[:, 1, :].rearrange("p (t f) -> p t f", t=BT)
    hid = rest.rearrange("p b n -> p (b n)")[:, 0:2 * HID].rearrange("p (b n) -> p b n", b=2)

    A32 = A[:, :, :].rearrange("p t n -> p (t n)").bitcast(F32)
    cut = [0]

    def carve(cols):
        cut[0] += cols
        return A32[:, cut[0] - cols:cut[0]]

    Z = [carve(TILES * SW).rearrange("p (t n) -> p t n", t=TILES)]
    Ab = [carve(TILES * SW // 2).bitcast(FP16).rearrange("p (t n) -> p t n", t=TILES)]
    mask = carve(SBANKS * SW).bitcast(FP16).rearrange("p (b n) -> p b n", b=2 * SBANKS)
    EARLY = cut[0] * 2 // NPAD
    Z.append(carve(TILES * SW).rearrange("p (t n) -> p t n", t=TILES))
    Ab.append(carve(TILES * SW // 2).bitcast(FP16).rearrange("p (t n) -> p t n", t=TILES))
    NEXT = cut[0] * 2 // NPAD
    XT = carve(NPAD)
    rowmax = carve(TILES + 1)[:, 0:TILES]
    rowsum = carve(2 * TILES).rearrange("p (c t) -> p c t", c=2)
    GONE = -(-cut[0] * 2 // NPAD)
    HT = arena[:, BUILD_AT:BUILD_AT + NPAD]
    H = parts.rearrange("p k t f -> p (k t f)").bitcast(F32)[:, 0:NPAD].rearrange("p (t f) -> p t f", t=TILES)

    psum = ctx.enter_context(nc.psum_tensor("psum", [P, 8, 512], F32))
    pflat = psum[:, :, :].rearrange("p b n -> p (b n)")

    Ad = nc.dram_tensor("adjacency_by_dst", (TILES, P, NPAD), FP16, kind="Internal").ap()
    At = nc.dram_tensor("adjacency_by_src", (P, TILES * NPAD), FP16, kind="Internal").ap()
    x3 = nc.dram_tensor("x_after_l2", (NPAD, D), F32, kind="Internal").ap()
    x3v = x3.rearrange("(t p) f -> p t f", p=P)
    x1 = nc.dram_tensor("x_after_l0", (NPAD, D), F32, kind="Internal").ap()
    x1v = x1.rearrange("(t p) f -> p t f", p=P)
    xin_v = t["x"][0:(TILES - 1) * P, :].rearrange("(t p) f -> p t f", p=P)
    Aflat = A[:, :, :].rearrange("p t n -> p (t n)")

    at[0] = BUILD_AT
    keyT = take(CHUNKS + AHEAD + 1)[0:EC]
    sloT = take(CHUNKS + HOTS, FP16)[0:EC]
    dstT = take(CHUNKS)[0:EC]
    shiT = take(CHUNKS)[0:EC]
    base_i = take(CHUNKS, I32)[0:1]
    widest = take(2)[0:1, 0:1]
    iota16 = take(KEYS, FP16)
    hot_key = take(HOTS * KEYS, FP16)[0:EC].rearrange("p (b n) -> p b n", b=HOTS)
    counts = take(BANKS * KEYS, FP16).rearrange("p (b n) -> p b n", b=BANKS)
    iota_each_i = counts[0:EC, 2:5, :].rearrange("p b n -> p (b n)").bitcast(I32)[:, 0:GROUP * P]
    iota_i = counts[:, 0:2, :].rearrange("p b n -> p (b n)").bitcast(I32)
    assert at[0] <= OVER
    at[0] = OVER
    stats = take(TILES * 6).rearrange("p (t s) -> p t s", t=TILES)
    out_of = take(2 * CHUNKS)[0:EC].rearrange("p (s k) -> p s k", s=2)
    hot_slo = take(HOTS * P, FP16)[0:EC].rearrange("p (g n c) -> p g n c", g=HOTS // GROUP, c=GROUP)
    at[0] = AFTER_G
    iota_each = take(GROUP * P, FP16)[0:EC].rearrange("p (n c) -> p n c", c=GROUP)

    prep_at = [(TILES - PREP_TILES) * NPAD // 2]

    def edge_array(cols=GROUPS * EC, dt=F32):
        v = A32[0:GC, prep_at[0]:prep_at[0] + cols]
        prep_at[0] += cols
        assert prep_at[0] <= TILES * NPAD // 2
        if cols == GROUPS * EC:
            v = v.rearrange("p (g j) -> p g j", g=GROUPS)
        return v if dt == F32 else v.bitcast(dt)

    dst_i, src_i, part_i = edge_array(dt=I32), edge_array(dt=I32), edge_array(dt=I32)
    dst_f, rel, shi, slo = edge_array(), edge_array(), edge_array(), edge_array()
    key, beyond = edge_array(), edge_array()
    base, base_ii = edge_array(GROUPS), edge_array(GROUPS, I32)
    span = edge_array(2)[:, 0:1]

    s_edges = sem("edges_loaded")
    s_ones = sem("ones_made")
    s_iota = sem("iota_made")
    s_iota16 = sem("iota16_made")
    s_ident = sem("ident_made")
    s_zero = sem("a_zeroed")
    s_prep = sem("dve_prep")
    s_keyT = sem("keys_transposed")
    s_keysb = sem("keys_in_sbuf")
    s_hk = sem("hot_pair_ready")
    s_out = sem("chunk_product_ready")
    s_cnt = sem("chunk_pair_counts_ready")
    s_wkey = sem("wide_round_key_steps")
    s_whot = sem("wide_hots_ready")
    s_wout = sem("wide_products_ready")
    s_wadd = sem("wide_window_ready")
    s_acc = sem("chunk_added")
    s_base = sem("bases_in_sbuf")

    BUILT = TURN + CHUNKS + 1

    s_x = sem("x_loaded")
    s_w = sem("layer_weights_loaded")
    s_eps = sem("eps_loaded")
    s_misc = sem("small_constants_ready")
    s_bn = sem("tile_stats_ready")
    s_mv = sem("mean_var_ready")
    s_ve = sem("variance_plus_eps_ready")
    s_rs = sem("rstd_ready")
    s_sh = sem("shift_ready")
    s_h = sem("h_block_ready")
    s_hi = sem("hi_part_ready")
    s_r1 = sem("rest_ready")
    s_scale = sem("pass_scale_ready")
    s_st = sem("pass_scale_steps")
    s_low = sem("low_half_scaled")
    s_bt = sem("block_top_ready")
    s_sp = sem("pass_scale_products")
    s_parts = sem("block_parts_ready")
    s_agg = sem("agg_block_ready")
    s_aggT = sem("agg_half_in_sbuf")
    s_hTp = sem("h_transposed")
    s_hT = sem("scaled_h_in_sbuf")
    s_y = sem("weight_product_ready")
    s_u = sem("scaled_product_ready")
    s_ub = sem("biased_product_ready")
    s_g = sem("block_output_ready")
    s_hp = sem("hidden_product_ready")
    s_hb = sem("hidden_biased")
    s_hbn = sem("hidden_stats_ready")
    s_hmv = sem("hidden_mean_var_ready")
    s_hve = sem("hidden_variance_plus_eps_ready")
    s_hrs = sem("hidden_rstd_ready")
    s_hn = sem("hidden_normalised")
    s_hnT = sem("hidden_transposed")
    s_gel = sem("gelu_ready")
    s_o = sem("mlp_product_ready")
    s_xb = sem("x_block_loaded")
    s_xbb = sem("x_block_biased")
    s_xn = sem("x_tile_updated")
    s_x1 = sem("x1_block_stored")
    s_tp = sem("adjacency_piece_transposed")
    s_ts = sem("adjacency_piece_staged")
    s_td = [sem(f"adjacency_stage{b}_stored") for b in range(STAGES)]
    s_dg = sem("degree_steps")
    s_dinv = sem("dinv_ready")
    s_self = sem("self_loops_added")
    s_at = sem("adjacency_saved")
    s_fin = sem("output_stored")
    s_gx = sem("x_reloaded")

    s_xT = sem("x_transposed")
    s_xTs = sem("xT_in_sbuf")
    s_hl = sem("attention_h_product")
    s_hls = sem("attention_hT_even_slice_ready")
    s_hlv = sem("attention_hT_odd_slice_ready")
    s_ht = sem("attention_h_transposed")
    s_hts = sem("attention_h_ready")
    s_ad = [sem(f"adjacency_slice_group{g}_loaded") for g in range(BLOCKS)]
    s_mask = sem("mask_ready")
    s_s = sem("scores_ready")
    s_z = sem("masked_scores_ready")
    s_rm = sem("row_peak_ready")
    s_rmT = sem("row_peak_transposed")
    s_top = sem("slice_top_ready")
    s_tb = sem("slice_top_broadcast")
    s_nt = sem("slice_neg_top_ready")
    s_e = sem("exp_ready")
    s_sum = sem("slice_row_sums_ready")
    s_p = sem("edge_weights_ready")
    s_pv = sem("weighted_sum_step")
    s_ot = sem("slice_sum_in_sbuf")
    s_fs = sem("softmax_total_steps")
    s_wt = sem("slice_weights_ready")
    s_ls = sem("slice_sums_ready")
    s_sc = sem("slices_scaled")
    s_x3p = sem("attention_output_product")
    s_x3 = sem("x3_ready")
    s_x3d = sem("x3_saved")
    s_back = [sem(f"adjacency_{w}_reloaded") for w in ("first_tiles", "next_tiles", "last_tiles")]

    def dst_view(a):
        return a.rearrange("o (g c j) -> c (o g) j", g=GROUPS, c=GC)

    block = ctx.enter_context(nc.Block())



    def blk(c):
        return ds(c * BT, BT)

    PN = BT * PIECES

    def piece(n):
        q, k = divmod(n, PIECES)
        return q, 4 * k, min(4, TILES - 4 * k)

    def pieces_at(tt):
        steps = TILES - ENDS
        return range(PN * min(tt, steps) // steps, PN * min(tt + 1, steps) // steps)

    def mlp_at(tt):
        q, r = divmod(tt, 3)
        step, q = (("hidden", q), ("output", q - 2), ("transpose", q - 1))[r]
        return (step if 0 <= q < BT else None), q

    @block.sync
    def _(sp):
        sp.dma_start(dst_i, dst_view(t["dst"])).then_inc(s_edges, 16)
        sp.dma_start(src_i, dst_view(t["src"])).then_inc(s_edges, 16)
        for c in range(BLOCKS):
            e = min((c + 1) * BT, TILES - 1)
            sp.dma_start(G[:, c * BT:e, :], xin_v[:, c * BT:e, :]).then_inc(s_x, 16)
        sp.wait_ge(s_misc, 1)
        sp.dma_start(G[0:LAST, TILES - 1, :], t["x"][(TILES - 1) * P:N, :]).then_inc(s_x, 16)
        sp.dma_start(one_eps, t["L0_gnn_eps"].partition_broadcast(P).rearrange("p a b -> p (a b)")).then_inc(s_eps, 16)
        sp.wait_ge(s_acc, BUILT)
        sp.dma_start(w1, t["L0_gnn_W1"]).then_inc(s_w, 16)
        sp.dma_start(w2, t["L0_gnn_W2"].rearrange("(k p) f -> p k f", p=P)).then_inc(s_w, 16)
        sp.dma_start(b1row, t["L0_gnn_b1"].partition_broadcast(P).rearrange("p a b -> p (a b)")).then_inc(s_w, 16)
        sp.dma_start(gamma, t["L0_gnn_ln_g"].rearrange("o (k p) -> p (o k)", p=P),
                     allow_slow_non_contiguous=True).then_inc(s_w, 16)
        sp.dma_start(beta, t["L0_gnn_ln_b"].rearrange("o (k p) -> p (o k)", p=P),
                     allow_slow_non_contiguous=True).then_inc(s_w, 16)
        sp.dma_start(brow[:, 0, :], t["L0_gnn_b2"].partition_broadcast(P).rearrange("p a b -> p (a b)")).then_inc(s_w, 16)

        def pieces_out(c):
            for n in range(PN):
                q, st, k = piece(n)
                sp.wait_ge(s_ts, c * PN + n + 1 + 2)
                sp.dma_start(Ad[ds(c * BT + q, 1), :, st * P:(st + k) * P].rearrange("o p n -> (o p) n"),
                             stage[n % STAGES][:, 0:k * P]).then_inc(s_td[n % STAGES], 16)

        def x1_out(m):
            sp.wait_ge(s_xn, (m + 1) * BT + 1)
            sp.dma_start(x1v[:, blk(m), :], G[:, blk(m), :]).then_inc(s_x1, 16)

        pieces_out(0)
        with sp.Fori(1, BLOCKS) as c:
            sp.wait_ge(s_xn, (c - 1) * BT + 1)
            sp.dma_start(xnew[:, :, :], xin_v[:, ds((c - 1) * BT, BT), :]).then_inc(s_xb, 32)
            pieces_out(c)
            x1_out(c - 1)
        sp.wait_ge(s_xn, (BLOCKS - 1) * BT + 1)
        sp.dma_start(xnew[:, 0:BT - 1, :], xin_v[:, (BLOCKS - 1) * BT:, :]).then_inc(s_xb, 16)
        sp.dma_start(xnew[0:LAST, BT - 1, :], t["x"][(TILES - 1) * P:N, :]).then_inc(s_xb, 16)
        x1_out(BLOCKS - 1)
        sp.wait_ge(s_hb, TILES)
        sp.wait_ge(s_xbb, BLOCKS)
        for l in range(3):
            sp.dma_start(wmat[:, l, :], t[f"L1_gnn_W{l + 1}"]).then_inc(s_w, 16)
            sp.dma_start(brow[:, l, :], t[f"L1_gnn_b{l + 1}"].partition_broadcast(P).rearrange("p a b -> p (a b)"))\
                .then_inc(s_w, 16)
        sp.wait_ge(s_self, 2)
        sp.dma_start(At, Aflat).then_inc(s_at, 16)
        sp.wait_ge(s_parts, 4 * BLOCKS)
        sp.wait_ge(s_x1, 16 * BLOCKS + 16)
        for c in range(BLOCKS):
            sp.dma_start(G[:, blk(c), :], x1v[:, blk(c), :]).then_inc(s_gx, 16)
        sp.wait_ge(s_g, 3 * BLOCKS + 1)
        for l, n in enumerate(("L2_gnn_W0", "L2_gnn_W1", "L2_gnn_W2")):
            sp.dma_start(wmat[:, l, :], t[n]).then_inc(s_w, 16)
        for l in range(2):
            sp.dma_start(bcol[:, l:l + 1], t[f"L2_gnn_b{l}"].rearrange("o p -> p o"),
                         allow_slow_non_contiguous=True).then_inc(s_w, 16)
        sp.dma_start(brow[:, 0, :], t["L2_gnn_b2"].partition_broadcast(P).rearrange("p a b -> p (a b)"))\
            .then_inc(s_w, 16)
        sp.wait_ge(s_at, 16)
        for l in range(2):
            def load(c, b):
                k = SLICES * l + c
                for g in range(BLOCKS):
                    sp.wait_ge(s_p, TILES * k + BT * (g + 1))
                    sp.wait_ge(s_ad[g], 16 * (k + 1))
                    sp.dma_start(Ab[b][:, g * BT:(g + 1) * BT, :],
                                 Ad[g * BT:(g + 1) * BT, :, ds(c * SW, SW)].rearrange("t p n -> p t n"))\
                        .then_inc(s_ad[g], 16)

            with sp.Fori(0, SLICES // 2) as i:
                c = i * 2
                load(c, 0)
                load(c + 1, 1)
        At_v = At.rearrange("p (t n) -> p t n", n=NPAD)
        sp.wait_ge(s_hls, SLICES)
        sp.wait_ge(s_hlv, SLICES)
        sp.wait_ge(s_xbb, 2 * BLOCKS)
        for l in range(2):
            sp.dma_start(wmat[:, l, :], t[f"L3_gnn_W{l + 1}"]).then_inc(s_w, 16)
            sp.dma_start(brow[:, l, :], t[f"L3_gnn_b{l + 1}"].partition_broadcast(P).rearrange("p a b -> p (a b)"))\
                .then_inc(s_w, 16)
        sp.wait_ge(s_pv, TILES * (2 * SLICES + 1))
        sp.wait_ge(s_z, TILES * 2 * SLICES + SBANKS)
        sp.dma_start(A[:, 0:EARLY, :], At_v[:, 0:EARLY, :]).then_inc(s_back[0], 16)
        sp.wait_ge(s_pv, TILES * (2 * SLICES + 2))
        sp.dma_start(A[:, EARLY:NEXT, :], At_v[:, EARLY:NEXT, :]).then_inc(s_back[1], 16)
        for c in range(BLOCKS):
            sp.wait_ge(s_x3, c + 1)
            if c == BLOCKS - 1:
                sp.wait_ge(s_sum, 2 * SLICES)
                sp.dma_start(A[:, NEXT:GONE, :], At_v[:, NEXT:GONE, :]).then_inc(s_back[2], 16)
            sp.dma_start(x3v[:, blk(c), :], G[:, blk(c), :]).then_inc(s_x3d, 16)
        sp.wait_ge(s_parts, 6 * BLOCKS)
        sp.wait_ge(s_x3d, 16 * BLOCKS)
        for c in range(BLOCKS):
            sp.dma_start(G[:, blk(c), :], x3v[:, blk(c), :]).then_inc(s_gx, 16)
        out_v = t["out"][0:(TILES - 1) * P, :].rearrange("(t p) f -> p t f", p=P)
        for c in range(BLOCKS):
            e = min((c + 1) * BT, TILES - 1)
            sp.wait_ge(s_g, 4 * BLOCKS + c + 2)
            sp.dma_start(out_v[:, c * BT:e, :], G[:, c * BT:e, :]).then_inc(s_fin, 16)
        sp.dma_start(t["out"][(TILES - 1) * P:N, :], G[0:LAST, TILES - 1, :]).then_inc(s_fin, 16)
        sp.wait_ge(s_fin, 16 * (BLOCKS + 1))

    def zeros_of(lo, hi):
        return A32[:, lo * NPAD // 2:hi * NPAD // 2]

    @block.gpsimd
    def _(pool):
        pool.memset(G[:, TILES - 1, :], 0.0).then_inc(s_misc, 1)
        pool.iota(iota_i, [[1, KEYS]], base=0, channel_multiplier=0).then_inc(s_iota, 1)
        pool.iota(iota_each_i.rearrange("p (n c) -> p n c", c=GROUP), [[1, P], [0, GROUP]], base=0,
                  channel_multiplier=0).then_inc(s_iota, 1)
        pool.memset(ident, 0.0).then_inc(s_ident, 1)
        pool.wait_ge(s_ident, 1)
        pool.affine_select(out=ident, in_=ident, compare_op=ALU.not_equal, fill=1.0, base=0,
                           pattern=[[-1, P]], channel_multiplier=1).then_inc(s_ident, 1)
        pool.memset(half_neg, -0.5).then_inc(s_ident, 1)
        pool.wait_ge(s_ident, 2)
        pool.tensor_copy(ident16, ident).then_inc(s_ident, 1)
        pool.memset(zeros_of(DVE_ZEROS + ACT_ZEROS, TILES - PREP_TILES), 0.0).then_inc(s_zero, 1)
        pool.wait_ge(s_ident, 4)
        pool.wait_ge(s_eps, 16)
        pool.tensor_scalar(one_eps, one_eps, 1.0, 1.0 / LN_SCALE, ALU.add, ALU.mult).then_inc(s_misc, 1)

        def norm_power(nb, c):
            pool.wait_ge(s_ve, BLOCKS * nb + c + 1)
            r = rstd[:, blk(c)]
            pool.tensor_tensor(r, r, half_neg[:, 0:BT], ALU.pow).then_inc(s_rs, 1)

        pool.wait_ge(s_ve, BLOCKS)
        pool.tensor_tensor(rstd, rstd, half_neg[:, 0:1].broadcast_to([P, TILES]), ALU.pow).then_inc(s_rs, BLOCKS)

        def hidden_powers(m):
            for q in range(BT):
                pool.wait_ge(s_hve, m * BT + q + 1)
                r = hrstd[:, q % 2:q % 2 + 1]
                pool.tensor_tensor(r, r, half_neg[:, 0:1], ALU.pow).then_inc(s_hrs, 1)

        with pool.Fori(0, BLOCKS - 1) as m:
            hidden_powers(m)
            norm_power(1, m)
        hidden_powers(BLOCKS - 1)
        pool.wait_ge(s_dg, 2)
        pool.tensor_tensor(dinv, dinv, half_neg[:, 0:1].broadcast_to([P, TILES]), ALU.pow).then_inc(s_dinv, 1)
        norm_power(1, BLOCKS - 1)
        for c in range(BLOCKS):
            norm_power(2, c)
        pool.wait_ge(s_w, 16 * 18)
        pool.wait_ge(s_h, 3 * BLOCKS)
        for c in range(BLOCKS):
            pool.tensor_tensor(G[:, blk(c), :], G[:, blk(c), :],
                               brow[:, 0, :].unsqueeze(1).broadcast_to([P, BT, D]), ALU.add).then_inc(s_xbb, 1)
        for c in range(BLOCKS):
            norm_power(3, c)

    @block.scalar
    def _(act):
        act.preload_act_table(ACT.Copy)
        act.wait_ge(s_ones, 2)
        for tt in range(DVE_ZEROS, DVE_ZEROS + ACT_ZEROS):
            last = act.activation(zeros_of(tt, tt + 1), zero.broadcast_to([P, NPAD // 2]), ACT.Copy)
        act.wait_ge(s_keyT, 1)
        for tt in range(TILES - PREP_TILES, TILES):
            last = act.activation(zeros_of(tt, tt + 1), zero.broadcast_to([P, NPAD // 2]), ACT.Copy)
        last.then_inc(s_zero, 1)
        act.wait_ge(s_sh, BLOCKS)
        for c in range(BLOCKS):
            for tt in range(c * BT, (c + 1) * BT):
                last = act.activation(G[:, tt, :], G[:, tt, :], ACT.Relu,
                                      bias=shift[:, tt:tt + 1], scale=rstd[:, tt:tt + 1])
            last.then_inc(s_h, 1)
        with act.Fori(0, CHUNKS // TURN) as i:
            for k in range(0, TURN, 2):
                b = k % BANKS
                act.wait_ge(s_out, i * TURN + TURN + k + 2)
                act.wait_ge(s_acc, i * TURN + TURN + k + 2 - BANKS)
                act.activation(counts[:, b:b + 2, :], psum[:, b:b + 2, 0:KEYS], ACT.Copy).then_inc(s_cnt, 1)

        def flat(v):
            return v.rearrange("p t f -> p (t f)")

        def split(p, nb, normal):
            for c in range(BLOCKS + 1):
                n = BLOCKS * p + c
                if c < BLOCKS:
                    if normal:
                        act.wait_ge(s_sh, BLOCKS * nb + c + 1)
                        if c >= 2:
                            act.wait_ge(s_r1, n - 1)
                            act.wait_ge(s_hi, n - 1)
                        for q in range(BT):
                            tt = c * BT + q
                            last = act.activation(work[:, c % 2, q * D:(q + 1) * D], G[:, tt, :], ACT.Relu,
                                                  bias=shift[:, tt:tt + 1], scale=rstd[:, tt:tt + 1])
                        last.then_inc(s_h, 1)
                        act.wait_ge(s_h, BLOCKS * nb + c + 1)
                        src = work[:, c % 2, :]
                    else:
                        if p:
                            act.wait_ge(s_g, BLOCKS * (p - 2) + c + 1 + 1)
                        src = flat(G[:, blk(c), :])
                    if c == 0 and p:
                        act.wait_ge(s_scale, p)
                    act.activation(flat(parts[:, 0, blk(c), :]), src, ACT.Copy,
                                   scale=scales[:, 0:1] if p else LN_SCALE).then_inc(s_hi, 1)
                if c and not normal:
                    act.wait_ge(s_r1, n)
                    act.activation(flat(parts[:, 1, blk(c - 1), :]), rest[:, (c - 1) % 2, :], ACT.Copy,
                                   scale=LOW_SCALE if p else 1.0).then_inc(s_parts, 1)

        act.wait_ge(s_acc, BUILT)
        act.wait_ge(s_h, BLOCKS)
        split(0, 0, False)
        act.wait_ge(s_w, 16 * 6)
        act.wait_ge(s_misc, 2)

        def gelu(m, q, ks):
            if ks[0] == 0:
                act.wait_ge(s_hnT, m * BT + q + 1)
                act.wait_ge(s_o, m * BT + q + 1)
            for k in ks:
                last = act.activation(gel[:, k, :], psum[:, 6, k * P:(k + 1) * P], ACT.Gelu,
                                      bias=beta[:, k:k + 1], scale=gamma[:, k:k + 1])
            if ks[-1] == 3:
                last.then_inc(s_gel, 1)

        def l0_step(c, m):
            for tt in range(TILES):
                for n in pieces_at(tt):
                    q, st, k = piece(n)
                    act.wait_ge(s_tp, c * PN + n + 1)
                    act.wait_ge(s_td[n % STAGES], 16 * (c * (PN // STAGES) + n // STAGES) + 16)
                    act.activation(stage[n % STAGES][:, 0:k * P], psum[:, 2 + n % 2, 0:k * P], ACT.Copy,
                                   accum_out=deg_parts[:, ds(c * BT + q, 1), st // 4:st // 4 + 1]
                                   .rearrange("p a b -> p (a b)")).then_inc(s_ts, 1)
                for back, ks in ((1, (2, 3)), (0, (0, 1))):
                    step, q = mlp_at(tt - back)
                    if m is not None and step == "transpose":
                        gelu(m, q, ks)
                if tt == HT_AT:
                    act.wait_ge(s_hTp, c + 1)
                    act.wait_ge(s_aggT, 2 * c + 2)
                    act.activation(hT, pflat[:, 4 * 512:4 * 512 + BW], ACT.Copy, scale=one_eps).then_inc(s_hT, 1)

        act.preload_act_table(ACT.Gelu)
        l0_step(0, None)
        with act.Fori(1, BLOCKS) as c:
            l0_step(c, c - 1)
        for q in range(BT):
            gelu(BLOCKS - 1, q, (0, 1, 2, 3))

        for l in range(3):
            act.wait_ge(s_agg, 2 * BLOCKS * (l + 1))
            split(l + 1, 1, l == 0)

        def normed(nb, done):
            for c in range(BLOCKS):
                act.wait_ge(s_sh, BLOCKS * nb + c + 1)
                if c >= 2:
                    act.wait_ge(done, c - 1)
                for q in range(BT):
                    tt = c * BT + q
                    last = act.activation(work[:, c % 2, q * D:(q + 1) * D], G[:, tt, :], ACT.Relu,
                                          bias=shift[:, tt:tt + 1], scale=rstd[:, tt:tt + 1])
                last.then_inc(s_h, 1)

        act.wait_ge(s_at, 16)
        act.wait_ge(s_agg, 2 * 4 * BLOCKS)
        act.wait_ge(s_w, 16 * 18)
        normed(2, s_xT)
        for l in range(2):
            for c in range(0, SLICES, 2):
                k = SLICES * l + c
                act.wait_ge(s_hl, k + 1)
                act.activation(HT[:, c * SW:(c + 1) * SW], psum[:, c % 4, 0:SW], ACT.Relu,
                               bias=bcol[:, l:l + 1]).then_inc(s_hls, 1)

            for n in range(PIECES):
                act.wait_ge(s_ht, PIECES * l + n + 1)
                w = min(4, TILES - 4 * n)
                act.activation(flat(H[:, 4 * n:4 * n + w, :]), psum[:, 5 + n % 2, 0:w * P], ACT.Copy)\
                    .then_inc(s_hts, 1)
            act.preload_act_table(ACT.Exp)

            def exps(c, b):
                k = SLICES * l + c
                act.wait_ge(s_nt, k + 1)
                for j in range(TILES):
                    act.activation(Z[b][:, j, :], Z[b][:, j, :], ACT.Exp, bias=neg_top[:, ds(c, 1)]).then_inc(s_e, 1)
                act.wait_ge(s_pv, TILES * (k + 3))
                act.activation(XT[:, ds(c * SW, SW)], psum[:, 5 + b, 0:SW], ACT.Copy).then_inc(s_ot, 2)

            with act.Fori(0, SLICES // 2) as i:
                c = i * 2
                exps(c, 0)
                exps(c + 1, 1)
            act.wait_ge(s_fs, 3 * l + 1)
            act.activation(wts, neg_top, ACT.Exp, bias=least, scale=-1.0).then_inc(s_wt, 1)
        act.wait_ge(s_x3, BLOCKS)
        for p in (4, 5):
            act.wait_ge(s_agg, 2 * BLOCKS * p)
            split(p, 3, p == 4)

    @block.tensor
    def _(pe):
        pe.wait_ge(s_ident, 4)
        pe.wait_ge(s_prep, PREPARED)
        for g in range(GROUPS):
            for b, v in enumerate((key, slo, dst_f, shi)):
                pe.transpose(psum[0:EC, b, g * GC:(g + 1) * GC], v[:, g, :], ident[0:GC, 0:GC])
            pe.transpose(psum[0:1, 4, g * GC:(g + 1) * GC], base[:, g:g + 1], ident[0:GC, 0:GC])
        pe.transpose(psum[0:1, 4, CHUNKS:CHUNKS + GC], span, ident[0:GC, 0:GC]).then_inc(s_keyT, 1)
        pe.wait_ge(s_keysb, 7)
        pe.sem_inc(s_out, TURN)
        with pe.Fori(0, CHUNKS // TURN) as i:
            for k in range(TURN):
                pe.wait_ge(s_hk, i * TURN + k + 1)
                if k % 2 == 0:
                    pe.wait_ge(s_cnt, i * (TURN // 2) + k // 2 + 1)
                pe.matmul(psum[:, k % BANKS, 0:KEYS], hot_slo[:, k % HOTS // GROUP, :, k % GROUP], hot_key[:, k % HOTS, :],
                          start=True, stop=True).then_inc(s_out, 1)
        pe.wait_ge(s_keysb, 7)
        _, flags = nc.values_load_multi_w_load_instructions(
            wide, engines=[mybir.EngineType.PE], min_val=0, max_val=1,
            skip_runtime_bounds_check_because="a comparison's result")
        with pe.If(flags[0]):
            with pe.Fori(0, ROUNDS) as r:
                def wide_products(n, first=False, last=False):
                    pe.wait_ge(s_whot, r * (CHUNKS // HOTS) + n + 1)
                    for k in range(HOTS):
                        done = pe.matmul(psum[:, 0, 0:KEYS], hot_slo[:, k // GROUP, :, k % GROUP], hot_key[:, k, :],
                                         start=(first and k == 0), stop=(last and k == HOTS - 1))
                    done.then_inc(s_wout, 1)

                pe.wait_ge(s_wadd, r + 1)
                wide_products(0, first=True)
                with pe.Fori(1, CHUNKS // HOTS - 1) as n:
                    wide_products(n)
                wide_products(CHUNKS // HOTS - 1, last=True)

        def aggregate(p, c, after=None, reloaded=False):
            n = BLOCKS * p + c
            first, last_steps = range(ENDS), range(TILES - ENDS, TILES)
            for group in (first, *([tt] for tt in range(ENDS, TILES - ENDS)), last_steps):
                for tt in group:
                    if tt % BT == 0:
                        pe.wait_ge(s_parts, BLOCKS * p + tt // BT + 1)
                    if reloaded and tt in (0, EARLY, NEXT):
                        pe.wait_ge(s_back[(0, EARLY, NEXT).index(tt)], 16)
                for h in range(2):
                    if group is first:
                        pe.wait_ge(s_aggT, 2 * n + 1 + h)
                    for tt in group:
                        for k in range(PARTS):
                            bank = h if p == 0 else 2 * k + h
                            start = tt == 0 and (k == 0 or p > 0)
                            stop = tt == TILES - 1 and (k == PARTS - 1 or p > 0)
                            last = pe.matmul(psum[:, bank, 0:HALF], parts[:, k, tt, :],
                                             A[:, tt, ds(c * BW + h * HALF, HALF)], start=start, stop=stop)
                    if group is last_steps:
                        last.then_inc(s_agg, 1)
                if after:
                    for tt in group:
                        after(tt)

        def mlp(m, step, q):
            g = m * BT + q
            if step == "hidden":
                pe.wait_ge(s_aggT, 2 * m + 4)
                if q >= 2:
                    pe.wait_ge(s_hb, g - 1)
                else:
                    pe.wait_ge(s_hT, m + 1)
                pe.matmul(psum[:, 4 + q % 2, :], aggT[:, q * P:(q + 1) * P], w1, start=True, stop=True)\
                    .then_inc(s_hp, 1)
            if step == "transpose":
                pe.wait_ge(s_hn, g + 1)
                pe.wait_ge(s_gel, g + 1)
                for k in range(4):
                    last = pe.transpose(psum[:, 6, k * P:(k + 1) * P], hid[:, q % 2, k * P:(k + 1) * P], ident)
                last.then_inc(s_hnT, 1)
            if step == "output":
                pe.wait_ge(s_gel, g + 2)
                pe.wait_ge(s_xn, g + 1)
                for k in range(4):
                    last = pe.matmul(psum[:, 7, 0:D], gel[:, k, :], w2[:, k, :], start=(k == 0), stop=(k == 3))
                last.then_inc(s_o, 1)

        def l0_step(c, m):
            def between(tt):
                for n in pieces_at(tt):
                    q, st, k = piece(n)
                    pe.wait_ge(s_ts, c * PN + n + (2 if n == 0 else 1))
                    for j in range(k):
                        last = pe.matmul(psum[:, 2 + n % 2, j * P:(j + 1) * P],
                                         A[:, st + j, ds((c * BT + q) * P, P)], ident16, start=True, stop=True)
                    last.then_inc(s_tp, 1)
                if m is not None:
                    mlp(m, *mlp_at(tt))
                if tt == HT_AT:
                    if m is not None:
                        pe.wait_ge(s_hb, (m + 1) * BT)
                    for q in range(BT):
                        for k in range(PARTS):
                            last = pe.matmul(pflat[:, 4 * 512 + q * P:4 * 512 + (q + 1) * P],
                                             parts[:, k, ds(c * BT + q, 1), :].rearrange("p a f -> p (a f)"), ident16,
                                             start=(k == 0), stop=(k == PARTS - 1))
                    last.then_inc(s_hTp, 1)

            aggregate(0, c, between)

        l0_step(0, None)
        pe.wait_ge(s_w, 16 * 6)
        with pe.Fori(1, BLOCKS) as c:
            l0_step(c, c - 1)
        for q in range(-1, BT + 2):
            for step, back in (("output", 2), ("hidden", -1), ("transpose", 1)):
                if 0 <= q - back < BT:
                    mlp(BLOCKS - 1, step, q - back)

        passes = [0]

        def gcn(p, l, scaled):
            def weigh(c):
                pe.wait_ge(s_aggT, (BLOCKS * p + c) * 2 + 4)
                pe.wait_ge(s_u, BLOCKS * (p - 1) + c + 1)
                for q in range(BT):
                    last = pe.matmul(pflat[:, 4 * 512 + q * P:4 * 512 + (q + 1) * P], aggT[:, q * P:(q + 1) * P],
                                     wmat[:, l, :], start=True, stop=True)
                last.then_inc(s_y, 1)

            aggregate(p, 0, reloaded=(p == 4))
            with pe.Fori(1, BLOCKS) as c:
                aggregate(p, c, lambda tt: weigh(c - 1) if tt == Y_AT else None)
            weigh(BLOCKS - 1)
            if l < scaled:
                m = passes[0]
                passes[0] += 1
                pe.wait_ge(s_st, SCALE_STEPS * m + 1)
                pe.transpose(psum[0:1, 7, 0:P], peak, ident).then_inc(s_sp, 1)
                pe.wait_ge(s_st, SCALE_STEPS * m + SCALE_STEPS)
                pe.matmul(psum[:, 7, 256:258], ones[0:1, :], top_bits, start=True, stop=True).then_inc(s_sp, 1)

        pe.wait_ge(s_w, 16 * 12)
        pe.wait_ge(s_self, 2)
        for l in range(3):
            gcn(l + 1, l, 2)

        pe.wait_ge(s_w, 16 * 18)
        pe.wait_ge(s_u, 3 * BLOCKS + 1)
        for c in range(BLOCKS):
            pe.wait_ge(s_h, 2 * BLOCKS + c + 1)
            if c >= 2:
                pe.wait_ge(s_xTs, c - 1)
            b = (4 + 2 * (c % 2)) * 512
            for q in range(BT):
                last = pe.transpose(pflat[:, b + q * P:b + (q + 1) * P], work[:, c % 2, q * D:(q + 1) * D], ident)
            last.then_inc(s_xT, 1)
        for l in range(2):
            if l:
                pe.wait_ge(s_sc, SLICES)
            else:
                pe.wait_ge(s_xTs, BLOCKS)
            for c in range(SLICES):
                k = SLICES * l + c
                if c >= 4:
                    pe.wait_ge(s_hlv if c % 2 else s_hls, SLICES // 2 * l + c // 2 - 1)
                pe.matmul(psum[:, c % 4, 0:SW], wmat[:, l, :], XT[:, c * SW:(c + 1) * SW], start=True, stop=True)\
                    .then_inc(s_hl, 1)
            pe.wait_ge(s_hls, SLICES // 2 * (l + 1))
            pe.wait_ge(s_hlv, SLICES // 2 * (l + 1))

            def turned(n):
                if n >= 2:
                    pe.wait_ge(s_hts, PIECES * l + n - 1)
                for tt in range(4 * n, min(4 * n + 4, TILES)):
                    last = pe.transpose(psum[:, 5 + n % 2, (tt - 4 * n) * P:(tt - 4 * n + 1) * P],
                                        HT[:, tt * P:(tt + 1) * P], ident)
                last.then_inc(s_ht, 1)

            def scores(c, j):
                m = TILES * (SLICES * l + c) + j
                pe.wait_ge(s_z, m + 1)
                pe.matmul(psum[:, j % SBANKS, 0:SW], HT[:, j * P:(j + 1) * P], HT[:, ds(c * SW, SW)],
                          start=True, stop=True).then_inc(s_s, 1)

            def weighted(c, b, j):
                k = SLICES * l + c
                if j == 0:
                    pe.wait_ge(s_ot, k + 1)
                pe.wait_ge(s_p, TILES * (k + 2) + j + 1)
                pe.matmul(psum[:, 5 + b, 0:SW], H[:, j, :], Z[b][:, j, :], start=(j == 0), stop=(j == TILES - 1))\
                    .then_inc(s_pv, 1)

            def turn_peak(c):
                pe.wait_ge(s_rm, SLICES * l + c + 1)
                pe.transpose(psum[0:1, 7, 0:P], peak, ident).then_inc(s_rmT, 1)

            def spread_top(c):
                pe.wait_ge(s_top, SLICES * l + c + 1)
                pe.matmul(psum[:, 7, 256:257], ones[0:1, :], top, start=True, stop=True).then_inc(s_tb, 1)

            def step(c, b):
                for j in range(LEAD):
                    scores(c + 1, j)
                    if j == 1:
                        turn_peak(c)
                    if j == 3:
                        spread_top(c)
                for j in range(TILES):
                    weighted(c, b, j)
                    if j + LEAD < TILES:
                        scores(c + 1, j + LEAD)

            for j in range(TILES):
                scores(0, j)
                n, r = divmod(j, TURN_EVERY)
                if r == TURN_EVERY - 1 and n < PIECES:
                    turned(n)
            pe.wait_ge(s_hts, PIECES * (l + 1))
            with pe.Fori(0, (SLICES - 2) // 2) as i:
                c = i * 2
                step(c, 0)
                step(c + 1, 1)
            step(SLICES - 2, 0)
            turn_peak(SLICES - 1)
            spread_top(SLICES - 1)
            for j in range(TILES):
                weighted(SLICES - 1, 1, j)
            pe.wait_ge(s_sum, SLICES * (l + 1))
            pe.matmul(psum[:, 7, 0:SLICES], ones, sums, start=True, stop=True).then_inc(s_ls, 1)
        pe.wait_ge(s_sc, 2 * SLICES)
        for c in range(BLOCKS):
            if c >= 2:
                pe.wait_ge(s_x3, c - 1)
            b = 2 * (c % 2) * 512
            for q in range(BT):
                tt = c * BT + q
                last = pe.matmul(pflat[:, b + q * P:b + (q + 1) * P], XT[:, tt * P:(tt + 1) * P], wmat[:, 2, :],
                                 start=True, stop=True)
            last.then_inc(s_x3p, 1)
        pe.wait_ge(s_w, 16 * 22)
        pe.wait_ge(s_x3, BLOCKS)
        for l in range(2):
            gcn(l + 4, l, 1)

    @block.vector
    def _(dve):
        prep = [0]

        def link(ins):
            prep[0] += 1
            ins.then_inc(s_prep, 1)
            dve.wait_ge(s_prep, prep[0])

        def flat(v):
            return v.rearrange("p t f -> p (t f)")

        def norm_start(nb, c, looped=False):
            n = BLOCKS * nb + c + 1
            if looped:
                dve.memset(scrap[:, 0:1], 0.0)
            for q in range(BT):
                last = dve.bn_stats(block_stats[:, q, :], tile_of(G, c, q))
            last.then_inc(s_bn, 1)
            dve.wait_ge(s_bn, n)
            if looped:
                dve.memset(scrap[:, 1:2], 0.0)
            for q in range(BT):
                last = dve.bn_aggr(block_mv[:, q, :], block_stats[:, q, :])
            last.then_inc(s_mv, 1)
            dve.wait_ge(s_mv, n)
            dve.tensor_copy(mean_var[:, blk(c), 0], block_mv[:, :, 0])
            dve.tensor_scalar(rstd[:, blk(c)], block_mv[:, :, 1], LN_EPS, None, ALU.add).then_inc(s_ve, 1)

        def tile_of(v, c, q):
            return v[:, ds(c * BT + q, 1), :].rearrange("p a f -> p (a f)")

        def norm_end(nb, c, degree):
            n = BLOCKS * nb + c + 1
            dve.wait_ge(s_rs, n)
            if degree:
                link(dve.tensor_tensor(rstd[:, blk(c)], rstd[:, blk(c)], dinv[:, blk(c)], ALU.mult))
            dve.scalar_tensor_tensor(out=shift[:, blk(c)], in0=mean_var[:, blk(c), 0], scalar=-1.0,
                                     in1=rstd[:, blk(c)], op0=ALU.mult, op1=ALU.mult).then_inc(s_sh, 1)

        for s, v in ((s_aggT, 2), (s_ts, 2), (s_x1, 16), (s_o, 1), (s_y, 1), (s_u, 1), (s_g, 1), (s_gel, 1),
                     (s_ot, 2), (s_p, 2 * TILES), (s_z, SBANKS), (s_pv, 2 * TILES), (s_cnt, BANKS // 2),
                     (s_wadd, 1), (s_wout, 1), (s_xn, 1)):
            dve.sem_inc(s, v)
        for b in range(STAGES):
            dve.sem_inc(s_td[b], 16)
        for g in range(BLOCKS):
            dve.sem_inc(s_ad[g], 16)
        dve.memset(ones, 1.0).then_inc(s_ones, 1)
        dve.memset(zero, 0.0).then_inc(s_ones, 1)
        dve.memset(zeros_of(0, DVE_ZEROS), 0.0).then_inc(s_zero, 1)
        dve.wait_ge(s_edges, 32)
        link(dve.tensor_copy(dst_f, dst_i))
        link(dve.tensor_reduce(base, dst_f, AX.X, ALU.min))
        link(dve.tensor_copy(base_ii, base))
        link(dve.tensor_scalar(base_ii, base_ii, 0xFFFE, None, ALU.bitwise_and))
        link(dve.tensor_copy(base, base_ii))
        link(dve.tensor_tensor(rel, dst_f, base.unsqueeze(2).broadcast_to([GC, GROUPS, EC]), ALU.subtract))
        link(dve.tensor_reduce(span, rel, AX.XY, ALU.max))
        link(dve.tensor_scalar(part_i, src_i, 7, None, ALU.arith_shift_right))
        link(dve.tensor_copy(shi, part_i))
        link(dve.tensor_scalar(dst_i, src_i, P - 1, None, ALU.bitwise_and))
        link(dve.tensor_copy(slo, dst_i))
        link(dve.scalar_tensor_tensor(out=key, in0=shi, scalar=float(WIN), in1=rel, op0=ALU.mult, op1=ALU.add))
        link(dve.tensor_scalar(beyond, rel, float(WIN), FAR, ALU.is_ge, ALU.mult))
        link(dve.tensor_tensor(key, key, beyond, ALU.add))
        assert prep[0] == PREPARED
        dve.wait_ge(s_iota, 2)
        dve.tensor_copy(iota16, iota_i).then_inc(s_iota16, 1)
        dve.tensor_copy(iota_each, iota_each_i.rearrange("p (n c) -> p n c", c=GROUP)).then_inc(s_iota16, 1)
        dve.memset(keyT[:, CHUNKS:], -1.0).then_inc(s_keysb, 1)
        dve.memset(sloT[:, CHUNKS:], -1.0).then_inc(s_keysb, 1)
        for c in range(BLOCKS):
            dve.wait_ge(s_x, 16 * (BLOCKS + 1))
            for tt in range(c * BT, (c + 1) * BT):
                last = dve.bn_stats(stats[:, tt, :], G[:, tt, :])
            last.then_inc(s_bn, 1)
        dve.wait_ge(s_bn, BLOCKS)
        for tt in range(TILES):
            last = dve.bn_aggr(mean_var[:, tt, :], stats[:, tt, :])
        last.then_inc(s_mv, BLOCKS)
        dve.wait_ge(s_mv, BLOCKS)
        dve.tensor_scalar(rstd, mean_var[:, :, 1], LN_EPS, None, ALU.add).then_inc(s_ve, BLOCKS)
        dve.wait_ge(s_keyT, 1)
        dve.tensor_copy(keyT[:, 0:CHUNKS], psum[0:EC, 0, 0:CHUNKS]).then_inc(s_keysb, 1)
        dve.tensor_copy(sloT[:, 0:CHUNKS], psum[0:EC, 1, 0:CHUNKS]).then_inc(s_keysb, 1)
        dve.tensor_copy(dstT, psum[0:EC, 2, 0:CHUNKS]).then_inc(s_keysb, 1)
        dve.tensor_scalar(shiT, psum[0:EC, 3, 0:CHUNKS], float(WIN), None, ALU.mult).then_inc(s_keysb, 1)
        link(dve.tensor_reduce(widest, psum[0:1, 4, CHUNKS:CHUNKS + GC], AX.X, ALU.max))
        dve.tensor_copy(base_i, psum[0:1, 4, 0:CHUNKS]).then_inc(s_base, 1)
        dve.tensor_scalar(wide, widest, float(WIN), None, ALU.is_ge).then_inc(s_keysb, 1)
        dve.wait_ge(s_rs, BLOCKS)
        dve.scalar_tensor_tensor(out=shift, in0=mean_var[:, :, 0], scalar=-1.0, in1=rstd, op0=ALU.mult,
                                 op1=ALU.mult).then_inc(s_sh, BLOCKS)
        dve.wait_ge(s_keysb, 7)
        dve.wait_ge(s_base, 1)
        dve.wait_ge(s_iota16, 2)
        dve.wait_ge(s_zero, 3)
        dve.sem_inc(s_acc, TURN)

        def hot_places(b, chunk):
            dve.tensor_tensor(hot_slo[:, b // GROUP, :, :], iota_each,
                              sloT[:, ds(chunk, GROUP)].unsqueeze(1).broadcast_to([EC, P, GROUP]), ALU.is_equal)

        def hot_keys(b, chunk):
            return dve.tensor_scalar(hot_key[:, b, :], iota16[0:EC, :], keyT[:, ds(chunk, 1)], None, ALU.is_equal)

        def hot(i, k):
            b = k % HOTS
            if k % GROUP == 0:
                dve.wait_ge(s_out, i * TURN + TURN + k + GROUP - HOTS)
                hot_places(b, i * TURN + k)
            else:
                dve.wait_ge(s_out, i * TURN + TURN + k + 1 - HOTS)
            hot_keys(b, i * TURN + k).then_inc(s_hk, 1)

        for k in range(AHEAD):
            hot(0, k)
        with dve.Fori(0, CHUNKS // TURN) as i:
            def first_destinations(k):
                return nc.values_load_multi_w_load_instructions(
                    base_i[:, ds(i * TURN + k, LOADED)], engines=[mybir.EngineType.DVE], min_val=0, max_val=N - 1,
                    skip_runtime_bounds_check_because="a destination is a node: 0 to N - 1")[1]

            def add(k, lo):
                dve.wait_ge(s_cnt, i * (TURN // 2) + k // 2 + 1 + BANKS // 2)
                dve.wait_ge(s_acc, i * TURN + TURN + k)
                win = A[:, :, ds(lo, WIN)]
                dve.tensor_tensor(win, win, counts[:, k % BANKS, :].rearrange("p (t w) -> p t w", w=WIN),
                                  ALU.add).then_inc(s_acc, 1)

            for k in range(TURN):
                if k % LOADED == 0:
                    lows = first_destinations(k)
                hot(i, k + AHEAD)
                add(k, lows[k % LOADED])
        dve.wait_ge(s_acc, BUILT - 1)
        dve.wait_ge(s_hk, CHUNKS + AHEAD)
        _, flags = nc.values_load_multi_w_load_instructions(
            wide, engines=[mybir.EngineType.DVE], min_val=0, max_val=1,
            skip_runtime_bounds_check_because="a comparison's result")
        with dve.If(flags[0]):
            with dve.Fori(0, ROUNDS) as r:
                wide_steps = [0]

                def wide_link(ins):
                    wide_steps[0] += 1
                    ins.then_inc(s_wkey, 1)
                    dve.wait_ge(s_wkey, r * WIDE_STEPS + wide_steps[0])

                dve.tensor_scalar(out_of[:, 0, :], dstT, float(WIN), FAR, ALU.is_ge, ALU.mult)
                dve.tensor_scalar(out_of[:, 1, :], dstT, 0.0, FAR, ALU.is_lt, ALU.mult)
                wide_link(dve.tensor_tensor(keyT[:, 0:CHUNKS], shiT, dstT, ALU.add))
                wide_link(dve.tensor_tensor(keyT[:, 0:CHUNKS], keyT[:, 0:CHUNKS], out_of[:, 0, :], ALU.add))
                dve.tensor_tensor(keyT[:, 0:CHUNKS], keyT[:, 0:CHUNKS], out_of[:, 1, :], ALU.add).then_inc(s_wkey, 1)
                dve.tensor_scalar(dstT, dstT, float(WIN), None, ALU.subtract).then_inc(s_wkey, 1)
                with dve.Fori(0, CHUNKS // HOTS) as n:
                    dve.wait_ge(s_wkey, r * WIDE_STEPS + WIDE_STEPS)
                    dve.wait_ge(s_wout, r * (CHUNKS // HOTS) + n + 1)
                    for k in range(HOTS):
                        if k % GROUP == 0:
                            hot_places(k, n * HOTS + k)
                        last = hot_keys(k, n * HOTS + k)
                    last.then_inc(s_whot, 1)
                dve.wait_ge(s_wout, r * (CHUNKS // HOTS) + CHUNKS // HOTS + 1)
                dve.tensor_copy(A[:, :, ds(r * WIN, WIN)], psum[:, 0, 0:KEYS].rearrange("p (t w) -> p t w", w=WIN))\
                    .then_inc(s_wadd, 1)
            dve.wait_ge(s_wadd, ROUNDS + 1)
        dve.sem_inc(s_acc, 1)

        def split(p, nb, normal, degree):
            lag = 2 if normal else 1
            for step in range(BLOCKS + lag):
                if normal and 1 <= step <= BLOCKS:
                    norm_end(nb, step - 1, degree)
                c = step + 1 - lag
                if c >= 1:
                    n = BLOCKS * p + c
                    dve.wait_ge(s_hi, n)
                    if c >= 3:
                        dve.wait_ge(s_parts, n - 2)
                    if p and not normal:
                        dve.wait_ge(s_g, BLOCKS * (p - 2) + c + 1)
                    src = work[:, (c - 1) % 2, :] if normal else flat(G[:, blk(c - 1), :])
                    dve.scalar_tensor_tensor(out=rest[:, (c - 1) % 2, :], in0=src,
                                             scalar=scales[:, 0:1] if p else LN_SCALE,
                                             in1=flat(parts[:, 0, blk(c - 1), :]),
                                             op0=ALU.mult, op1=ALU.subtract).then_inc(s_r1, 1)
                    if normal:
                        dve.wait_ge(s_r1, n)
                        dve.tensor_scalar(flat(parts[:, 1, blk(c - 1), :]), rest[:, (c - 1) % 2, :], LOW_SCALE,
                                          None, ALU.mult).then_inc(s_parts, 1)

        split(0, 0, False, False)
        dve.wait_ge(s_w, 16 * 6)

        def aggregated(c):
            dve.wait_ge(s_hT, c + 1)
            for h in range(2):
                dve.wait_ge(s_agg, 2 * c + 1 + h)
                dve.scalar_tensor_tensor(out=aggT[:, h * HALF:(h + 1) * HALF], in0=psum[:, h, 0:HALF],
                                         scalar=1.0 / LN_SCALE, in1=hT[:, h * HALF:(h + 1) * HALF],
                                         op0=ALU.mult, op1=ALU.add).then_inc(s_aggT, 1)

        def mlp(m, last=False):
            for q in range(BT + 2):
                g = m * BT + q
                b = q % 2
                if q < BT:
                    if q >= 2:
                        dve.wait_ge(s_hnT, g - 1)
                    dve.wait_ge(s_hp, g + 1)
                    dve.tensor_tensor(hid[:, b, :], psum[:, 4 + b, :], b1row, ALU.add).then_inc(s_hb, 1)
                    dve.wait_ge(s_hb, g + 1)
                    dve.bn_stats(hstat, hid[:, b, :]).then_inc(s_hbn, 1)
                if 1 <= q <= BT:
                    dve.wait_ge(s_hrs, g)
                if q < BT:
                    dve.wait_ge(s_hbn, g + 1)
                if 1 <= q <= BT:
                    dve.tensor_scalar(hid[:, 1 - b, :], hid[:, 1 - b, :], hmv[:, 1 - b, 0:1],
                                      hrstd[:, 1 - b:2 - b], ALU.subtract, ALU.mult).then_inc(s_hn, 1)
                elif q == 0:
                    dve.memset(scrap, 0.0)
                if q < BT:
                    dve.bn_aggr(hmv[:, b, :], hstat).then_inc(s_hmv, 1)
                    dve.wait_ge(s_hmv, g + 1)
                    dve.tensor_scalar(hrstd[:, b:b + 1], hmv[:, b, 1:2], LN_EPS, None, ALU.add).then_inc(s_hve, 1)
                if q == 1:
                    dve.wait_ge(s_xb, 32 * (m + 1))
                    dve.tensor_tensor(xnew, xnew, brow[:, 0, :].unsqueeze(1).broadcast_to([P, BT, D]), ALU.add)\
                        .then_inc(s_xbb, 1)
                if q >= 2:
                    if last and q == 2:
                        for b in range(STAGES):
                            dve.wait_ge(s_td[b], 16 + 16 * BLOCKS * PN // STAGES)
                    dve.wait_ge(s_o, g)
                    if q == 2:
                        dve.wait_ge(s_xbb, m + 1)
                    dve.tensor_tensor(tile_of(G, m, q - 2), xnew[:, q - 2, :], psum[:, 7, 0:D], ALU.add)\
                        .then_inc(s_xn, 1)
            dve.wait_ge(s_xn, (m + 1) * BT + 1)
            norm_start(1, m, looped=not last)

        aggregated(0)
        with dve.Fori(1, BLOCKS) as c:
            mlp(c - 1)
            aggregated(c)
        dve.wait_ge(s_ts, BLOCKS * PN + 2)
        dve.tensor_reduce(dinv, deg_parts, AX.X, ALU.add).then_inc(s_dg, 1)
        dve.wait_ge(s_dg, 1)
        dve.tensor_scalar(dinv, dinv, 1.0, 1.0, ALU.add, ALU.max).then_inc(s_dg, 1)
        mlp(BLOCKS - 1, last=True)
        dve.wait_ge(s_agg, 2 * BLOCKS)
        dve.wait_ge(s_tp, BLOCKS * PN)
        W = NPAD + P
        dve_diag = Aflat[:, 0:(TILES - 1) * W].rearrange("p (t w) -> p t w", w=W)[:, :, 0:P]
        dve.tensor_tensor(dve_diag, dve_diag, ident16.unsqueeze(1).broadcast_to([P, TILES - 1, P]), ALU.add)\
            .then_inc(s_self, 1)
        lastd = A[:, TILES - 1, (TILES - 1) * P:]
        dve.tensor_tensor(lastd, lastd, ident16, ALU.add).then_inc(s_self, 1)

        passes = [0]
        low = rest[:, 0, :].rearrange("p (h n) -> p h n", h=2)

        def static_scale():
            dve.memset(scales[:, 0:1], LN_SCALE).then_inc(s_scale, 1)
            link(dve.tensor_scalar(dinv_out, dinv, 1.0 / LN_SCALE, None, ALU.mult))

        def gcn(p, l, final):
            with dve.Fori(0, BLOCKS) as c:
                n = BLOCKS * (p - 1) + c + 1
                dve.wait_ge(s_y, n)
                for h in range(2):
                    dve.wait_ge(s_agg, 2 * (BLOCKS * p + c) + 1 + h)
                    dve.tensor_scalar(low[:, h, :], psum[:, 2 + h, 0:HALF], 1.0 / LOW_SCALE, None, ALU.mult)\
                        .then_inc(s_low, 1)
                    dve.wait_ge(s_low, 2 * n + h - 1)
                    dve.tensor_tensor(aggT[:, h * HALF:(h + 1) * HALF], low[:, h, :], psum[:, h, 0:HALF],
                                      ALU.add).then_inc(s_aggT, 1)
                dve.wait_ge(s_y, n + 1)
                u = work[:, 0, :].rearrange("p (t f) -> p t f", t=BT)
                v = work[:, 1, :].rearrange("p (t f) -> p t f", t=BT)
                y = pflat[:, 4 * 512:4 * 512 + BW].rearrange("p (t f) -> p t f", t=BT)
                d = dinv[:, blk(c)].unsqueeze(2).broadcast_to([P, BT, D])
                dve.tensor_tensor(u, y, dinv_out[:, blk(c)].unsqueeze(2).broadcast_to([P, BT, D]), ALU.mult)\
                    .then_inc(s_u, 1)
                dve.wait_ge(s_u, n + 1)
                dve.tensor_tensor(v, u, brow[:, l, :].unsqueeze(1).broadcast_to([P, BT, D]), ALU.add)\
                    .then_inc(s_ub, 1)
                dve.wait_ge(s_ub, n)
                if final:
                    dve.tensor_tensor(G[:, blk(c), :], G[:, blk(c), :], v, ALU.add).then_inc(s_g, 1)
                    if p == 3:
                        dve.wait_ge(s_g, n + 1)
                        norm_start(2, c, looped=True)
                else:
                    dve.scalar_tensor_tensor(out=G[:, blk(c), :], in0=v, scalar=0.0, in1=d, op0=ALU.max,
                                             op1=ALU.mult).then_inc(s_g, 1)
                    dve.wait_ge(s_g, n + 1)
                    dve.tensor_reduce(block_top[:, ds(c, 1)], G[:, blk(c), :], AX.XY, ALU.max).then_inc(s_bt, 1)
            if final:
                return
            m = passes[0]
            passes[0] += 1
            steps = [SCALE_STEPS * m]

            def scale_step(ins):
                steps[0] += 1
                ins.then_inc(s_st, 1)
                return steps[0]

            dve.wait_ge(s_bt, BLOCKS * (m + 1))
            scale_step(dve.tensor_reduce(peak, block_top, AX.X, ALU.max))
            dve.wait_ge(s_sp, 2 * m + 1)
            dve.wait_ge(s_st, scale_step(dve.tensor_reduce(top_bits[:, 0:1], psum[0:1, 7, 0:P], AX.X, ALU.max)))
            dve.wait_ge(s_st, scale_step(dve.tensor_scalar(top_bits[:, 0:1], top_bits[:, 0:1], LEAST_TOP, None,
                                                           ALU.max)))
            bits = top_bits.bitcast(I32)
            dve.wait_ge(s_st, scale_step(dve.tensor_scalar(bits[:, 1:2], bits[:, 0:1], EXPONENT, None,
                                                           ALU.bitwise_and)))
            scale_step(dve.tensor_scalar(bits[:, 0:1], bits[:, 1:2], -1.0, float((127 + 127 + TOP_POWER) << 23),
                                         ALU.mult, ALU.add))
            dve.wait_ge(s_sp, 2 * m + 2)
            dve.tensor_copy(scales[:, 0:1], psum[:, 7, 256:257]).then_inc(s_scale, 1)
            link(dve.tensor_scalar(scales[:, 1:2], psum[:, 7, 257:258], 2.0 ** -TOP_POWER, None, ALU.mult))
            link(dve.tensor_scalar(dinv_out, dinv, scales[:, 1:2], None, ALU.mult))

        dve.wait_ge(s_dinv, 1)
        dve.wait_ge(s_w, 16 * 12)
        static_scale()
        for l in range(3):
            split(l + 1, 1, l == 0, True)
            if l == 2:
                dve.wait_ge(s_gx, 16 * BLOCKS)
            gcn(l + 1, l, l == 2)

        dve.wait_ge(s_g, 3 * BLOCKS + 1)
        for c in range(BLOCKS):
            norm_end(2, c, False)
        dve.wait_ge(s_at, 16)
        for c in range(BLOCKS):
            dve.wait_ge(s_xT, c + 1)
            b = (4 + 2 * (c % 2)) * 512
            dve.tensor_copy(XT[:, c * BW:(c + 1) * BW], pflat[:, b:b + BW]).then_inc(s_xTs, 1)
        dve.wait_ge(s_w, 16 * 18)
        dve.wait_ge(s_agg, 2 * 4 * BLOCKS)
        for l in range(2):
            for c in range(1, SLICES, 2):
                dve.wait_ge(s_hl, SLICES * l + c + 1)
                dve.tensor_scalar(HT[:, c * SW:(c + 1) * SW], psum[:, c % 4, 0:SW], bcol[:, l:l + 1], 0.0,
                                  ALU.add, ALU.max).then_inc(s_hlv, 1)
            def edges(c, b, j):
                k = SLICES * l + c
                dve.wait_ge(s_ad[j // BT], 16 * (k + 2))
                h = j // SBANKS % 2
                dve.tensor_scalar(mask[:, SBANKS * h:SBANKS * (h + 1), :], Ab[b][:, j:j + SBANKS, :], 1.0, None,
                                  ALU.min).then_inc(s_mask, 1)

            def masked_waits(c, j):
                m = TILES * (SLICES * l + c) + j
                dve.wait_ge(s_s, m + 1)
                dve.wait_ge(s_pv, m + 1)
                if j % SBANKS == 0:
                    dve.wait_ge(s_mask, BLOCKS * (SLICES * l + c) + j // SBANKS + 1)

            def masked(b, j):
                dve.tensor_tensor_reduce(Z[b][:, j, :], mask[:, j % (2 * SBANKS), :], psum[:, j % SBANKS, 0:SW], 1.0,
                                         0.0, ALU.mult, ALU.max, rowmax[:, j:j + 1]).then_inc(s_z, 1)

            def weights(c, b, j):
                k = SLICES * l + c
                dve.wait_ge(s_e, TILES * k + j + 1)
                dve.tensor_tensor_reduce(Z[b][:, j, :], Z[b][:, j, :], Ab[b][:, j, :], 1.0, 0.0,
                                         ALU.mult, ALU.add, rowsum[:, b, j:j + 1]).then_inc(s_p, 1)

            def slice_sum(c, b):
                dve.wait_ge(s_p, TILES * (SLICES * l + c + 3))
                dve.tensor_reduce(sums[:, ds(c, 1)], rowsum[:, b, :], AX.X, ALU.add).then_inc(s_sum, 1)

            def slice_peak(c):
                dve.wait_ge(s_z, TILES * (SLICES * l + c + 1) + SBANKS)
                dve.tensor_reduce(peak, rowmax, AX.X, ALU.max).then_inc(s_rm, 1)

            def slice_top(c):
                dve.wait_ge(s_rmT, SLICES * l + c + 1)
                dve.tensor_reduce(top, psum[0:1, 7, 0:P], AX.X, ALU.max).then_inc(s_top, 1)

            def slice_neg(c):
                dve.wait_ge(s_tb, SLICES * l + c + 1)
                dve.tensor_scalar(neg_top[:, ds(c, 1)], psum[:, 7, 256:257], -1.0, None, ALU.mult).then_inc(s_nt, 1)

            def step(c, b):
                slice_peak(c)
                edges(c + 1, 1 - b, 0)
                masked_waits(c + 1, 0)
                slice_top(c)
                masked(1 - b, 0)
                masked_waits(c + 1, 1)
                slice_neg(c)
                masked(1 - b, 1)
                for j in range(TILES):
                    n = j + 2
                    if n < TILES:
                        if n % SBANKS == 0:
                            edges(c + 1, 1 - b, n)
                        masked_waits(c + 1, n)
                    weights(c, b, j)
                    if n < TILES:
                        masked(1 - b, n)
                slice_sum(c, b)

            for j in range(TILES):
                if j % SBANKS == 0:
                    edges(0, 0, j)
                masked_waits(0, j)
                masked(0, j)
            with dve.Fori(0, (SLICES - 2) // 2) as i:
                c = i * 2
                step(c, 0)
                step(c + 1, 1)
            step(SLICES - 2, 0)
            slice_peak(SLICES - 1)
            slice_top(SLICES - 1)
            slice_neg(SLICES - 1)
            for j in range(TILES):
                weights(SLICES - 1, 1, j)
            slice_sum(SLICES - 1, 1)
            dve.wait_ge(s_nt, SLICES * (l + 1))
            dve.tensor_reduce(least, neg_top, AX.X, ALU.min).then_inc(s_fs, 1)
            dve.wait_ge(s_ls, l + 1)
            dve.wait_ge(s_wt, l + 1)
            dve.tensor_tensor_reduce(scale8, wts, psum[:, 7, 0:SLICES], 1.0, 0.0, ALU.mult, ALU.add,
                                     total[:, 0:1]).then_inc(s_fs, 1)
            dve.wait_ge(s_fs, 3 * l + 2)
            dve.reciprocal(total[:, 1:2], total[:, 0:1]).then_inc(s_fs, 1)
            dve.wait_ge(s_fs, 3 * l + 3)
            link(dve.tensor_scalar(scale8, wts, total[:, 1:2], None, ALU.mult))
            dve.wait_ge(s_ot, SLICES * (l + 1) + 2)
            for c in range(SLICES):
                v = XT[:, c * SW:(c + 1) * SW]
                dve.tensor_scalar(v, v, scale8[:, c:c + 1], None, ALU.mult).then_inc(s_sc, 1)
        dve.wait_ge(s_xbb, 2 * BLOCKS)
        for c in range(BLOCKS):
            dve.wait_ge(s_x3p, c + 1)
            b = 2 * (c % 2) * 512
            g = flat(G[:, blk(c), :])
            dve.tensor_tensor(g, g, pflat[:, b:b + BW], ALU.add).then_inc(s_x3, 1)
            dve.wait_ge(s_x3, c + 1)
            norm_start(3, c)

        dve.wait_ge(s_x3, BLOCKS)
        dve.wait_ge(s_w, 16 * 22)
        static_scale()
        for l in range(2):
            split(l + 4, 3, l == 0, True)
            dve.wait_ge(s_x3d, 16 * BLOCKS)
            if l:
                dve.wait_ge(s_gx, 32 * BLOCKS)
            gcn(l + 4, l, l == 1)


_INS = ["x", "src", "dst", "L0_gnn_eps", "L0_gnn_W1", "L0_gnn_b1", "L0_gnn_ln_g", "L0_gnn_ln_b", "L0_gnn_W2",
        "L0_gnn_b2", "L1_gnn_W1", "L1_gnn_b1", "L1_gnn_W2", "L1_gnn_b2", "L1_gnn_W3", "L1_gnn_b3",
        "L2_gnn_W0", "L2_gnn_b0", "L2_gnn_W1", "L2_gnn_b1", "L2_gnn_W2", "L2_gnn_b2",
        "L3_gnn_W1", "L3_gnn_b1", "L3_gnn_W2", "L3_gnn_b2"]


def kernel(**inputs):
    import numpy as _np
    import concourse.bacc as _bacc
    from concourse import mybir as _mybir
    from concourse.bass_utils import run_bass_kernel_spmd as _run

    nc = _bacc.Bacc("TRN2", target_bir_lowering=False, num_devices=1)
    arrays, t = {}, {}
    for name in _INS:
        a = _np.ascontiguousarray(inputs[name])
        if a.ndim < 2:
            a = a.reshape(1, -1)
        if a.ndim == 3:
            a = a.reshape(a.shape[1:])
        arrays["in_" + name] = a
        t[name] = nc.dram_tensor("in_" + name, a.shape, _mybir.dt.from_np(a.dtype), kind="ExternalInput").ap()
    t["out"] = nc.dram_tensor("out", (N, D), F32, kind="ExternalOutput").ap()
    gnn_kernel(nc, t)
    r = _run(nc, [arrays], core_ids=[0])
    return r.results[0]["out"]
```
